# Optimizing a Trainium2 kernel written in Bass

```python
import numpy as np
import jax
import jax.numpy as jnp

def _softmax(x, axis=-1):
    return jax.nn.softmax(x, axis=axis)

def _gelu(x):
    return jax.nn.gelu(x, approximate=True)

def _silu(x):
    return jax.nn.silu(x)

def _sigmoid(x):
    return jax.nn.sigmoid(x)

def _layernorm(x, axis=-1, eps=1e-05):
    m = jnp.mean(x, axis=axis, keepdims=True)
    v = jnp.var(x, axis=axis, keepdims=True)
    return (x - m) / jnp.sqrt(v + eps)

def _scatter_add(tgt, idx, src, axis=0):
    return tgt.at[idx].add(src)

def _segment_sum(src, seg, n):
    return jax.ops.segment_sum(src, seg, n)
kernel_name = 'mk_vit_tower_d1_tok_img1024_r4_202159'

def setup_inputs(seed: int=0):
    np.random.seed(seed)
    _w = jnp.asarray

    def _rec_inputs():
        import jax
        import jax.numpy as jnp
        _rk = jax.random.key(seed)
        x = -0.00016672 + 0.999947 * jax.random.normal(jax.random.fold_in(_rk, 1), (64, 3, 96, 96), jnp.float32)
        return x
    x = _rec_inputs()

    def _L0_tok_setup():
        import jax, jax.numpy as jnp
        import numpy as np
        B, C, H, W = (64, 3, 96, 96)
        P = 16
        NP = H // P * (W // P)
        PD = C * P * P
        ED = 256
        NCLS = 1

        def _layernorm(x, g, b, eps=1e-05):
            mu = jnp.mean(x, axis=-1, keepdims=True)
            var = jnp.mean(jnp.square(x - mu), axis=-1, keepdims=True)
            return (x - mu) * jax.lax.rsqrt(var + eps) * g + b
        key = jax.random.key(seed)
        ks = jax.random.split(key, 8)
        x = jax.random.normal(ks[0], (B, C, H, W), dtype=jnp.float32)
        ln1_g = jnp.ones((PD,), jnp.float32)
        ln1_b = jnp.zeros((PD,), jnp.float32)
        W_proj = jax.random.normal(ks[1], (PD, ED), jnp.float32) / np.sqrt(PD)
        b_proj = jnp.zeros((ED,), jnp.float32)
        ln2_g = jnp.ones((ED,), jnp.float32)
        ln2_b = jnp.zeros((ED,), jnp.float32)
        cls_token = jax.random.normal(ks[2], (1, NCLS, ED), jnp.float32)
        pos_emb = jax.random.normal(ks[3], (1, NP + NCLS, ED), jnp.float32)
        return {'x': x, 'ln1_g': ln1_g, 'ln1_b': ln1_b, 'W_proj': W_proj, 'b_proj': b_proj, 'ln2_g': ln2_g, 'ln2_b': ln2_b, 'cls_token': cls_token, 'pos_emb': pos_emb}
    _L0_tok_all = _L0_tok_setup()
    _L0_tok_in = {k: v for k, v in _L0_tok_all.items() if k in ('ln1_g', 'ln1_b', 'W_proj', 'b_proj', 'ln2_g', 'ln2_b', 'cls_token', 'pos_emb')}
    del _L0_tok_all

    def _L0_attn_setup():
        import jax, jax.numpy as jnp
        import numpy as np
        B, L, H = (8, 512, 256)
        MASK_IDENTITY = True
        key = jax.random.key(seed)
        ks = jax.random.split(key, 7)
        s = 1.0 / np.sqrt(H)
        return {'x': jax.random.normal(ks[0], (B, L, H), dtype=jnp.float32), 'Wq': jax.random.uniform(ks[1], (H, H), jnp.float32, -s, s), 'bq': jax.random.uniform(ks[2], (H,), jnp.float32, -s, s), 'Wk': jax.random.uniform(ks[3], (H, H), jnp.float32, -s, s), 'bk': jax.random.uniform(ks[4], (H,), jnp.float32, -s, s), 'Wv': jax.random.uniform(ks[5], (H, H), jnp.float32, -s, s), 'bv': jax.random.uniform(ks[6], (H,), jnp.float32, -s, s)}
    _L0_attn_all = _L0_attn_setup()
    _L0_attn_in = {k: v for k, v in _L0_attn_all.items() if k in ('Wq', 'bq', 'Wk', 'bk', 'Wv', 'bv')}
    del _L0_attn_all

    def _L0_ffn_setup():
        import jax, jax.numpy as jnp
        from jax import lax
        import numpy as np
        B, S, D, H, DO, E, K = (4, 512, 256, 1024, 256, 8, 2)
        CAP_FACTOR = 1.5
        LN_EPS = 1e-05
        key = jax.random.key(seed)
        ks = jax.random.split(key, 8)
        s_in = 1.0 / np.sqrt(D)
        s_h = 1.0 / np.sqrt(H)
        return {'x': jax.random.normal(ks[0], (B, S, D), dtype=jnp.float32), 'router_w': jax.random.normal(ks[1], (D, E), dtype=jnp.float32) * s_in, 'router_b': jnp.zeros((E,), dtype=jnp.float32), 'w1': jax.random.normal(ks[2], (E, D, H), dtype=jnp.float32) * s_in, 'b1': jnp.zeros((E, H), dtype=jnp.float32), 'w2': jax.random.normal(ks[3], (E, H, DO), dtype=jnp.float32) * s_h, 'b2': jnp.zeros((E, DO), dtype=jnp.float32), 'ln_g': jnp.ones((DO,), dtype=jnp.float32), 'ln_b': jnp.zeros((DO,), dtype=jnp.float32)}
    _L0_ffn_all = _L0_ffn_setup()
    _L0_ffn_in = {k: v for k, v in _L0_ffn_all.items() if k in ('router_w', 'router_b', 'w1', 'b1', 'w2', 'b2', 'ln_g', 'ln_b')}
    del _L0_ffn_all
    return {'x': x, 'L0_tok_ln1_g': _L0_tok_in['ln1_g'], 'L0_tok_ln1_b': _L0_tok_in['ln1_b'], 'L0_tok_W_proj': _L0_tok_in['W_proj'], 'L0_tok_b_proj': _L0_tok_in['b_proj'], 'L0_tok_ln2_g': _L0_tok_in['ln2_g'], 'L0_tok_ln2_b': _L0_tok_in['ln2_b'], 'L0_tok_cls_token': _L0_tok_in['cls_token'], 'L0_tok_pos_emb': _L0_tok_in['pos_emb'], 'L0_attn_Wq': _L0_attn_in['Wq'], 'L0_attn_bq': _L0_attn_in['bq'], 'L0_attn_Wk': _L0_attn_in['Wk'], 'L0_attn_bk': _L0_attn_in['bk'], 'L0_attn_Wv': _L0_attn_in['Wv'], 'L0_attn_bv': _L0_attn_in['bv'], 'L0_ffn_router_w': _L0_ffn_in['router_w'], 'L0_ffn_router_b': _L0_ffn_in['router_b'], 'L0_ffn_w1': _L0_ffn_in['w1'], 'L0_ffn_b1': _L0_ffn_in['b1'], 'L0_ffn_w2': _L0_ffn_in['w2'], 'L0_ffn_b2': _L0_ffn_in['b2'], 'L0_ffn_ln_g': _L0_ffn_in['ln_g'], 'L0_ffn_ln_b': _L0_ffn_in['ln_b']}

def reference(x, L0_tok_ln1_g, L0_tok_ln1_b, L0_tok_W_proj, L0_tok_b_proj, L0_tok_ln2_g, L0_tok_ln2_b, L0_tok_cls_token, L0_tok_pos_emb, L0_attn_Wq, L0_attn_bq, L0_attn_Wk, L0_attn_bk, L0_attn_Wv, L0_attn_bv, L0_ffn_router_w, L0_ffn_router_b, L0_ffn_w1, L0_ffn_b1, L0_ffn_w2, L0_ffn_b2, L0_ffn_ln_g, L0_ffn_ln_b):
    import jax
    import jax.numpy as jnp

    def _L0_tok_ref(x, ln1_g, ln1_b, W_proj, b_proj, ln2_g, ln2_b, cls_token, pos_emb):
        import jax, jax.numpy as jnp
        import numpy as np
        B, C, H, W = (64, 3, 96, 96)
        P = 16
        NP = H // P * (W // P)
        PD = C * P * P
        ED = 256
        NCLS = 1

        def _layernorm(x, g, b, eps=1e-05):
            mu = jnp.mean(x, axis=-1, keepdims=True)
            var = jnp.mean(jnp.square(x - mu), axis=-1, keepdims=True)
            return (x - mu) * jax.lax.rsqrt(var + eps) * g + b
        b = x.shape[0]
        h, w = (H // P, W // P)
        patches = x.reshape(b, C, h, P, w, P)
        patches = patches.transpose(0, 2, 4, 3, 5, 1).reshape(b, h * w, P * P * C)
        z = _layernorm(patches, ln1_g, ln1_b)
        z = jnp.einsum('bnp,pe->bne', z, W_proj) + b_proj
        z = _layernorm(z, ln2_g, ln2_b)
        cls = jnp.broadcast_to(cls_token, (b, NCLS, ED))
        z = jnp.concatenate([cls, z], axis=1)
        z = z + pos_emb
        return z

    def _L0_attn_ref(x, Wq, bq, Wk, bk, Wv, bv):
        import jax, jax.numpy as jnp
        import numpy as np
        B, L, H = (8, 512, 256)
        MASK_IDENTITY = True
        q = jnp.einsum('blh,oh->blo', x, Wq) + bq
        k = jnp.einsum('blh,oh->blo', x, Wk) + bk
        v = jnp.einsum('blh,oh->blo', x, Wv) + bv
        hidden = q.shape[-1]
        attn = jnp.einsum('blh,bmh->blm', q / hidden, k)
        if MASK_IDENTITY:
            mask_value = -jnp.finfo(attn.dtype).max
            eye = jnp.eye(attn.shape[-1], dtype=bool)
            attn = jnp.where(eye[None, :, :], mask_value, attn)
        attn = jax.nn.softmax(attn, axis=-1)
        return jnp.einsum('blm,bmh->blh', attn, v)

    def _L0_ffn_ref(x, router_w, router_b, w1, b1, w2, b2, ln_g, ln_b):
        import jax, jax.numpy as jnp
        from jax import lax
        import numpy as np
        B, S, D, H, DO, E, K = (4, 512, 256, 1024, 256, 8, 2)
        CAP_FACTOR = 1.5
        LN_EPS = 1e-05
        Bx, Sx, Dx = x.shape
        N = Bx * Sx
        capacity = max(int(N * CAP_FACTOR / E), K)
        logits = jnp.einsum('bsd,de->bse', x, router_w) + router_b
        probs = jax.nn.softmax(logits, axis=-1)
        topv, topi = lax.top_k(probs, K)
        topv = topv / topv.sum(axis=-1, keepdims=True)
        flat_i = topi.reshape(-1)
        flat_v = topv.reshape(-1)
        mask = flat_i[None, :] == jnp.arange(E)[:, None]
        prio = jnp.where(mask, flat_v[None, :], -1.0)
        pv, pp = lax.top_k(prio, capacity)
        valid = pv > 0.0
        tok = jnp.where(valid, pp // K, 0)
        w = jnp.where(valid, pv, 0.0)
        x_flat = x.reshape(N, Dx)
        xin = x_flat[tok]
        h = jax.nn.gelu(jnp.einsum('ecd,edh->ech', xin, w1) + b1[:, None, :], approximate=False)
        out_e = jnp.einsum('ech,eho->eco', h, w2) + b2[:, None, :]
        out_e = out_e * w[..., None]
        out = jnp.zeros((N, DO), dtype=x.dtype)
        out = out.at[tok.reshape(-1)].add(out_e.reshape(-1, DO))
        out = out.reshape(Bx, Sx, DO)
        mu = out.mean(axis=-1, keepdims=True)
        var = out.var(axis=-1, keepdims=True)
        out = (out - mu) / jnp.sqrt(var + LN_EPS) * ln_g + ln_b
        return out
    h = _L0_tok_ref(x, L0_tok_ln1_g, L0_tok_ln1_b, L0_tok_W_proj, L0_tok_b_proj, L0_tok_ln2_g, L0_tok_ln2_b, L0_tok_cls_token, L0_tok_pos_emb)
    h = h + _L0_attn_ref(_layernorm(h, axis=-1), L0_attn_Wq, L0_attn_bq, L0_attn_Wk, L0_attn_bk, L0_attn_Wv, L0_attn_bv)
    h = h + _L0_ffn_ref(_layernorm(h, axis=-1), L0_ffn_router_w, L0_ffn_router_b, L0_ffn_w1, L0_ffn_b1, L0_ffn_w2, L0_ffn_b2, L0_ffn_ln_g, L0_ffn_ln_b)
    return h

_drawn_inputs = setup_inputs


def setup_inputs(seed=0):
    import zlib

    import numpy as np

    out = dict(_drawn_inputs(seed))
    spreads = {'L0_tok_ln1_g': (1.0, 0.2),
     'L0_tok_ln1_b': (0.0, 0.1),
     'L0_tok_b_proj': (0.0, 0.1),
     'L0_tok_ln2_g': (1.0, 0.2),
     'L0_tok_ln2_b': (0.0, 0.1),
     'L0_ffn_router_b': (0.0, 0.1),
     'L0_ffn_b1': (0.0, 0.1),
     'L0_ffn_b2': (0.0, 0.1),
     'L0_ffn_ln_g': (1.0, 0.2),
     'L0_ffn_ln_b': (0.0, 0.1)}
    factors = {'L0_attn_bq': 24.774, 'L0_attn_bk': 64.0}
    for name, (base, spread) in spreads.items():
        noise = np.random.default_rng([zlib.crc32(name.encode()), seed]).standard_normal(out[name].shape)
        drawn = base * np.exp(spread * noise) if base else spread * noise
        out[name] = jnp.asarray(drawn.astype(out[name].dtype))
    for name, factor in factors.items():
        out[name] = (out[name] * factor).astype(out[name].dtype)
    return out
```

```python
from contextlib import ExitStack

import concourse.bass as bass
from concourse import mybir

fp32 = mybir.dt.float32
bf16 = mybir.dt.bfloat16
i32 = mybir.dt.int32
u32 = mybir.dt.uint32
ALU = mybir.AluOpType
ACT = mybir.ActivationFunctionType
AX = mybir.AxisListType

EPS = 1e-5
MASKED = -3.0e38


def rep(ap, dim, n):
    shape = list(ap.shape)
    shape[dim] = n
    return ap.broadcast_to(shape)


def vit_tower(nc, x, ln1_g, ln1_b, w_proj, b_proj, ln2_g, ln2_b, cls_token, pos_emb,
              wq_t, bq, wk_t, bk, wv_t, bv, router_w, router_b, w1, b1, w2, b2, ln_g, ln_b, out):
    IMAGES, PATCHES, PD = x.shape
    ED = w_proj.shape[1]
    L = PATCHES + 1
    PER = 128 // L
    P = 112
    TILES = -(-IMAGES // PER)
    LIVE_LAST = (IMAGES - PER * (TILES - 1)) * L
    PC = PD // 128
    EC = ED // 128
    E, _, HID = w1.shape
    HC = HID // 128
    CAP = int(IMAGES * L * 1.5 / E)
    JT = -(-CAP // P)
    SLOTS = JT * P
    COLS = E * JT
    PAD = 24
    Q = 2 * TILES
    HALF = PD // 2
    TRASH = Q * P
    WAYS = 16
    SHIFTS = [26, 22, 18, 14, 10, 6, 2, 0]

    ctx = ExitStack()
    with ctx:
        def sb(name, shape, dt=fp32):
            return ctx.enter_context(nc.sbuf_tensor(name, shape, dt))

        def sem(name):
            return ctx.enter_context(nc.semaphore(name))

        x2_rows = nc.dram_tensor("x2_rows", [TILES * P, ED], fp32, kind="Internal").ap()
        y_rows = nc.dram_tensor("y_rows", [TRASH + COLS * P, ED], fp32, kind="Internal").ap()

        ident = sb("ident", [128, 128])
        wproj = sb("wproj", [128, PC, ED])
        ln1g = sb("ln1g", [128, PC])
        ln1b = sb("ln1b", [128, PC])
        onesrow = sb("onesrow", [1, 128])
        bproj = sb("bproj", [1, ED])
        zbias = sb("zbias", [P, ED])
        g2m = sb("g2m", [P, ED])
        posb = sb("posb", [P, ED])
        posadd = sb("posadd", [P, ED])
        wq = sb("wq", [128, EC, ED])
        wk = sb("wk", [128, EC, ED])
        wv = sb("wv", [128, EC, ED])
        bqk = sb("bqk", [128, 2 * EC])
        bvb = sb("bvb", [P, ED])
        amask = sb("amask", [P, P])
        rw = sb("rw", [128, EC, E])
        rbb = sb("rbb", [P, E])
        neghalf = sb("neghalf", [P, 1])
        lng = sb("lng", [P, ED])
        lnb = sb("lnb", [P, ED])
        b1t = sb("b1t", [128, E * HC])
        b2b = sb("b2b", [P, E, ED])
        xin = sb("xin", [P, 2, PD])
        xstat = sb("xstat", [P, 2, 6])
        xmv = sb("xmv", [P, 2])
        xn = sb("xn", [P, 2, PD])
        xnT = sb("xnT", [128, PC, P])
        zb = sb("zb", [P, ED])
        zstat = sb("zstat", [P, 6])
        zmv = sb("zmv", [P, 2])
        zn = sb("zn", [P, ED])
        hstat = sb("hstat", [P, 6])
        hmv = sb("hmv", [P, 2])
        x1 = sb("x1", [P, 2, ED])
        x1T = sb("x1T", [128, 2, EC * P])
        qkT = sb("qkT", [128, 2 * EC, P])
        v = sb("v", [P, 2, ED])
        masked = sb("masked", [P, P])
        smax = sb("smax", [P, 1])
        nmax = sb("nmax", [P, 1])
        prob = sb("prob", [P, P])
        psumr = sb("psumr", [P, 2])
        rinv = sb("rinv", [P, 1])
        probT = sb("probT", [P, P])
        gstat = sb("gstat", [P, 6])
        gmv = sb("gmv", [P, 2])
        x2 = sb("x2", [P, 2, ED])
        x2T = sb("x2T", [128, EC * P])
        rs = sb("rs", [P, 4, 2])
        H = sb("H", [P, TILES, ED])
        LG = sb("LG", [P, E, TILES])
        erev = sb("erev", [P, E, TILES])
        eqm = sb("eqm", [P, E, TILES])
        oh1 = sb("oh1", [P, E, TILES])
        oh2 = sb("oh2", [P, E, TILES])
        lg2 = sb("lg2", [P, E, TILES])
        m12 = sb("m12", [P, 2, TILES])
        f12 = sb("f12", [P, 2, TILES])
        dl = sb("dl", [P, TILES])
        ed = sb("ed", [P, TILES])
        gate = sb("gate", [P, 2, TILES])
        valid = sb("valid", [P, TILES])
        V = sb("V", [P, E, PAD])
        V2 = sb("V2", [P, E, TILES])
        digit = sb("digit", [128, len(SHIFTS)], i32)
        pidx = sb("pidx", [128, 1], i32)
        thr = sb("thr", [128, 1], i32)
        cand = sb("cand", [128, 1], i32)
        cnt = sb("cnt", [128, 1])
        won = sb("won", [128, 1], bf16)
        dwon = sb("dwon", [128, 1], i32)
        junk = sb("junk", [128, 6 * 4 * P], bf16)
        grp = sb("grp", [128, 128], bf16)
        pick = sb("pick", [128, E])
        thrrow = sb("thrrow", [128, E])
        thrb = sb("thrb", [P, E])
        onesf = sb("onesf", [128, 128])
        onesb = sb("onesb", [128, 128], bf16)
        below = sb("below", [128, 128], bf16)
        ge = sb("ge", [P, 2, E, TILES], bf16)
        keep0 = sb("keep0", [P, 2 * E, TILES])
        tincl = sb("tincl", [P, 2 * E, TILES])
        pos = sb("pos", [P, 2, E, TILES])
        okeq = sb("okeq", [P, E, TILES])
        ok = sb("ok", [P, E, TILES])
        base1 = sb("base1", [P, E, TILES])
        aslot = sb("aslot", [P, E, TILES])
        s12 = sb("s12", [P, 2, TILES])
        hi = sb("hi", [P, Q])
        lo = sb("lo", [P, Q])
        wtok = sb("wtok", [P, 2, TILES])
        iorow = sb("iorow", [P, P])
        qidx = sb("qidx", [P, Q])
        row1 = sb("row1", [P, 1])
        ohlo = sb("ohlo", [P, Q, P], bf16)
        ohhi = sb("ohhi", [P, Q, COLS], bf16)
        ohval = sb("ohval", [P, Q, 2, COLS], bf16)
        trash = sb("trash", [P, COLS])
        drow = sb("drow", [P, COLS])
        empty = sb("empty", [P, COLS])
        kch = sb("kch", [P, COLS])
        idf = sb("idf", [P, COLS])
        gidx = sb("gidx", [P, COLS], u32)
        didx = sb("didx", [P, COLS], u32)
        w1s = sb("w1s", [128, 2, EC, HID])
        w2s = sb("w2s", [128, 2, HC, ED])
        gst = sb("gst", [P, 2, JT], u32)
        dst = sb("dst", [P, 2, JT], u32)
        xg = sb("xg", [P, 2, JT, ED])
        xgT = sb("xgT", [128, 2, EC, SLOTS])
        hT = sb("hT", [128, 2, HC, SLOTS])
        y = sb("y", [P, 2, JT, ED])
        zero = hT[0:P, 1, :, :].rearrange("p a b -> p (a b)")
        vrep = hT[0:P, 0, :, :].rearrange("p a b -> p (a b)")[:, 0:PAD * 128].rearrange("p (t m) -> p t m", m=128)
        w1flat = w1s[0:P, :, :, :].rearrange("p a c h -> p (a c h)")

        def within_w1(first, *dims):
            n = 1
            for d in dims:
                n *= d
            flat = w1flat[:, first * ED:first * ED + n]
            return flat.rearrange("p (a f) -> p a f", f=ED) if len(dims) == 2 else \
                flat.rearrange("p (a b f) -> p a b f", a=dims[0], f=ED)

        yin = within_w1(0, 2, 2, ED)
        ya = within_w1(4, 2, ED)
        yc = within_w1(6, 2, ED)
        yn = within_w1(8, 2, ED)
        yo = within_w1(10, 2, ED)
        ystat = sb("ystat", [P, 6])
        ymv = sb("ymv", [P, 2, 2])
        yrs = sb("yrs", [P, 2, 2])

        ps = [ctx.enter_context(nc.psum_tensor(f"ps{b}", [128, 512], fp32)) for b in range(2)]
        pall = ctx.enter_context(nc.psum_tensor("pall", [128, 6, 512], fp32))

        def bank(b):
            return ps[b][:, :] if b < 2 else pall[:, b - 2, :]

        c_dma = sem("c_dma"); c_pool = sem("c_pool"); c_dve = sem("c_dve"); c_pe = sem("c_pe")
        s_zero = sem("s_zero"); s_xz = sem("s_xz"); s_fill = sem("s_fill")
        x_in = [sem("x_in0"), sem("x_in1")]
        x_st = sem("x_st"); x_mv = sem("x_mv"); x_rs0 = sem("x_rs0"); x_rs = sem("x_rs"); x_n = sem("x_n")
        xT_ps = sem("xT_ps"); xT_sb = sem("xT_sb"); z_ps = sem("z_ps"); z_b = sem("z_b")
        z_st = sem("z_st"); z_mv = sem("z_mv"); z_rs0 = sem("z_rs0"); z_rs = sem("z_rs"); z_n = sem("z_n")
        h_g = sem("h_g"); h_ok = sem("h_ok")
        h_st = sem("h_st"); h_mv = sem("h_mv"); h_rs0 = sem("h_rs0"); h_rs = sem("h_rs"); x1_ok = sem("x1_ok")
        x1T_ps = sem("x1T_ps"); x1T_sb = sem("x1T_sb"); qk_ps = sem("qk_ps"); v_ps = sem("v_ps")
        qk_sb = sem("qk_sb"); v_sb = sem("v_sb"); s_ps = sem("s_ps"); s_msk = sem("s_msk"); s_nmx = sem("s_nmx")
        p_ok = sem("p_ok"); pT_ps = sem("pT_ps"); pT_sb = sem("pT_sb"); o_ps = sem("o_ps")
        r_inv = sem("r_inv"); g_h = sem("g_h"); g_st = sem("g_st"); g_mv = sem("g_mv")
        g_rs0 = sem("g_rs0"); g_rs = sem("g_rs"); x2_ok = sem("x2_ok")
        x2_out = [sem("x2_out0"), sem("x2_out1")]
        x2T_ps = sem("x2T_ps"); x2T_sb = sem("x2T_sb"); l_ps = sem("l_ps"); l_sb = sem("l_sb")
        d_seq = sem("d_seq")
        r_dl = sem("r_dl"); r_ed = sem("r_ed"); r_V = sem("r_V"); r_VT = sem("r_VT"); r_won = sem("r_won")
        r_n = sem("r_n"); r_pick = sem("r_pick"); r_thr = sem("r_thr"); r_ge = sem("r_ge"); r_pos = sem("r_pos")
        r_lo = sem("r_lo"); r_val = sem("r_val"); r_list = sem("r_list"); r_idx = sem("r_idx")
        w_in = [sem("w_in0"), sem("w_in1")]
        i_st = sem("i_st")
        g_in = [sem("g_in0"), sem("g_in1")]
        gT_ps = sem("gT_ps"); gT_sb = sem("gT_sb"); u_ps = sem("u_ps"); u_sb = sem("u_sb")
        y_ps = sem("y_ps"); y_free = sem("y_free"); y_sb = sem("y_sb");
        y_out = [sem("y_out0"), sem("y_out1")]
        hb = sem("hb")
        z_in = [sem("z_in0"), sem("z_in1")]
        a_ok = sem("a_ok"); c_ok = sem("c_ok"); c_st = sem("c_st"); c_mv = sem("c_mv"); c_rs0 = sem("c_rs0")
        c_rs = sem("c_rs"); n_ok = sem("n_ok"); o_g = sem("o_g"); o_ok = sem("o_ok")
        o_out = [sem("o_out0"), sem("o_out1")]

        block = ctx.enter_context(nc.Block())

        def live(t):
            return not isinstance(t, int) or 0 <= t < TILES

        def need(eng, s, n):
            if not isinstance(n, int) or n > 0:
                eng.wait_ge(s, n)

        turn = {}

        def plain(eng, *waits):
            for w, n in waits:
                need(eng, w, n)
            if not isinstance(waits[0][1], int):
                if eng.engine not in turn:
                    turn[eng.engine] = sem(f"turn_{len(turn)}")
                eng.sem_inc(turn[eng.engine], 1)

        SKEW = 5
        STEPS = TILES + SKEW

        def pipeline(eng, step, lo_, hi_, first=0):
            assert (hi_ - lo_) % 2 == 0
            for i in range(first, lo_):
                step(i, i % 2)
            with eng.Fori(0, (hi_ - lo_) // 2) as j:
                i = j * 2 + lo_
                step(i, lo_ % 2)
                step(i + 1, (lo_ + 1) % 2)
            for i in range(hi_, STEPS):
                step(i, i % 2)

        def at(t):
            return t if isinstance(t, int) else bass.ds(t, 1)

        def tile_of(buf, t):
            if isinstance(t, int):
                return buf[:, t, :]
            return buf[:, bass.ds(t, 1), :].rearrange("p a f -> p (a f)")

        def col(buf, t):
            return buf[:, t:t + 1] if isinstance(t, int) else buf[:, bass.ds(t, 1)]

        def yuse(t, par):
            return 16 * (t // 2 + 1) if isinstance(t, int) else (t - par + 2) * 8

        def e_count(e, par, n):
            return (e // 2 + 1) * n if isinstance(e, int) else (e - par + 2) * (n // 2)

        @block.sync
        def _(sp):
            def load_x(t, par):
                n = min(PER, IMAGES - PER * t) if isinstance(t, int) else PER
                for m in range(PER):
                    if m < n:
                        src = x[PER * t + m] if isinstance(t, int) else \
                            x[bass.ds(t * PER + m, 1)].rearrange("a r f -> (a r) f")
                        sp.dma_start(xin[m * L + 1:(m + 1) * L, par, :], src).then_inc(x_in[par], 16)

            sp.wait_ge(s_xz, 1)
            load_x(0, 0)
            load_x(1, 1)
            for e in range(2):
                sp.dma_start(w1s[:, e, :, :], w1[e].rearrange("(c p) h -> p c h", p=128)).then_inc(w_in[e], 16)
                sp.dma_start(w2s[:, e, :, :], w2[e].rearrange("(k p) o -> p k o", p=128)).then_inc(w_in[e], 16)

            def step(i, par):
                t = i + 2
                if live(t):
                    need(sp, x_n, i + 1)
                    load_x(t, par)
                t = i - 4
                if live(t):
                    need(sp, x2_ok, t + 1)
                    dram = x2_rows[t * P:(t + 1) * P, :] if isinstance(t, int) else x2_rows[bass.ds(t * P, P), :]
                    sp.dma_start(dram, x2[:, par, :]).then_inc(x2_out[par], 16)
            pipeline(sp, step, 7, 19)

            for e in range(2, E):
                sp.wait_ge(y_ps, (e - 1) * JT)
                sp.dma_start(w1s[:, e % 2, :, :], w1[e].rearrange("(c p) h -> p c h", p=128)).then_inc(w_in[e % 2], 16)
                sp.dma_start(w2s[:, e % 2, :, :], w2[e].rearrange("(k p) o -> p k o", p=128)).then_inc(w_in[e % 2], 16)

            for par in range(2):
                sp.wait_ge(y_out[par], 16 * JT * E // 2)
            y_v = y_rows[0:TRASH, :].rearrange("(k t p) f -> p t k f", k=2, p=P)

            def load_y(t, par):
                src = y_v[:, t, :, :] if isinstance(t, int) else y_v[:, bass.ds(t, 1), :, :].rearrange("p a k f -> p (a k) f")
                sp.dma_start(yin[:, par, :, :], src).then_inc(z_in[par], 16)

            def store(t, par):
                sp.wait_ge(o_ok, t + 1)
                rows = PER * L
                sp.dma_start(out_rows(t, 0, 96), yo[0:96, par, :]).then_inc(o_out[par], 16)
                sp.dma_start(out_rows(t, 96, rows), yo[96:rows, par, :]).then_inc(o_out[par], 16)

            def out_rows(t, a, b):
                if isinstance(t, int):
                    return out[t * PER * L + a:t * PER * L + b, :]
                return out[bass.ds(t * (PER * L) + a, b - a), :]

            load_y(0, 0)
            load_y(1, 1)
            with sp.Fori(0, (TILES - 2) // 2) as j:
                for par in range(2):
                    t = j * 2 + par
                    sp.wait_ge(c_ok, t + 1)
                    load_y(t + 2, par)
                    store(t, par)
            store(TILES - 2, 0)
            t = TILES - 1
            sp.wait_ge(o_ok, t + 1)
            sp.dma_start(out_rows(t, 0, 32), yo[0:32, 1, :]).then_inc(o_out[1], 16)
            sp.dma_start(out_rows(t, 32, LIVE_LAST), yo[32:LIVE_LAST, 1, :]).then_inc(o_out[1], 16)
            for par in range(2):
                sp.wait_ge(o_out[par], 16 * TILES)
                sp.wait_ge(x2_out[par], 16 * (TILES // 2))
                sp.wait_ge(y_out[par], 16 * JT * E // 2)

        @block.scalar
        def _(act):
            n = 0

            def load(dst_, src):
                nonlocal n
                nc.scalar.dma_start(dst_, src).then_inc(c_dma, 16)
                n += 1

            load(wproj[:, :, :], w_proj.rearrange("(c p) e -> p c e", p=128))
            load(ln1g[:, :], ln1_g)
            load(ln1b[:, :], ln1_b)
            load(bproj[:, :], b_proj)
            load(wq[:, :, :], wq_t.rearrange("(c p) o -> p c o", p=128))
            load(wk[:, :, :], wk_t.rearrange("(c p) o -> p c o", p=128))
            load(wv[:, :, :], wv_t.rearrange("(c p) o -> p c o", p=128))
            load(bqk[:, 0:EC], bq)
            load(bqk[:, EC:2 * EC], bk)
            load(bvb[:, :], rep(bv, 0, P))
            load(rw[:, :, :], router_w.rearrange("(c p) e -> p c e", p=128))
            load(rbb[:, :], rep(router_b, 0, P))
            load(lng[:, :], rep(ln_g, 0, P))
            load(lnb[:, :], rep(ln_b, 0, P))
            load(b1t[:, :], b1)
            load(b2b[:, :, :].rearrange("p a b -> p (a b)"), rep(b2, 0, P))
            act.wait_ge(s_zero, 1)
            for m in range(PER):
                load(g2m[m * L + 1:(m + 1) * L, :], rep(ln2_g, 0, PATCHES))
                load(posadd[m * L + 1:(m + 1) * L, :], rep(ln2_b, 0, PATCHES))
                load(posadd[m * L:m * L + 1, :], cls_token)
                load(posb[m * L:(m + 1) * L, :], pos_emb)
            assert n == 16 + 4 * PER
            act.wait_ge(c_dma, 16 * n)

            def step(i, par):
                t = i - 3
                if live(t):
                    need(act, s_nmx, t + 1)
                    need(act, pT_ps, t)
                    need(act, r_inv, t - 1)
                    nc.scalar.activation(prob[:, :], masked[:, :], ACT.Exp, bias=nmax[:, 0:1], scale=1.0 / ED,
                                         accum_out=psumr[:, (par + 1) % 2:(par + 1) % 2 + 1]).then_inc(p_ok, 1)
                t = i
                if live(t):
                    need(act, xT_ps, t + 1)
                    need(act, z_ps, t)
                    nc.scalar.copy(xnT[:, 0:3, :].rearrange("p a b -> p (a b)"), ps[0][:, 0:3 * P])
                    nc.scalar.copy(xnT[:, 3:6, :].rearrange("p a b -> p (a b)"), ps[1][:, 0:3 * P]).then_inc(xT_sb, 1)
                t = i - 2
                if live(t):
                    need(act, qk_ps, t + 1)
                    need(act, s_ps, t)
                    for c in range(2 * EC):
                        a = nc.scalar.activation(qkT[:, c, :], bank(3)[:, c * P:(c + 1) * P], ACT.Identity,
                                                 bias=bqk[:, c:c + 1])
                    a.then_inc(qk_sb, 1)
                t = i - 3
                if live(t):
                    need(act, pT_ps, t + 1)
                    need(act, o_ps, t)
                    nc.scalar.copy(probT[:, :], bank(5)[0:P, 0:P]).then_inc(pT_sb, 1)
                t = i - 1
                if live(t):
                    need(act, x1T_ps, t + 1)
                    need(act, v_ps, t - 1)
                    nc.scalar.copy(x1T[:, (par + 1) % 2, :], bank(6)[:, 0:EC * P]).then_inc(x1T_sb, 1)
                t = i - 4
                if live(t):
                    need(act, x2T_ps, t + 1)
                    need(act, l_ps, t)
                    nc.scalar.copy(x2T[:, :], bank(4)[:, 0:EC * P]).then_inc(x2T_sb, 1)
            pipeline(act, step, 6, 22)

            act.wait_ge(r_dl, 1)
            nc.scalar.activation(ed[:, :], dl[:, :], ACT.Exp).then_inc(r_ed, 1)

            act.wait_ge(s_fill, 16 * 4)

            def gelu(e, par):
                for k in range(HC):
                    u = e * HC + k
                    act.wait_ge(u_ps, u + 1)
                    nc.scalar.activation(hT[:, par, k, :], bank(k % 4)[:, 0:SLOTS], ACT.Gelu,
                                         bias=col(b1t, u)).then_inc(u_sb, 1)

            with act.Fori(0, E // 2) as j:
                for par in range(2):
                    gelu(j * 2 + par, par)

            def first_choice(t, par, skip=False):
                act.wait_ge(z_in[par], yuse(t, par))
                if not skip:
                    act.wait_ge(c_ok, t - 1)
                nc.scalar.activation(ya[:, par, :], yin[:, par, 0, :], ACT.Copy, scale=col(wt1, t)).then_inc(a_ok, 1)
            wt1 = wtok[:, 0, :]
            first_choice(0, 0, True)
            first_choice(1, 1, True)
            with act.Fori(0, (TILES - 2) // 2) as j:
                for par in range(2):
                    first_choice(j * 2 + 2 + par, par)

        @block.tensor
        def _(pe):
            pe.wait_ge(c_pool, 5)
            pe.wait_ge(c_dma, 16 * (16 + 4 * PER))
            pe.wait_ge(c_dve, 1)
            for c in range(PC):
                nc.tensor.matmul(bank(2)[0:P, 0:ED], xnT[:, c, :], wproj[:, c, :], start=(c == 0), stop=False)
            nc.tensor.matmul(bank(2)[0:P, 0:ED], onesrow[0:1, 0:P], bproj[0:1, :], start=False, stop=True)\
                .then_inc(c_pe, 1)
            pe.wait_ge(c_dve, 2)

            def step(i, par):
                odd = (par + 1) % 2
                t = i
                if live(t):
                    need(pe, x_n, t + 1)
                    need(pe, xT_sb, t)
                    for c in range(PC):
                        m = nc.tensor.transpose(ps[c // 3][:, (c % 3) * P:(c % 3 + 1) * P],
                                                xn[:, par, c * 128:(c + 1) * 128], ident[0:P, 0:P])
                    m.then_inc(xT_ps, 1)
                t = i - 2
                if live(t):
                    need(pe, x1T_sb, t + 1)
                    need(pe, qk_sb, t)
                    xt = x1T[:, par, :].rearrange("p (c r) -> p c r", c=EC)
                    for o in range(2 * EC):
                        w = wq if o < EC else wk
                        for c in range(EC):
                            m = nc.tensor.matmul(bank(3)[:, o * P:(o + 1) * P],
                                                 w[:, c, (o % EC) * 128:(o % EC + 1) * 128], xt[:, c, :],
                                                 start=(c == 0), stop=(c == EC - 1))
                    m.then_inc(qk_ps, 1)
                    need(pe, x2T_sb, t - 2)
                    need(pe, v_sb, t)
                    for c in range(EC):
                        m = nc.tensor.matmul(bank(4)[0:P, 0:ED], xt[:, c, :], wv[:, c, :],
                                             start=(c == 0), stop=(c == EC - 1))
                    m.then_inc(v_ps, 1)
                t = i - 3
                if live(t):
                    need(pe, p_ok, t + 1)
                    nc.tensor.transpose(bank(5)[0:P, 0:P], prob[:, :], ident[0:P, 0:P]).then_inc(pT_ps, 1)
                t = i - 5
                if live(t):
                    need(pe, x2T_sb, t + 1)
                    need(pe, l_sb, t)
                    need(pe, g_h, t + 2 if not isinstance(t, int) else min(t + 2, TILES))
                    for c in range(EC):
                        m = nc.tensor.matmul(bank(7)[0:P, 0:E], x2T[:, c * P:(c + 1) * P], rw[:, c, :],
                                             start=(c == 0), stop=(c == EC - 1))
                    m.then_inc(l_ps, 1)
                t = i
                if live(t):
                    need(pe, xT_sb, t + 1)
                    need(pe, z_b, t)
                    for c in range(PC):
                        m = nc.tensor.matmul(bank(2)[0:P, 0:ED], xnT[:, c, :], wproj[:, c, :],
                                             start=(c == 0), stop=(c == PC - 1))
                    m.then_inc(z_ps, 1)
                t = i - 3
                if live(t):
                    need(pe, pT_sb, t + 1)
                    need(pe, v_sb, t + 1)
                    need(pe, l_sb, t - 1)
                    need(pe, g_h, t)
                    nc.tensor.matmul(bank(7)[0:P, 0:ED], probT[:, :], v[:, odd, :], start=True, stop=True)\
                        .then_inc(o_ps, 1)
                t = i - 2
                if live(t):
                    need(pe, qk_sb, t + 1)
                    need(pe, s_msk, t)
                    for c in range(EC):
                        m = nc.tensor.matmul(bank(5)[0:P, 0:P], qkT[:, c, :], qkT[:, EC + c, :],
                                             start=(c == 0), stop=(c == EC - 1))
                    m.then_inc(s_ps, 1)
                t = i - 1
                if live(t):
                    need(pe, x1_ok, t + 1)
                    need(pe, x1T_sb, t)
                    for c in range(EC):
                        m = nc.tensor.transpose(bank(6)[:, c * P:(c + 1) * P],
                                                x1[:, odd, c * 128:(c + 1) * 128], ident[0:P, 0:P])
                    m.then_inc(x1T_ps, 1)
                t = i - 4
                if live(t):
                    need(pe, x2_ok, t + 1)
                    if not isinstance(t, int) or t + 3 <= TILES:
                        need(pe, v_sb, t + 3)
                    for c in range(EC):
                        m = nc.tensor.transpose(bank(4)[:, c * P:(c + 1) * P],
                                                x2[:, par, c * 128:(c + 1) * 128], ident[0:P, 0:P])
                    m.then_inc(x2T_ps, 1)
            pipeline(pe, step, 6, 22)

            pe.wait_ge(r_V, 1)
            pe.wait_ge(l_sb, TILES)
            pe.wait_ge(g_h, TILES)
            pe.wait_ge(x2T_sb, TILES)
            for t in range(PAD):
                m = nc.tensor.transpose(pall[:, t // 4, (t % 4) * P:(t % 4 + 1) * P], vrep[:, t, :], ident[0:P, 0:P])
            m.then_inc(r_VT, 1)
            for r in range(len(SHIFTS)):
                pe.wait_ge(r_won, r + 1)
                nc.tensor.matmul(ps[0][:, 0:1], grp[:, :], won[:, :], start=True, stop=True).then_inc(r_n, 1)
            pe.wait_ge(r_pick, 1)
            nc.tensor.matmul(ps[0][0:P, 0:E], onesf[:, 0:P], thrrow[:, :], start=True, stop=True).then_inc(r_thr, 1)
            pe.wait_ge(r_ge, 1)
            gev = ge[:, :, :, :].rearrange("p s e t -> p (s e t)")
            n = 2 * E * TILES
            nc.tensor.matmul(bank(2)[0:P, 0:n], below[0:P, 0:P], gev, start=True, stop=True)
            nc.tensor.matmul(bank(3)[0:P, 0:n], onesb[0:P, 0:P], gev, start=True, stop=True).then_inc(r_pos, 1)
            pe.wait_ge(r_lo, 1)
            pe.wait_ge(r_val, 1)
            for q in range(Q):
                m = nc.tensor.matmul(bank(4)[0:P, 0:2 * COLS], ohlo[:, q, :],
                                     ohval[:, q, :, :].rearrange("p a b -> p (a b)"),
                                     start=(q == 0), stop=(q == Q - 1))
            m.then_inc(r_list, 1)

            def transposes(e, par):
                pe.wait_ge(g_in[par], e_count(e, par, 16 * JT))
                pe.wait_ge(gT_sb, e)
                for c in range(EC):
                    for j in range(JT):
                        m = nc.tensor.transpose(bank(4 + c)[:, j * P:(j + 1) * P],
                                                xg[:, par, j, c * 128:(c + 1) * 128], ident[0:P, 0:P])
                m.then_inc(gT_ps, 1)

            def expert(e, par, last=False):
                pe.wait_ge(w_in[par], e_count(e, par, 32))
                pe.wait_ge(gT_sb, e + 1)
                for k in range(HC):
                    u = e * HC + k
                    need(pe, u_sb, u - 3)
                    for c in range(EC):
                        m = nc.tensor.matmul(bank(k % 4)[:, 0:SLOTS], w1s[:, par, c, k * 128:(k + 1) * 128],
                                             xgT[:, par, c, :], start=(c == 0), stop=(c == EC - 1))
                    m.then_inc(u_ps, 1)
                if not last:
                    transposes(e + 1, 1 - par)
                for j in range(JT):
                    need(pe, y_sb, e * JT + j - 1)
                    for k in range(HC):
                        if j == 0:
                            pe.wait_ge(u_sb, e * HC + k + 1)
                        m = nc.tensor.matmul(bank(6 + j % 2)[0:P, 0:ED], hT[:, par, k, j * P:(j + 1) * P],
                                             w2s[:, par, k, :], start=(k == 0), stop=(k == HC - 1))
                    m.then_inc(y_ps, 1)

            pe.wait_ge(g_in[0], 16 * JT)
            for c in range(EC):
                for j in range(JT):
                    m = nc.tensor.transpose(bank(4 + c)[:, j * P:(j + 1) * P],
                                            xg[:, 0, j, c * 128:(c + 1) * 128], ident[0:P, 0:P])
            m.then_inc(gT_ps, 1)
            expert(0, 0)
            expert(1, 1)
            with pe.Fori(0, (E - 4) // 2) as jj:
                for par in range(2):
                    expert(jj * 2 + 2 + par, par)
            expert(E - 2, 0)
            expert(E - 1, 1, last=True)

        @block.vector
        def _(dve):
            V_ = nc.vector
            V_.memset(g2m[:, :], 0.0)
            V_.memset(posb[:, :], 0.0)
            V_.memset(posadd[:, :], 0.0).then_inc(s_zero, 1)
            V_.memset(xin[:, :, :], 0.0).then_inc(s_xz, 1)
            V_.memset(V[:, :, :], 0.0)
            dve.wait_ge(c_dma, 16 * (16 + 4 * PER))
            V_.tensor_copy(xnT[:, :, :], rep(ln1b[:, :].rearrange("p (c a) -> p c a", a=1), 2, P)).then_inc(c_dve, 1)
            V_.tensor_tensor(posb[:, :], posb[:, :], posadd[:, :], ALU.add)
            dve.wait_ge(c_pe, 1)
            V_.tensor_copy(zbias[:, :], bank(2)[0:P, 0:ED])
            for c in range(PC):
                m = V_.tensor_scalar(wproj[:, c, :], wproj[:, c, :], ln1g[:, c:c + 1], None, ALU.mult)
            m.then_inc(c_dve, 1)
            dve.wait_ge(c_dve, 2)
            dve.wait_ge(c_pool, 5)

            def stats_x(t, par):
                three = 48
                if isinstance(t, int):
                    n = sum(min(PER, IMAGES - PER * s) for s in range(par, t + 1, 2))
                    dve.wait_ge(x_in[par], 16 * n)
                else:
                    dve.wait_ge(x_in[par], (t - par + 2) * (three // 2))
                for hlf in range(2):
                    m = V_.bn_stats(xstat[:, hlf, :], xin[:, par, hlf * HALF:(hlf + 1) * HALF])
                m.then_inc(x_st, 1)
                plain(dve, (x_st, t + 1), (x_rs0, t))
                V_.bn_aggr(xmv[:, :], xstat[:, :, :].rearrange("p a b -> p (a b)")).then_inc(x_mv, 1)

            def norm_x(t, par):
                dve.wait_ge(x_rs, t + 1)
                dve.wait_ge(x_mv, t + 1)
                need(dve, xT_ps, t - 1)
                V_.tensor_scalar(xn[:, par, :], xin[:, par, :], xmv[:, 0:1], rs[:, 0, 1:2],
                                 ALU.subtract, ALU.mult).then_inc(x_n, 1)

            stats_x(0, 0)
            norm_x(0, 0)

            def step(i, par):
                odd = (par + 1) % 2
                t = i - 3
                if live(t):
                    plain(dve, (s_ps, t + 1), (p_ok, t), (s_nmx, t))
                    V_.tensor_tensor_reduce(masked[:, :], bank(5)[0:P, 0:P], amask[:, :], 1.0, MASKED,
                                            ALU.add, ALU.max, smax[:, 0:1]).then_inc(s_msk, 1)
                    need(dve, s_msk, t + 1)
                    V_.tensor_scalar(nmax[:, :], smax[:, :], -1.0 / ED, None, ALU.mult).then_inc(s_nmx, 1)
                t = i - 1
                if live(t):
                    need(dve, z_ps, t + 1)
                    need(dve, z_n, t)
                    V_.tensor_tensor(zb[:, :], bank(2)[0:P, 0:ED], zbias[:, :], ALU.add).then_inc(z_b, 1)
                    need(dve, z_b, t + 1)
                    V_.bn_stats(zstat[:, :], zb[:, :]).then_inc(z_st, 1)
                    plain(dve, (z_st, t + 1))
                    V_.bn_aggr(zmv[:, :], zstat[:, :]).then_inc(z_mv, 1)
                t = i - 4
                if live(t):
                    need(dve, o_ps, t + 1)
                    need(dve, g_h, t)
                    V_.reciprocal(rinv[:, :], psumr[:, par:par + 1]).then_inc(r_inv, 1)
                    need(dve, r_inv, t + 1)
                    V_.scalar_tensor_tensor(tile_of(H, t), bank(7)[0:P, 0:ED], rinv[:, 0:1], tile_of(H, t),
                                            ALU.mult, ALU.add).then_inc(g_h, 1)
                t = i - 1
                if live(t):
                    need(dve, z_rs, t + 1)
                    need(dve, h_g, t)
                    V_.tensor_scalar(zn[:, :], zb[:, :], zmv[:, 0:1], rs[:, 1, 1:2],
                                     ALU.subtract, ALU.mult).then_inc(z_n, 1)
                t = i - 4
                if live(t):
                    plain(dve, (g_h, t + 1), (g_mv, t))
                    V_.bn_stats(gstat[:, :], tile_of(H, t)).then_inc(g_st, 1)
                    plain(dve, (g_st, t + 1), (x2_ok, t))
                    V_.bn_aggr(gmv[:, :], gstat[:, :]).then_inc(g_mv, 1)
                t = i - 2
                if live(t):
                    need(dve, v_ps, t + 1)
                    need(dve, o_ps, t - 1)
                    V_.tensor_tensor(v[:, par, :], bank(4)[0:P, 0:ED], bvb[:, :], ALU.add).then_inc(v_sb, 1)
                t = i + 1
                if live(t):
                    stats_x(t, odd)
                t = i - 1
                if live(t):
                    plain(dve, (h_ok, t + 1))
                    V_.bn_stats(hstat[:, :], tile_of(H, t)).then_inc(h_st, 1)
                    plain(dve, (h_st, t + 1), (x1_ok, t))
                    V_.bn_aggr(hmv[:, :], hstat[:, :]).then_inc(h_mv, 1)
                t = i - 4
                if live(t):
                    need(dve, g_rs, t + 1)
                    need(dve, x2T_ps, t - 1)
                    if isinstance(t, int):
                        need(dve, x2_out[par], 16 * (t // 2))
                    else:
                        need(dve, x2_out[par], (t - par) * 8)
                    V_.tensor_scalar(x2[:, par, :], tile_of(H, t), gmv[:, 0:1], rs[:, 3, 1:2],
                                     ALU.subtract, ALU.mult).then_inc(x2_ok, 1)
                t = i - 5
                if live(t):
                    need(dve, l_ps, t + 1)
                    V_.tensor_tensor(LG[:, :, at(t)] if not isinstance(t, int) else LG[:, :, t:t + 1],
                                     bank(7)[0:P, 0:E].rearrange("p (e a) -> p e a", a=1),
                                     rbb[:, :].rearrange("p (e a) -> p e a", a=1), ALU.add).then_inc(l_sb, 1)
                t = i - 1
                if live(t):
                    need(dve, h_rs, t + 1)
                    need(dve, x1T_ps, t - 1)
                    V_.tensor_scalar(x1[:, odd, :], tile_of(H, t), hmv[:, 0:1], rs[:, 2, 1:2],
                                     ALU.subtract, ALU.mult).then_inc(x1_ok, 1)
                t = i + 1
                if live(t):
                    norm_x(t, odd)
            pipeline(dve, step, 7, 19)

            seq = 0

            def link(inst):
                nonlocal seq
                seq += 1
                inst.then_inc(d_seq, 1)
                dve.wait_ge(d_seq, seq)

            def over_e(a):
                return a.rearrange("p e t -> p t e")

            def per_tile(a):
                return rep(a.rearrange("p (a t) -> p a t", a=1), 1, E)

            dve.wait_ge(l_sb, TILES)
            dve.wait_ge(c_pool, 5)
            for k, s in enumerate(SHIFTS):
                link(V_.tensor_scalar(digit[:, k:k + 1], pidx[:, :], WAYS - 1, s if s else 2, ALU.bitwise_and,
                                      ALU.logical_shift_left if s else ALU.logical_shift_right))
            scores = LG
            for k, oh in enumerate((oh1, oh2)):
                link(V_.tensor_reduce(m12[:, k, :], over_e(scores[:, :, :]), AX.X, ALU.max))
                link(V_.tensor_tensor(eqm[:, :, :], scores[:, :, :], per_tile(m12[:, k, :]), ALU.is_equal))
                link(V_.tensor_tensor(eqm[:, :, :], eqm[:, :, :], erev[:, :, :], ALU.mult))
                link(V_.tensor_reduce(f12[:, k, :], over_e(eqm[:, :, :]), AX.X, ALU.max))
                link(V_.tensor_tensor(oh[:, :, :], eqm[:, :, :], per_tile(f12[:, k, :]), ALU.is_equal))
                if k == 0:
                    link(V_.scalar_tensor_tensor(lg2[:, :, :].rearrange("p e t -> p (e t)"),
                                                 oh1[:, :, :].rearrange("p e t -> p (e t)"), MASKED,
                                                 LG[:, :, :].rearrange("p e t -> p (e t)"), ALU.mult, ALU.add))
                    scores = lg2
            V_.tensor_tensor(dl[:, :], m12[:, 1, :], m12[:, 0, :], ALU.subtract).then_inc(r_dl, 1)
            dve.wait_ge(r_ed, 1)
            link(V_.tensor_scalar(dl[:, :], ed[:, :], 1.0, None, ALU.add))
            link(V_.reciprocal(gate[:, 0, :], dl[:, :]))
            link(V_.tensor_tensor(gate[:, 0, :], gate[:, 0, :], valid[:, :], ALU.mult))
            link(V_.tensor_tensor(gate[:, 1, :], gate[:, 0, :], ed[:, :], ALU.mult))
            V_.tensor_tensor(V[:, :, 0:TILES], oh1[:, :, :], per_tile(gate[:, 0, :]), ALU.mult)
            link(V_.tensor_tensor(V2[:, :, :], oh2[:, :, :], per_tile(gate[:, 1, :]), ALU.mult))
            link(V_.tensor_tensor(V[:, :, 0:TILES], V[:, :, 0:TILES], V2[:, :, :], ALU.add))
            link(V_.memset(thr[:, :].bitcast(fp32), 0.0))
            V_.tensor_copy(vrep[:, :, :].rearrange("p t (e w) -> p t e w", w=WAYS),
                           rep(V[:, :, :].rearrange("p e (t a) -> p t e a", a=1), 3, WAYS)).then_inc(r_V, 1)
            dve.wait_ge(r_VT, 1)
            for r, s in enumerate(SHIFTS):
                link(V_.tensor_tensor(cand[:, :], thr[:, :], digit[:, r:r + 1], ALU.bitwise_or))
                link(V_.tensor_scalar(junk[:, :].rearrange("p (a b) -> p a b", a=6), pall[:, :, 0:4 * P],
                                      cand[:, :].bitcast(fp32), None, ALU.is_ge, ALU.add, accum_out=cnt[:, 0:1]))
                V_.tensor_scalar(won[:, :], cnt[:, :], CAP - 0.5, None, ALU.is_ge).then_inc(r_won, 1)
                dve.wait_ge(r_n, r + 1)
                link(V_.tensor_scalar(dwon[:, :], ps[0][:, 0:1], 0.25 if s == 0 else 1.0, -1.0, ALU.mult, ALU.add))
                link(V_.tensor_scalar(dwon[:, :], dwon[:, :], s, None, ALU.logical_shift_left))
                link(V_.tensor_tensor(thr[:, :], thr[:, :], dwon[:, :], ALU.bitwise_or))
            V_.tensor_scalar(thrrow[:, :], pick[:, :], thr[:, :].bitcast(fp32), None, ALU.mult).then_inc(r_pick, 1)
            dve.wait_ge(r_thr, 1)
            link(V_.tensor_copy(thrb[:, :], ps[0][0:P, 0:E]))
            thre = rep(thrb[:, :].rearrange("p (e a) -> p e a", a=1), 2, TILES)
            V_.tensor_tensor(ge[:, 0, :, :], V[:, :, 0:TILES], thre, ALU.is_gt)
            V_.tensor_tensor(ge[:, 1, :, :], V[:, :, 0:TILES], thre, ALU.is_equal).then_inc(r_ge, 1)
            link(V_.tensor_scalar(okeq[:, :, :], V[:, :, 0:TILES], 0.0, None, ALU.is_gt))
            dve.wait_ge(r_ge, 1)
            dve.wait_ge(r_pos, 1)
            n = 2 * E * TILES
            link(V_.tensor_tensor_scan(tincl[:, :, :].rearrange("p a t -> p (a t)"),
                                       keep0[:, :, :].rearrange("p a t -> p (a t)"), bank(3)[0:P, 0:n], 0.0,
                                       ALU.mult, ALU.add))
            posf = pos[:, :, :, :].rearrange("p s e t -> p (s e t)")
            link(V_.tensor_tensor(posf, tincl[:, :, :].rearrange("p a t -> p (a t)"), bank(3)[0:P, 0:n], ALU.subtract))
            link(V_.tensor_tensor(posf, posf, bank(2)[0:P, 0:n], ALU.add))
            above = rep(tincl[:, 0:E, TILES - 1:TILES], 2, TILES)
            link(V_.tensor_tensor(pos[:, 1, :, :], pos[:, 1, :, :], above, ALU.add))
            link(V_.tensor_tensor(okeq[:, :, :], okeq[:, :, :], ge[:, 1, :, :], ALU.mult))
            link(V_.tensor_scalar(ok[:, :, :], pos[:, 1, :, :], CAP - 0.5, None, ALU.is_le))
            link(V_.tensor_tensor(okeq[:, :, :], okeq[:, :, :], ok[:, :, :], ALU.mult))
            V_.tensor_tensor(pos[:, 0, :, :], pos[:, 0, :, :], base1[:, :, :], ALU.add)
            link(V_.tensor_tensor(pos[:, 1, :, :], pos[:, 1, :, :], base1[:, :, :], ALU.add))
            V_.tensor_tensor(pos[:, 0, :, :], pos[:, 0, :, :], ge[:, 0, :, :], ALU.mult)
            link(V_.tensor_tensor(pos[:, 1, :, :], pos[:, 1, :, :], okeq[:, :, :], ALU.mult))
            link(V_.tensor_tensor(aslot[:, :, :], pos[:, 0, :, :], pos[:, 1, :, :], ALU.add))
            for k, oh in enumerate((oh1, oh2)):
                link(V_.tensor_tensor(eqm[:, :, :], aslot[:, :, :], oh[:, :, :], ALU.mult))
                link(V_.tensor_reduce(s12[:, k, :], over_e(eqm[:, :, :]), AX.X, ALU.add))
            s12f = s12[:, :, :].rearrange("p k t -> p (k t)")
            link(V_.tensor_scalar(wtok[:, :, :].rearrange("p k t -> p (k t)"), s12f, 0.5, None, ALU.is_ge))
            link(V_.tensor_tensor(wtok[:, :, :], wtok[:, :, :], gate[:, :, :], ALU.mult))
            BIG = 1.5 * 2.0 ** 23
            link(V_.tensor_scalar(hi[:, :], s12f, 1.0 / P, -0.5 - 0.5 / P, ALU.mult, ALU.add))
            link(V_.tensor_scalar(hi[:, :], hi[:, :], BIG, None, ALU.add))
            link(V_.tensor_scalar(hi[:, :], hi[:, :], -BIG, None, ALU.add))
            link(V_.scalar_tensor_tensor(lo[:, :], hi[:, :], -float(P), s12f, ALU.mult, ALU.add))
            link(V_.tensor_scalar(lo[:, :], lo[:, :], -1.0, None, ALU.add))
            hib = rep(hi[:, :].rearrange("p (q a) -> p q a", a=1), 2, COLS)
            lob = rep(lo[:, :].rearrange("p (q a) -> p q a", a=1), 2, P)
            link(V_.tensor_tensor(ohhi[:, :, :], hib, rep(iorow[:, 0:COLS].rearrange("p (a c) -> p a c", a=1), 1, Q),
                                  ALU.is_equal))
            V_.tensor_scalar(ohval[:, :, 0, :], ohhi[:, :, :], row1[:, 0:1], None, ALU.mult)
            V_.tensor_tensor(ohval[:, :, 1, :], ohhi[:, :, :],
                             rep(qidx[:, :].rearrange("p (q a) -> p q a", a=1), 2, COLS), ALU.mult).then_inc(r_val, 1)
            V_.tensor_tensor(ohlo[:, :, :], lob, rep(iorow[:, :].rearrange("p (a c) -> p a c", a=1), 1, Q),
                             ALU.is_equal).then_inc(r_lo, 1)
            dve.wait_ge(r_list, 1)
            link(V_.tensor_copy(drow[:, :], bank(4)[0:P, 0:COLS]))
            link(V_.tensor_scalar(kch[:, :], bank(4)[0:P, COLS:2 * COLS], TILES - 0.5, None, ALU.is_ge))
            link(V_.tensor_scalar(empty[:, :], drow[:, :], 0.5, None, ALU.is_le))
            link(V_.scalar_tensor_tensor(drow[:, :], bank(4)[0:P, COLS:2 * COLS], float(P), drow[:, :],
                                         ALU.mult, ALU.add))
            link(V_.tensor_scalar(drow[:, :], drow[:, :], -1.0, None, ALU.add))
            link(V_.scalar_tensor_tensor(idf[:, :], kch[:, :], -float(TILES * P), drow[:, :], ALU.mult, ALU.add))
            link(V_.tensor_scalar(idf[:, :], idf[:, :], 0.0, None, ALU.max))
            V_.tensor_copy(gidx[:, :], idf[:, :])
            link(V_.tensor_tensor(empty[:, :], empty[:, :], trash[:, :], ALU.mult))
            link(V_.tensor_tensor(drow[:, :], drow[:, :], empty[:, :], ALU.add))
            V_.tensor_copy(didx[:, :], drow[:, :]).then_inc(r_idx, 1)

            def take_xg(e, par):
                dve.wait_ge(gT_ps, e + 1)
                for c in range(EC):
                    m = V_.tensor_copy(xgT[:, par, c, :], bank(4 + c)[:, 0:SLOTS])
                m.then_inc(gT_sb, 1)

            def take_y(e, par, first=False):
                if not first:
                    dve.wait_ge(y_out[par], e_count(e, par, 16 * JT) - 16 * JT)
                for j in range(JT):
                    dve.wait_ge(y_ps, e * JT + j + 1)
                    b2e = b2b[:, e, :] if isinstance(e, int) else b2b[:, bass.ds(e, 1), :].rearrange("p a f -> p (a f)")
                    V_.tensor_tensor(y[:, par, j, :], bank(6 + j % 2)[0:P, 0:ED], b2e, ALU.add).then_inc(y_sb, 1)

            take_xg(0, 0)
            take_xg(1, 1)
            take_y(0, 0, first=True)
            take_xg(2, 0)
            take_y(1, 1, first=True)
            with dve.Fori(0, (E - 4) // 2) as j:
                for par in range(2):
                    e = j * 2 + 2 + par
                    take_xg(e + 1, 1 - par)
                    take_y(e, par)
            take_xg(E - 1, 1)
            take_y(E - 2, 0)
            take_y(E - 1, 1)

            def summed(t, par, first=False):
                dve.wait_ge(a_ok, t + 1)
                if not first:
                    dve.wait_ge(n_ok, t - 1)
                V_.scalar_tensor_tensor(yc[:, par, :], yin[:, par, 1, :], col(wtok[:, 1, :], t), ya[:, par, :],
                                        ALU.mult, ALU.add).then_inc(c_ok, 1)
                dve.wait_ge(c_ok, t + 1)
                V_.bn_stats(ystat[:, :], yc[:, par, :]).then_inc(c_st, 1)
                plain(dve, (c_st, t + 1))
                V_.bn_aggr(ymv[:, par, :], ystat[:, :]).then_inc(c_mv, 1)

            def normed(t, par, first=False):
                dve.wait_ge(c_rs, t + 1)
                if not first:
                    dve.wait_ge(o_g, t - 1)
                V_.tensor_scalar(yn[:, par, :], yc[:, par, :], ymv[:, par, 0:1], yrs[:, par, 1:2],
                                 ALU.subtract, ALU.mult).then_inc(n_ok, 1)

            summed(0, 0, True)
            summed(1, 1, True)
            normed(0, 0, True)
            normed(1, 1, True)
            with dve.Fori(0, (TILES - 2) // 2) as j:
                t = j * 2 + 2
                summed(t, 0)
                summed(t + 1, 1)
                normed(t, 0)
                normed(t + 1, 1)

        @block.gpsimd
        def _(pool):
            G = nc.gpsimd
            p_seq = sem("p_seq")
            seq = 0

            def link(inst):
                nonlocal seq
                seq += 1
                inst.then_inc(p_seq, 1)
                pool.wait_ge(p_seq, seq)

            link(G.memset(ident[:, :], 0.0))
            G.affine_select(out=ident[:, :], in_=ident[:, :], compare_op=ALU.not_equal, fill=1.0, base=0,
                            pattern=[[-1, 128]], channel_multiplier=1).then_inc(c_pool, 1)
            G.memset(neghalf[:, :], -0.5)
            G.memset(onesrow[:, :], 1.0)
            link(G.memset(amask[:, :], MASKED))
            for m in range(PER):
                lo_, hi_ = m * L, (m + 1) * L
                blk = amask[:, lo_:hi_]
                link(G.memset(blk, 0.0))
                link(G.affine_select(out=blk, in_=blk, compare_op=ALU.is_ge, fill=MASKED, base=-lo_,
                                     pattern=[[0, L]], channel_multiplier=1))
                link(G.affine_select(out=blk, in_=blk, compare_op=ALU.is_ge, fill=MASKED, base=hi_ - 1,
                                     pattern=[[0, L]], channel_multiplier=-1))
            G.affine_select(out=amask[:, :], in_=amask[:, :], compare_op=ALU.not_equal, fill=MASKED, base=0,
                            pattern=[[-1, P]], channel_multiplier=1).then_inc(c_pool, 1)
            G.memset(onesf[:, :], 1.0)
            link(G.memset(onesb[:, :], 1.0))
            G.affine_select(out=below[:, :], in_=onesb[:, :], compare_op=ALU.is_gt, fill=0.0, base=0,
                            pattern=[[1, 128]], channel_multiplier=-1)
            g3 = grp[:, :].rearrange("p (e w) -> p e w", w=WAYS)
            link(G.affine_select(out=g3, in_=onesb[:, :].rearrange("p (e w) -> p e w", w=WAYS), compare_op=ALU.is_ge,
                                 fill=0.0, base=0, pattern=[[-WAYS, E], [0, WAYS]], channel_multiplier=1))
            link(G.affine_select(out=g3, in_=g3, compare_op=ALU.is_ge, fill=0.0, base=WAYS - 1,
                                 pattern=[[WAYS, E], [0, WAYS]], channel_multiplier=-1))
            G.affine_select(out=pick[:, :], in_=onesf[:, 0:E], compare_op=ALU.is_equal, fill=0.0, base=0,
                            pattern=[[-WAYS, E]], channel_multiplier=1).then_inc(c_pool, 1)
            link(G.memset(valid[:, :], 1.0))
            G.affine_select(out=valid[:, TILES - 1:TILES], in_=valid[:, TILES - 1:TILES], compare_op=ALU.is_gt,
                            fill=0.0, base=LIVE_LAST, pattern=[[0, 1]], channel_multiplier=-1)
            G.affine_select(out=valid[:, 0:TILES - 1], in_=valid[:, 0:TILES - 1], compare_op=ALU.is_gt,
                            fill=0.0, base=PER * L, pattern=[[0, TILES - 1]], channel_multiplier=-1)
            G.memset(keep0[:, :, :], 1.0)
            link(G.memset(row1[:, :], 0.0))
            G.memset(keep0[:, :, 0:1], 0.0)
            f = dict(allow_small_or_imprecise_dtypes=True)
            G.iota(erev[:, :, :], [[-1, E], [0, TILES]], base=E, channel_multiplier=0, **f)
            G.iota(base1[:, :, :], [[SLOTS, E], [0, TILES]], base=1, channel_multiplier=0, **f)
            G.iota(iorow[:, :], [[1, P]], base=0, channel_multiplier=0, **f)
            G.iota(qidx[:, :], [[1, Q]], base=0, channel_multiplier=0, **f)
            G.iota(trash[:, :], [[P, COLS]], base=TRASH + 1, channel_multiplier=1, **f)
            G.iota(row1[:, :], [[0, 1]], base=1, channel_multiplier=1, **f)
            G.iota(pidx[:, :], [[0, 1]], base=0, channel_multiplier=1).then_inc(c_pool, 1)
            link(G.memset(zero, 0.0))
            per = HC * SLOTS // ED
            yz = y_rows[0:TRASH, :].rearrange("(q p) f -> p q f", p=P)
            k = 0
            while k * per < Q:
                m = min(per, Q - k * per)
                pool.dma_start(yz[:, k * per:k * per + m, :],
                               zero[:, 0:m * ED].rearrange("p (q f) -> p q f", f=ED)).then_inc(s_fill, 16)
                k += 1
            assert k == 4
            G.memset(neghalf[:, :], -0.5).then_inc(c_pool, 1)
            pool.wait_ge(c_pool, 5)
            pool.wait_ge(c_dve, 2)

            def rstd(slot, mv, ready, n, mid, done):
                plain(pool, (ready, n))
                G.tensor_scalar(rs[:, slot, 0:1], mv[:, 1:2], EPS, None, ALU.add).then_inc(mid, 1)
                need(pool, mid, n)
                G.tensor_tensor(rs[:, slot, 1:2], rs[:, slot, 0:1], neghalf[:, :], ALU.pow).then_inc(done, 1)

            rstd(0, xmv, x_mv, 1, x_rs0, x_rs)

            def step(i, par):
                t = i - 1
                if live(t):
                    rstd(1, zmv, z_mv, t + 1, z_rs0, z_rs)
                    need(pool, z_n, t + 1)
                    G.tensor_tensor(tile_of(H, t), zn[:, :], g2m[:, :], ALU.mult).then_inc(h_g, 1)
                    plain(pool, (h_g, t + 1))
                    G.tensor_tensor(tile_of(H, t), tile_of(H, t), posb[:, :], ALU.add).then_inc(h_ok, 1)
                t = i - 4
                if live(t):
                    need(pool, x2_ok, t)
                    rstd(3, gmv, g_mv, t + 1, g_rs0, g_rs)
                t = i + 1
                if live(t):
                    need(pool, x_n, t)
                    rstd(0, xmv, x_mv, t + 1, x_rs0, x_rs)
                t = i - 1
                if live(t):
                    need(pool, x1_ok, t)
                    rstd(2, hmv, h_mv, t + 1, h_rs0, h_rs)
            pipeline(pool, step, 7, 21)

            pool.wait_ge(r_idx, 1)
            for par in range(2):
                pool.wait_ge(x2_out[par], 16 * (TILES // 2))
            pool.wait_ge(s_fill, 16 * 4)

            def icol(buf, e):
                return buf[:, e * JT:(e + 1) * JT] if isinstance(e, int) else buf[:, bass.ds(e * JT, JT)]

            def gather(e, par):
                G.tensor_copy(dst[:, par, :], icol(didx, e))
                G.tensor_copy(gst[:, par, :], icol(gidx, e)).then_inc(i_st, 1)
                plain(pool, (i_st, e + 1))
                for j in range(JT):
                    pool.indirect_dma_start(
                        xg[:, par, j, :], None, x2_rows,
                        bass.IndirectOffsetOnAxis(ap=gst[:, par, j:j + 1], axis=0)).then_inc(g_in[par], 16)

            def scatter(e, par):
                for j in range(JT):
                    plain(pool, (y_sb, e * JT + j + 1))
                    pool.indirect_dma_start(
                        y_rows, bass.IndirectOffsetOnAxis(ap=dst[:, par, j:j + 1], axis=0),
                        y[:, par, j, :], None).then_inc(y_out[par], 16)

            gather(0, 0)
            gather(1, 1)

            def serve(e, par, more=True):
                scatter(e, par)
                pool.wait_ge(y_ps, (e + 1) * JT)
                if more:
                    pool.wait_ge(y_out[par], e_count(e, par, 16 * JT))
                    gather(e + 2, par)
            with pool.Fori(0, (E - 2) // 2) as j:
                for par in range(2):
                    serve(j * 2 + par, par)
            serve(E - 2, 0, more=False)
            serve(E - 1, 1, more=False)

            with pool.Fori(0, TILES) as t:
                G.tensor_tensor(tile_of(H, t), tile_of(H, t), lnb[:, :], ALU.add).then_inc(hb, 1)
            pool.wait_ge(hb, TILES)

            def rstd4(t, par):
                plain(pool, (c_mv, t + 1))
                G.tensor_scalar(yrs[:, par, 0:1], ymv[:, par, 1:2], EPS, None, ALU.add).then_inc(c_rs0, 1)
                pool.wait_ge(c_rs0, t + 1)
                G.tensor_tensor(yrs[:, par, 1:2], yrs[:, par, 0:1], neghalf[:, :], ALU.pow).then_inc(c_rs, 1)

            def finish(t, par, first=False):
                pool.wait_ge(n_ok, t + 1)
                if not first:
                    pool.wait_ge(o_out[par], 32 * (t // 2) if isinstance(t, int) else (t - par) * 16)
                G.tensor_tensor(yo[:, par, :], yn[:, par, :], lng[:, :], ALU.mult).then_inc(o_g, 1)
                plain(pool, (o_g, t + 1))
                G.tensor_tensor(yo[:, par, :], yo[:, par, :], tile_of(H, t), ALU.add).then_inc(o_ok, 1)

            rstd4(0, 0)
            rstd4(1, 1)
            finish(0, 0, True)
            finish(1, 1, True)
            with pool.Fori(0, (TILES - 2) // 2) as j:
                t = j * 2 + 2
                rstd4(t, 0)
                rstd4(t + 1, 1)
                finish(t, 0)
                finish(t + 1, 1)


def kernel(**inputs):
    import numpy as np
    import concourse.bacc as bacc
    from concourse.bass_utils import run_bass_kernel_spmd

    a = {k: np.asarray(v_) for k, v_ in inputs.items()}
    B, C, S, _ = a["x"].shape
    ED = a["L0_tok_W_proj"].shape[1]
    n = round((a["L0_tok_pos_emb"].shape[1] - 1) ** 0.5)
    p = S // n
    E, D, HID = a["L0_ffn_w1"].shape
    col = lambda w: w.reshape(-1, 128).T
    arrays = {
        "x": a["x"].reshape(B, C, n, p, n, p).transpose(0, 2, 4, 3, 5, 1).reshape(B, n * n, p * p * C),
        "ln1_g": col(a["L0_tok_ln1_g"]), "ln1_b": col(a["L0_tok_ln1_b"]),
        "w_proj": a["L0_tok_W_proj"], "b_proj": a["L0_tok_b_proj"].reshape(1, ED),
        "ln2_g": a["L0_tok_ln2_g"].reshape(1, ED), "ln2_b": a["L0_tok_ln2_b"].reshape(1, ED),
        "cls_token": a["L0_tok_cls_token"].reshape(1, ED), "pos_emb": a["L0_tok_pos_emb"][0],
        "wq_t": a["L0_attn_Wq"].T, "bq": col(a["L0_attn_bq"]),
        "wk_t": a["L0_attn_Wk"].T, "bk": col(a["L0_attn_bk"]),
        "wv_t": a["L0_attn_Wv"].T, "bv": a["L0_attn_bv"].reshape(1, ED),
        "router_w": a["L0_ffn_router_w"], "router_b": a["L0_ffn_router_b"].reshape(1, E),
        "w1": a["L0_ffn_w1"], "b1": a["L0_ffn_b1"].reshape(E * HID // 128, 128).T,
        "w2": a["L0_ffn_w2"], "b2": a["L0_ffn_b2"].reshape(1, -1),
        "ln_g": a["L0_ffn_ln_g"].reshape(1, ED), "ln_b": a["L0_ffn_ln_b"].reshape(1, ED),
    }
    arrays = {f"in_{k}": np.ascontiguousarray(v_) for k, v_ in arrays.items()}
    nc = bacc.Bacc("TRN2", target_bir_lowering=False, num_devices=1)
    ins = [nc.dram_tensor(k, v_.shape, mybir.dt.from_np(v_.dtype), kind="ExternalInput").ap()
           for k, v_ in arrays.items()]
    out = nc.dram_tensor("out", (B * (n * n + 1), ED), fp32, kind="ExternalOutput").ap()
    vit_tower(nc, *ins, out)
    got = run_bass_kernel_spmd(nc, [arrays], core_ids=[0])
    return got.results[0]["out"].reshape(B, n * n + 1, ED)
```

```python
from contextlib import ExitStack

import concourse.bass as bass
from concourse import mybir

fp32 = mybir.dt.float32
fp32r = mybir.dt.float32r
bf16 = mybir.dt.bfloat16
i32 = mybir.dt.int32
u32 = mybir.dt.uint32
ALU = mybir.AluOpType
ACT = mybir.ActivationFunctionType
AX = mybir.AxisListType

EPS = 1e-5
MASKED = -3.0e38


def rep(ap, dim, n):
    shape = list(ap.shape)
    shape[dim] = n
    return ap.broadcast_to(shape)


def vit_tower(nc, x, ln1_g, ln1_b, w_proj, b_proj, ln2_g, ln2_b, cls_token, pos_emb,
              wq_t, bq, wk_t, bk, wv_t, bv, router_w, router_b, w1, b1, w2, b2, ln_g, ln_b, out):
    IMAGES, PATCHES, PD = x.shape
    ED = w_proj.shape[1]
    L = PATCHES + 1
    PER = 128 // L
    P = 112
    TILES = -(-IMAGES // PER)
    LIVE_LAST = (IMAGES - PER * (TILES - 1)) * L
    PC = PD // 128
    EC = ED // 128
    E, _, HID = w1.shape
    HC = HID // 128
    CAP = int(IMAGES * L * 1.5 / E)
    JT = -(-CAP // P)
    SLOTS = JT * P
    COLS = E * JT
    PAD = 24
    Q = 2 * TILES
    HALF = PD // 2
    TRASH = Q * P
    WAYS = 16
    SHIFTS = [26, 22, 18, 14, 10, 6, 2, 0]

    ctx = ExitStack()
    with ctx:
        def sb(name, shape, dt=fp32):
            return ctx.enter_context(nc.sbuf_tensor(name, shape, dt))

        def sem(name):
            return ctx.enter_context(nc.semaphore(name))

        x2_rows = nc.dram_tensor("x2_rows", [TILES * P, ED], fp32, kind="Internal").ap()
        y_rows = nc.dram_tensor("y_rows", [TRASH + COLS * P, ED], fp32, kind="Internal").ap()

        ident = sb("ident", [128, 128])
        wproj = sb("wproj", [128, PC, ED])
        ln1g = sb("ln1g", [128, PC])
        ln1b = sb("ln1b", [128, PC])
        onesrow = sb("onesrow", [1, 128])
        bproj = sb("bproj", [1, ED])
        zbias = sb("zbias", [P, ED])
        g2m = sb("g2m", [P, ED])
        posb = sb("posb", [P, ED])
        posadd = sb("posadd", [P, ED])
        wq = sb("wq", [128, EC, ED])
        wk = sb("wk", [128, EC, ED])
        wv = sb("wv", [128, EC, ED])
        bqk = sb("bqk", [128, 2 * EC])
        bvb = sb("bvb", [P, ED])
        amask = sb("amask", [P, P])
        rw = sb("rw", [128, EC, E])
        rbb = sb("rbb", [P, E])
        neghalf = sb("neghalf", [P, 1])
        lng = sb("lng", [P, ED])
        lnb = sb("lnb", [P, ED])
        b1t = sb("b1t", [128, E * HC])
        b2b = sb("b2b", [P, E, ED])
        stage = sb("stage", [128, 2 * EC * HID])
        xin = stage[0:P, 0:2 * PD].rearrange("p (s f) -> p s f", s=2)
        xn = stage[0:P, 2 * PD:4 * PD].rearrange("p (s f) -> p s f", s=2)
        xnT = stage[:, 4 * PD:4 * PD + PC * P].rearrange("p (c r) -> p c r", c=PC)
        w1r = stage[:, 0:EC * HID].rearrange("p (c h) -> p c h", c=EC)
        w2r = stage[:, EC * HID:2 * EC * HID].rearrange("p (k o) -> p k o", k=HC)
        rows = sb("rows", [P, 4 * JT * ED])
        xg = rows[:, 0:2 * JT * ED].rearrange("p (s j f) -> p s j f", s=2, j=JT)
        y = rows[:, 2 * JT * ED:4 * JT * ED].rearrange("p (s j f) -> p s j f", s=2, j=JT)
        ohlo = rows[:, 0:Q * P // 2].bitcast(bf16).rearrange("p (q c) -> p q c", q=Q)
        ohhi = rows[:, Q * P // 2:Q * (P + COLS) // 2].bitcast(bf16).rearrange("p (q c) -> p q c", q=Q)
        yin = rows[:, 0:8 * ED].rearrange("p (s t k f) -> p s t k f", s=2, t=2, k=2)
        scratch128 = sb("scratch", [128, 14 * ED])
        scratch = scratch128[0:P, :]
        zero = scratch
        junk = scratch128[:, 0:3 * 4 * P].bitcast(bf16)
        vrep = scratch[:, 0:PAD * 128].rearrange("p (t m) -> p t m", m=128)

        def tiles(first, n):
            return scratch[:, first * ED:(first + n) * ED].rearrange("p (a f) -> p a f", f=ED)

        ya, yc, yd, yu = tiles(0, 2), tiles(2, 2), tiles(4, 2), tiles(6, 2)
        yo = tiles(8, 4)
        xstat = sb("xstat", [P, 2, 6])
        xmv = sb("xmv", [P, 2])
        zb = sb("zb", [P, ED])
        zstat = sb("zstat", [P, 6])
        zmv = sb("zmv", [P, 2])
        zn = sb("zn", [P, ED])
        hstat = sb("hstat", [P, 6])
        hmv = sb("hmv", [P, 2])
        x1 = sb("x1", [P, 2, ED])
        x1T = sb("x1T", [128, 2, EC * P])
        qkT = sb("qkT", [128, 2 * EC, P])
        v = sb("v", [P, 2, ED])
        masked = sb("masked", [P, P])
        smax = sb("smax", [P, 1])
        nmax = sb("nmax", [P, 1])
        prob = sb("prob", [P, P])
        psumr = sb("psumr", [P, 2])
        rinv = sb("rinv", [P, 1])
        probT = sb("probT", [P, P])
        gstat = sb("gstat", [P, 6])
        gmv = sb("gmv", [P, 2])
        x2 = sb("x2", [P, 2, ED])
        x2T = sb("x2T", [128, EC * P])
        rs = sb("rs", [P, 4, 2])
        H = sb("H", [P, TILES, ED])
        LG = sb("LG", [P, E, TILES])
        erev = sb("erev", [P, E, TILES])
        eqm = sb("eqm", [P, E, TILES])
        oh1 = sb("oh1", [P, E, TILES])
        oh2 = sb("oh2", [P, E, TILES])
        lg2 = sb("lg2", [P, E, TILES])
        m12 = sb("m12", [P, 2, TILES])
        f12 = sb("f12", [P, 2, TILES])
        dl = sb("dl", [P, TILES])
        ed = sb("ed", [P, TILES])
        gate = sb("gate", [P, 2, TILES])
        valid = sb("valid", [P, TILES])
        V = sb("V", [P, E, PAD])
        V2 = sb("V2", [P, E, TILES])
        digit = sb("digit", [128, len(SHIFTS)], i32)
        pidx = sb("pidx", [128, 1], i32)
        thr = sb("thr", [128, 1], i32)
        cand = sb("cand", [128, 1], i32)
        cnt = sb("cnt", [128, 1])
        won = sb("won", [128, 1], bf16)
        dwon = sb("dwon", [128, 1], i32)
        grp = sb("grp", [128, 128], bf16)
        pick = sb("pick", [128, E])
        thrrow = sb("thrrow", [128, E])
        thrb = sb("thrb", [P, E])
        onesf = sb("onesf", [128, 128])
        onesb = sb("onesb", [128, 128], bf16)
        below = sb("below", [128, 128], bf16)
        ge = sb("ge", [P, 2, E, TILES], bf16)
        keep0 = sb("keep0", [P, 2 * E, TILES])
        tincl = sb("tincl", [P, 2 * E, TILES])
        pos = sb("pos", [P, 2, E, TILES])
        okeq = sb("okeq", [P, E, TILES])
        ok = sb("ok", [P, E, TILES])
        base1 = sb("base1", [P, E, TILES])
        aslot = sb("aslot", [P, E, TILES])
        s12 = sb("s12", [P, 2, TILES])
        hi = sb("hi", [P, Q])
        lo = sb("lo", [P, Q])
        wtok = sb("wtok", [P, 2, TILES])
        iorow = sb("iorow", [P, P])
        qidx = sb("qidx", [P, Q])
        row1 = sb("row1", [P, 1])
        iorowb = sb("iorowb", [P, P], bf16)
        ohval = sb("ohval", [P, Q, 2, COLS], bf16)
        trash = sb("trash", [P, COLS])
        drow = sb("drow", [P, COLS])
        empty = sb("empty", [P, COLS])
        kch = sb("kch", [P, COLS])
        idf = sb("idf", [P, COLS])
        gidx = sb("gidx", [P, COLS], u32)
        didx = sb("didx", [P, COLS], u32)
        w1h = sb("w1h", [128, EC, HID], fp32r)
        w1l = sb("w1l", [128, EC, HID], fp32r)
        w2h = sb("w2h", [128, HC, ED], fp32r)
        w2l = sb("w2l", [128, HC, ED], fp32r)
        gst = sb("gst", [P, 2, JT], u32)
        dst = sb("dst", [P, 2, JT], u32)
        xgh = sb("xgh", [128, EC, SLOTS], fp32r)
        xgl = sb("xgl", [128, EC, SLOTS], fp32r)
        hr = sb("hr", [128, 2, SLOTS])
        hh = sb("hh", [128, HC, SLOTS], fp32r)
        hl = sb("hl", [128, HC, SLOTS], fp32r)
        ystat = sb("ystat", [P, 2, 6])
        ymv = sb("ymv", [P, 2, 2])
        yrs = sb("yrs", [P, 2, 2])

        ps = [ctx.enter_context(nc.psum_tensor(f"ps{b}", [128, 512], fp32)) for b in range(2)]
        pall = ctx.enter_context(nc.psum_tensor("pall", [128, 6, 512], fp32))

        def bank(b):
            return ps[b][:, :] if b < 2 else pall[:, b - 2, :]

        c_w = sem("c_w"); c_g = sem("c_g"); c_a = sem("c_a"); c_l = sem("c_l"); c_pool = sem("c_pool"); c_dve = sem("c_dve"); c_pe = sem("c_pe")
        s_zero = sem("s_zero"); s_xz = sem("s_xz"); s_fill = sem("s_fill")
        x_in = [sem("x_in0"), sem("x_in1")]
        x_st = sem("x_st"); x_mv = sem("x_mv"); x_rs0 = sem("x_rs0"); x_rs = sem("x_rs"); x_n = sem("x_n")
        xT_ps = sem("xT_ps"); xT_sb = sem("xT_sb"); z_ps = sem("z_ps"); z_b = sem("z_b")
        z_st = sem("z_st"); z_mv = sem("z_mv"); z_rs0 = sem("z_rs0"); z_rs = sem("z_rs"); z_n = sem("z_n")
        h_g = sem("h_g"); h_ok = sem("h_ok")
        h_st = sem("h_st"); h_mv = sem("h_mv"); h_rs0 = sem("h_rs0"); h_rs = sem("h_rs"); x1_ok = sem("x1_ok")
        x1T_ps = sem("x1T_ps"); x1T_sb = sem("x1T_sb"); qk_ps = sem("qk_ps"); v_ps = sem("v_ps")
        qk_sb = sem("qk_sb"); v_sb = sem("v_sb"); s_ps = sem("s_ps"); s_msk = sem("s_msk"); s_nmx = sem("s_nmx")
        p_ok = sem("p_ok"); pT_ps = sem("pT_ps"); pT_sb = sem("pT_sb"); o_ps = sem("o_ps")
        r_inv = sem("r_inv"); g_h = sem("g_h"); g_st = sem("g_st"); g_mv = sem("g_mv")
        g_rs0 = sem("g_rs0"); g_rs = sem("g_rs"); x2_ok = sem("x2_ok")
        x2_out = [sem("x2_out0"), sem("x2_out1")]
        x2T_ps = sem("x2T_ps"); x2T_sb = sem("x2T_sb"); l_ps = sem("l_ps"); l_sb = sem("l_sb")
        d_seq = sem("d_seq")
        r_dl = sem("r_dl"); r_ed = sem("r_ed"); r_V = sem("r_V"); r_VT = sem("r_VT"); r_won = sem("r_won")
        r_n = sem("r_n"); r_pick = sem("r_pick"); r_thr = sem("r_thr"); r_ge = sem("r_ge"); r_pos = sem("r_pos")
        r_lo = sem("r_lo"); r_hi = sem("r_hi"); r_val = sem("r_val"); r_list = sem("r_list"); r_idx = sem("r_idx")
        w1_in = sem("w1_in"); w2_in = sem("w2_in")
        w1_hi = sem("w1_hi"); w1_lo = sem("w1_lo"); w2_hi = sem("w2_hi"); w2_lo = sem("w2_lo")
        i_st = sem("i_st")
        i_dst = sem("i_dst")
        g_in = [[sem(f"g_in{a}_{b}") for b in range(JT)] for a in range(2)]
        gT_ps = sem("gT_ps"); x_hi = sem("x_hi"); x_lo = sem("x_lo"); h_hi = sem("h_hi"); h_lo = sem("h_lo"); u_ps = sem("u_ps"); u_sb = sem("u_sb")
        y_ps = sem("y_ps"); y_free = sem("y_free"); y_sb = sem("y_sb");
        y_out = [sem("y_out0"), sem("y_out1")]
        hb = sem("hb")
        z_in = [sem("z_in0"), sem("z_in1")]
        a_ok = sem("a_ok"); c_ok = sem("c_ok"); c_st = sem("c_st"); c_mv = sem("c_mv"); c_rs0 = sem("c_rs0")
        c_rs = sem("c_rs"); c_d = sem("c_d"); u_ok = sem("u_ok"); o_ok = sem("o_ok")
        o_out = [sem("o_out0"), sem("o_out1")]

        block = ctx.enter_context(nc.Block())

        def live(t):
            return not isinstance(t, int) or 0 <= t < TILES

        def need(eng, s, n):
            if not isinstance(n, int) or n > 0:
                eng.wait_ge(s, n)

        turn = {}

        def plain(eng, *waits):
            for w, n in waits:
                need(eng, w, n)
            if not isinstance(waits[0][1], int):
                if eng.engine not in turn:
                    turn[eng.engine] = sem(f"turn_{len(turn)}")
                eng.sem_inc(turn[eng.engine], 1)

        N_W, N_G, N_A, N_L = 16 * 4, 16 * 4 * PER, 16 * 8, 16 * 4
        SKEW = 5
        STEPS = TILES + SKEW

        def pipeline(eng, step, lo_, hi_, first=0):
            assert (hi_ - lo_) % 2 == 0
            for i in range(first, lo_):
                step(i, i % 2)
            with eng.Fori(0, (hi_ - lo_) // 2) as j:
                i = j * 2 + lo_
                step(i, lo_ % 2)
                step(i + 1, (lo_ + 1) % 2)
            for i in range(hi_, STEPS):
                step(i, i % 2)

        def at(t):
            return t if isinstance(t, int) else bass.ds(t, 1)

        def tile_of(buf, t):
            if isinstance(t, int):
                return buf[:, t, :]
            return buf[:, bass.ds(t, 1), :].rearrange("p a f -> p (a f)")

        def col(buf, t):
            return buf[:, t:t + 1] if isinstance(t, int) else buf[:, bass.ds(t, 1)]

        def ycount(q, par):
            return 32 * (q // 2 + 1) if isinstance(q, int) else (q - par + 2) * 16

        def e_count(e, par, n):
            return (e // 2 + 1) * n if isinstance(e, int) else (e - par + 2) * (n // 2)

        @block.sync
        def _(sp):
            def load_x(t, par):
                n = min(PER, IMAGES - PER * t) if isinstance(t, int) else PER
                for m in range(PER):
                    if m < n:
                        src = x[PER * t + m] if isinstance(t, int) else \
                            x[bass.ds(t * PER + m, 1)].rearrange("a r f -> (a r) f")
                        sp.dma_start(xin[m * L + 1:(m + 1) * L, par, :], src).then_inc(x_in[par], 16)

            sp.wait_ge(s_xz, 1)
            load_x(0, 0)
            load_x(1, 1)

            def step(i, par):
                t = i + 2
                if live(t):
                    need(sp, x_n, i + 1)
                    load_x(t, par)
                t = i - 4
                if live(t):
                    need(sp, x2_ok, t + 1)
                    dram = x2_rows[t * P:(t + 1) * P, :] if isinstance(t, int) else x2_rows[bass.ds(t * P, P), :]
                    sp.dma_start(dram, x2[:, par, :]).then_inc(x2_out[par], 16)
            pipeline(sp, step, 7, 19)

            def load_w1(e):
                src = w1[e:e + 1] if isinstance(e, int) else w1[bass.ds(e, 1)]
                sp.dma_start(w1r[:, :, :], src.rearrange("a (c p) h -> p (a c) h", p=128)).then_inc(w1_in, 16)

            def load_w2(e):
                src = w2[e:e + 1] if isinstance(e, int) else w2[bass.ds(e, 1)]
                sp.dma_start(w2r[:, :, :], src.rearrange("a (k p) o -> p (a k) o", p=128)).then_inc(w2_in, 16)

            sp.wait_ge(x_n, TILES)
            sp.wait_ge(xT_ps, TILES)
            sp.wait_ge(z_ps, TILES)
            load_w1(0)
            load_w2(0)
            with sp.Fori(0, E - 1) as j:
                sp.wait_ge(w1_lo, j + 1)
                load_w1(j + 1)
                sp.wait_ge(w2_lo, j * 2 + 2)
                load_w2(j + 1)

            for par in range(2):
                sp.wait_ge(y_out[par], 16 * JT * E // 2)
            y_v = y_rows[0:TRASH, :].rearrange("(k t p) f -> p t k f", k=2, p=P)
            PAIRS = TILES // 2
            o_v = out[0:(TILES - 1) * PER * L, :].rearrange("(t r) f -> r t f", r=PER * L)

            def load_y(q, par):
                src = y_v[:, 2 * q:2 * q + 2, :, :] if isinstance(q, int) else y_v[:, bass.ds(q * 2, 2), :, :]
                for k in range(2):
                    sp.dma_start(yin[:, par, :, k, :], src[:, :, k, :]).then_inc(z_in[par], 16)

            def store(q, par):
                sp.wait_ge(o_ok, q * 2 + 2)
                src = yo[:, 2 * par:2 * par + 2, :]
                dst_ = o_v[:, 2 * q:2 * q + 2, :] if isinstance(q, int) else o_v[:, bass.ds(q * 2, 2), :]
                sp.dma_start(dst_[0:96, :, :], src[0:96, :, :]).then_inc(o_out[par], 16)
                sp.dma_start(dst_[96:PER * L, :, :], src[96:PER * L, :, :]).then_inc(o_out[par], 16)

            load_y(0, 0)
            load_y(1, 1)
            with sp.Fori(0, (PAIRS - 3) // 2) as j:
                for par in range(2):
                    q = j * 2 + par
                    sp.wait_ge(c_ok, q * 2 + 2)
                    load_y(q + 2, par)
                    store(q, par)
            q = PAIRS - 3
            sp.wait_ge(c_ok, q * 2 + 2)
            load_y(q + 2, 0)
            store(q, 0)
            store(q + 1, 1)
            t = TILES - 2
            sp.wait_ge(o_ok, TILES)
            rows_ = PER * L
            for a, b, k in ((0, 96, 0), (96, rows_, 0), (0, 32, 1), (32, LIVE_LAST, 1)):
                sp.dma_start(out[(t + k) * rows_ + a:(t + k) * rows_ + b, :], yo[a:b, k, :]).then_inc(o_out[0], 16)
            sp.wait_ge(o_out[0], 32 * (PAIRS // 2) + 64)
            sp.wait_ge(o_out[1], 32 * (PAIRS // 2))
            for par in range(2):
                sp.wait_ge(x2_out[par], 16 * (TILES // 2))
                sp.wait_ge(y_out[par], 16 * JT * E // 2)

        @block.scalar
        def _(act):
            def load(done, dst_, src):
                nc.scalar.dma_start(dst_, src).then_inc(done, 16)

            load(c_w, wproj[:, :, :], w_proj.rearrange("(c p) e -> p c e", p=128))
            load(c_w, ln1g[:, :], ln1_g)
            load(c_w, ln1b[:, :], ln1_b)
            load(c_w, bproj[:, :], b_proj)
            act.wait_ge(s_zero, 1)
            for m in range(PER):
                load(c_g, g2m[m * L + 1:(m + 1) * L, :], rep(ln2_g, 0, PATCHES))
                load(c_g, posadd[m * L + 1:(m + 1) * L, :], rep(ln2_b, 0, PATCHES))
                load(c_g, posadd[m * L:m * L + 1, :], cls_token)
                load(c_g, posb[m * L:(m + 1) * L, :], pos_emb)
            load(c_a, wq[:, :, :], wq_t.rearrange("(c p) o -> p c o", p=128))
            load(c_a, wk[:, :, :], wk_t.rearrange("(c p) o -> p c o", p=128))
            load(c_a, wv[:, :, :], wv_t.rearrange("(c p) o -> p c o", p=128))
            load(c_a, bqk[:, 0:EC], bq)
            load(c_a, bqk[:, EC:2 * EC], bk)
            load(c_a, bvb[:, :], rep(bv, 0, P))
            load(c_a, rw[:, :, :], router_w.rearrange("(c p) e -> p c e", p=128))
            load(c_a, rbb[:, :], rep(router_b, 0, P))
            load(c_l, lng[:, :], rep(ln_g, 0, P))
            load(c_l, lnb[:, :], rep(ln_b, 0, P))
            load(c_l, b1t[:, :], b1)
            load(c_l, b2b[:, :, :].rearrange("p a b -> p (a b)"), rep(b2, 0, P))

            def step(i, par):
                t = i - 3
                if live(t):
                    need(act, s_nmx, t + 1)
                    need(act, pT_ps, t)
                    need(act, r_inv, t - 1)
                    nc.scalar.activation(prob[:, :], masked[:, :], ACT.Exp, bias=nmax[:, 0:1], scale=1.0 / ED,
                                         accum_out=psumr[:, (par + 1) % 2:(par + 1) % 2 + 1]).then_inc(p_ok, 1)
                t = i
                if live(t):
                    need(act, xT_ps, t + 1)
                    need(act, z_ps, t)
                    nc.scalar.copy(xnT[:, 0:3, :].rearrange("p a b -> p (a b)"), ps[0][:, 0:3 * P])
                    nc.scalar.copy(xnT[:, 3:6, :].rearrange("p a b -> p (a b)"), ps[1][:, 0:3 * P]).then_inc(xT_sb, 1)
                if isinstance(i, int) and i == 2:
                    act.wait_ge(c_a, N_A)
                t = i - 2
                if live(t):
                    need(act, qk_ps, t + 1)
                    need(act, s_ps, t)
                    for c in range(2 * EC):
                        a = nc.scalar.activation(qkT[:, c, :], bank(3)[:, c * P:(c + 1) * P], ACT.Identity,
                                                 bias=bqk[:, c:c + 1])
                    a.then_inc(qk_sb, 1)
                t = i - 3
                if live(t):
                    need(act, pT_ps, t + 1)
                    need(act, o_ps, t)
                    nc.scalar.copy(probT[:, :], bank(5)[0:P, 0:P]).then_inc(pT_sb, 1)
                t = i - 1
                if live(t):
                    need(act, x1T_ps, t + 1)
                    need(act, v_ps, t - 1)
                    nc.scalar.copy(x1T[:, (par + 1) % 2, :], bank(6)[:, 0:EC * P]).then_inc(x1T_sb, 1)
                t = i - 4
                if live(t):
                    need(act, x2T_ps, t + 1)
                    need(act, l_ps, t)
                    nc.scalar.copy(x2T[:, :], bank(4)[:, 0:EC * P]).then_inc(x2T_sb, 1)
            pipeline(act, step, 6, 22)

            act.wait_ge(r_dl, 1)
            nc.scalar.activation(ed[:, :], dl[:, :], ACT.Exp).then_inc(r_ed, 1)

            act.wait_ge(c_l, N_L)

            def w1_high(e):
                act.wait_ge(w1_in, 16 * e + 16)
                need(act, u_ps, e * HC)
                nc.scalar.copy(w1h[:, :, :], w1r[:, :, :]).then_inc(w1_hi, 1)

            def w2_high(e, half):
                if half == 0:
                    act.wait_ge(w2_in, 16 * e + 16)
                    need(act, y_ps, e * JT)
                k = half * HC // 2
                nc.scalar.copy(w2h[:, k:k + HC // 2, :], w2r[:, k:k + HC // 2, :]).then_inc(w2_hi, 1)

            def x_high(e):
                act.wait_ge(gT_ps, e + 1)
                nc.scalar.copy(xgh[:, :, :], pall[:, 2:4, 0:SLOTS]).then_inc(x_hi, 1)

            def gelu(e, k):
                u = e * HC + k
                act.wait_ge(u_ps, u + 1)
                need(act, h_lo, u - 1)
                nc.scalar.activation(hr[:, k % 2, :], bank(k % 4)[:, 0:SLOTS], ACT.Gelu,
                                     bias=col(b1t, u)).then_inc(u_sb, 1)

            def expert(e, last=False):
                w2_high(e, 0)
                gelu(e, 0)
                gelu(e, 1)
                w2_high(e, 1)
                for k in range(2, HC):
                    gelu(e, k)
                if not last:
                    x_high(e + 1)
                    w1_high(e + 1)

            w1_high(0)
            x_high(0)
            expert(0)
            with act.Fori(0, E - 2) as j:
                expert(j + 1)
            expert(E - 1, last=True)

            def first_choice(q, par, k, first=False):
                t = q * 2 + k
                if k == 0:
                    act.wait_ge(z_in[par], ycount(q, par))
                if not first:
                    act.wait_ge(c_ok, t - 1)
                nc.scalar.activation(ya[:, k, :], yin[:, par, k, 0, :], ACT.Copy,
                                     scale=col(wtok[:, 0, :], t)).then_inc(a_ok, 1)

            def scaled(q, k, first=False):
                t = q * 2 + k
                act.wait_ge(c_d, t + 1)
                act.wait_ge(c_rs, q + 1)
                if not first:
                    act.wait_ge(o_ok, t - 1)
                nc.scalar.activation(yu[:, k, :], yd[:, k, :], ACT.Copy, scale=yrs[:, 1, k:k + 1]).then_inc(u_ok, 1)

            for k in range(2):
                first_choice(0, 0, k, True)
            for k in range(2):
                first_choice(1, 1, k)
            for k in range(2):
                scaled(0, k, True)
            with act.Fori(0, (TILES // 2 - 3) // 2) as j:
                for par in range(2):
                    q = j * 2 + 1 + par
                    for k in range(2):
                        first_choice(q + 1, par, k)
                    for k in range(2):
                        scaled(q, k)
            q = TILES // 2 - 2
            for k in range(2):
                first_choice(q + 1, 0, k)
            for q in (q, q + 1):
                for k in range(2):
                    scaled(q, k)

        @block.tensor
        def _(pe):
            pe.wait_ge(c_pool, 5)
            pe.wait_ge(c_w, N_W)
            pe.wait_ge(c_dve, 1)
            for c in range(PC):
                nc.tensor.matmul(bank(2)[0:P, 0:ED], xnT[:, c, :], wproj[:, c, :], start=(c == 0), stop=False)
            nc.tensor.matmul(bank(2)[0:P, 0:ED], onesrow[0:1, 0:P], bproj[0:1, :], start=False, stop=True)\
                .then_inc(c_pe, 1)
            pe.wait_ge(c_dve, 2)

            def step(i, par):
                odd = (par + 1) % 2
                t = i
                if live(t):
                    need(pe, x_n, t + 1)
                    need(pe, xT_sb, t)
                    for c in range(PC):
                        m = nc.tensor.transpose(ps[c // 3][:, (c % 3) * P:(c % 3 + 1) * P],
                                                xn[:, par, c * 128:(c + 1) * 128], ident[0:P, 0:P])
                    m.then_inc(xT_ps, 1)
                if isinstance(i, int) and i == 2:
                    pe.wait_ge(c_a, N_A)
                t = i - 2
                if live(t):
                    need(pe, x1T_sb, t + 1)
                    need(pe, qk_sb, t)
                    xt = x1T[:, par, :].rearrange("p (c r) -> p c r", c=EC)
                    for o in range(2 * EC):
                        w = wq if o < EC else wk
                        for c in range(EC):
                            m = nc.tensor.matmul(bank(3)[:, o * P:(o + 1) * P],
                                                 w[:, c, (o % EC) * 128:(o % EC + 1) * 128], xt[:, c, :],
                                                 start=(c == 0), stop=(c == EC - 1))
                    m.then_inc(qk_ps, 1)
                    need(pe, x2T_sb, t - 2)
                    need(pe, v_sb, t)
                    for c in range(EC):
                        m = nc.tensor.matmul(bank(4)[0:P, 0:ED], xt[:, c, :], wv[:, c, :],
                                             start=(c == 0), stop=(c == EC - 1))
                    m.then_inc(v_ps, 1)
                t = i - 3
                if live(t):
                    need(pe, p_ok, t + 1)
                    nc.tensor.transpose(bank(5)[0:P, 0:P], prob[:, :], ident[0:P, 0:P]).then_inc(pT_ps, 1)
                t = i - 5
                if live(t):
                    need(pe, x2T_sb, t + 1)
                    need(pe, l_sb, t)
                    need(pe, g_h, t + 2 if not isinstance(t, int) else min(t + 2, TILES))
                    for c in range(EC):
                        m = nc.tensor.matmul(bank(7)[0:P, 0:E], x2T[:, c * P:(c + 1) * P], rw[:, c, :],
                                             start=(c == 0), stop=(c == EC - 1))
                    m.then_inc(l_ps, 1)
                t = i
                if live(t):
                    need(pe, xT_sb, t + 1)
                    need(pe, z_b, t)
                    for c in range(PC):
                        m = nc.tensor.matmul(bank(2)[0:P, 0:ED], xnT[:, c, :], wproj[:, c, :],
                                             start=(c == 0), stop=(c == PC - 1))
                    m.then_inc(z_ps, 1)
                t = i - 3
                if live(t):
                    need(pe, pT_sb, t + 1)
                    need(pe, v_sb, t + 1)
                    need(pe, l_sb, t - 1)
                    need(pe, g_h, t)
                    nc.tensor.matmul(bank(7)[0:P, 0:ED], probT[:, :], v[:, odd, :], start=True, stop=True)\
                        .then_inc(o_ps, 1)
                t = i - 2
                if live(t):
                    need(pe, qk_sb, t + 1)
                    need(pe, s_msk, t)
                    for c in range(EC):
                        m = nc.tensor.matmul(bank(5)[0:P, 0:P], qkT[:, c, :], qkT[:, EC + c, :],
                                             start=(c == 0), stop=(c == EC - 1))
                    m.then_inc(s_ps, 1)
                t = i - 1
                if live(t):
                    need(pe, x1_ok, t + 1)
                    need(pe, x1T_sb, t)
                    for c in range(EC):
                        m = nc.tensor.transpose(bank(6)[:, c * P:(c + 1) * P],
                                                x1[:, odd, c * 128:(c + 1) * 128], ident[0:P, 0:P])
                    m.then_inc(x1T_ps, 1)
                t = i - 4
                if live(t):
                    need(pe, x2_ok, t + 1)
                    if not isinstance(t, int) or t + 3 <= TILES:
                        need(pe, v_sb, t + 3)
                    for c in range(EC):
                        m = nc.tensor.transpose(bank(4)[:, c * P:(c + 1) * P],
                                                x2[:, par, c * 128:(c + 1) * 128], ident[0:P, 0:P])
                    m.then_inc(x2T_ps, 1)
            pipeline(pe, step, 6, 22)

            pe.wait_ge(l_sb, TILES)
            pe.wait_ge(g_h, TILES)
            pe.wait_ge(x2T_sb, TILES)
            for t in range(PAD):
                if t % (PAD // 2) == 0:
                    pe.wait_ge(r_V, 2 * t // PAD + 1)
                m = nc.tensor.transpose(pall[:, t // 4, (t % 4) * P:(t % 4 + 1) * P], vrep[:, t, :], ident[0:P, 0:P])
            m.then_inc(r_VT, 1)
            for r in range(len(SHIFTS)):
                pe.wait_ge(r_won, r + 1)
                nc.tensor.matmul(ps[0][:, 0:1], grp[:, :], won[:, :], start=True, stop=True).then_inc(r_n, 1)
            pe.wait_ge(r_pick, 1)
            nc.tensor.matmul(ps[0][0:P, 0:E], onesf[:, 0:P], thrrow[:, :], start=True, stop=True).then_inc(r_thr, 1)
            pe.wait_ge(r_ge, 1)
            gev = ge[:, :, :, :].rearrange("p s e t -> p (s e t)")
            n = 2 * E * TILES
            nc.tensor.matmul(bank(2)[0:P, 0:n], below[0:P, 0:P], gev, start=True, stop=True)
            nc.tensor.matmul(bank(3)[0:P, 0:n], onesb[0:P, 0:P], gev, start=True, stop=True).then_inc(r_pos, 1)
            pe.wait_ge(r_val, 2)
            for q in range(Q):
                if q % 4 == 0:
                    pe.wait_ge(r_lo, q // 4 + 1)
                m = nc.tensor.matmul(bank(4)[0:P, 0:2 * COLS], ohlo[:, q, :],
                                     ohval[:, q, :, :].rearrange("p a b -> p (a b)"),
                                     start=(q == 0), stop=(q == Q - 1))
            m.then_inc(r_list, 1)

            def transposes(e, par):
                pe.wait_ge(x_lo, e) if not isinstance(e, int) else need(pe, x_lo, e)
                for j in range(JT):
                    pe.wait_ge(g_in[par][j], e_count(e, par, 16))
                    for c in range(EC):
                        m = nc.tensor.transpose(bank(4 + c)[:, j * P:(j + 1) * P],
                                                xg[:, par, j, c * 128:(c + 1) * 128], ident[0:P, 0:P])
                m.then_inc(gT_ps, 1)

            def expert(e, par, last=False):
                pe.wait_ge(w1_lo, e + 1)
                pe.wait_ge(x_lo, e + 1)
                for k in range(HC):
                    need(pe, u_sb, e * HC + k - 3)
                    n = 0
                    for c in range(EC):
                        for w, xs in ((w1h, xgh), (w1h, xgl), (w1l, xgh)):
                            m = nc.tensor.matmul(bank(k % 4)[:, 0:SLOTS], w[:, c, k * 128:(k + 1) * 128], xs[:, c, :],
                                                 start=(n == 0), stop=(n == 3 * EC - 1))
                            n += 1
                    m.then_inc(u_ps, 1)
                if not last:
                    transposes(e + 1, 1 - par)
                for j in range(JT):
                    need(pe, y_sb, e * JT + j - 1)
                    n = 0
                    for k in range(HC):
                        if j == 0:
                            if k % (HC // 2) == 0:
                                pe.wait_ge(w2_lo, e * 2 + 1 + 2 * k // HC)
                            pe.wait_ge(h_lo, e * HC + k + 1)
                        for hs, w in ((hh, w2h), (hh, w2l), (hl, w2h)):
                            m = nc.tensor.matmul(bank(6 + j % 2)[0:P, 0:ED], hs[:, k, j * P:(j + 1) * P], w[:, k, :],
                                                 start=(n == 0), stop=(n == 3 * HC - 1))
                            n += 1
                    m.then_inc(y_ps, 1)

            transposes(0, 0)
            expert(0, 0)
            expert(1, 1)
            with pe.Fori(0, (E - 4) // 2) as j:
                for par in range(2):
                    expert(j * 2 + 2 + par, par)
            expert(E - 2, 0)
            expert(E - 1, 1, last=True)

        @block.vector
        def _(dve):
            V_ = nc.vector
            V_.memset(g2m[:, :], 0.0)
            V_.memset(posb[:, :], 0.0)
            V_.memset(posadd[:, :], 0.0).then_inc(s_zero, 1)
            V_.memset(xin[:, :, :], 0.0).then_inc(s_xz, 1)
            V_.memset(V[:, :, :], 0.0)
            V_.memset(thr[:, :].bitcast(fp32), 0.0)
            dve.wait_ge(c_w, N_W)
            V_.tensor_copy(xnT[:, :, :], rep(ln1b[:, :].rearrange("p (c a) -> p c a", a=1), 2, P)).then_inc(c_dve, 1)
            dve.wait_ge(c_pe, 1)
            V_.tensor_copy(zbias[:, :], bank(2)[0:P, 0:ED])
            for c in range(PC):
                m = V_.tensor_scalar(wproj[:, c, :], wproj[:, c, :], ln1g[:, c:c + 1], None, ALU.mult)
            m.then_inc(c_dve, 1)
            dve.wait_ge(c_g, N_G)
            V_.tensor_tensor(posb[:, :], posb[:, :], posadd[:, :], ALU.add).then_inc(c_dve, 1)
            dve.wait_ge(c_dve, 2)
            dve.wait_ge(c_pool, 5)

            def stats_x(t, par):
                three = 48
                if isinstance(t, int):
                    n = sum(min(PER, IMAGES - PER * s) for s in range(par, t + 1, 2))
                    dve.wait_ge(x_in[par], 16 * n)
                else:
                    dve.wait_ge(x_in[par], (t - par + 2) * (three // 2))
                for hlf in range(2):
                    m = V_.bn_stats(xstat[:, hlf, :], xin[:, par, hlf * HALF:(hlf + 1) * HALF])
                m.then_inc(x_st, 1)
                plain(dve, (x_st, t + 1), (x_rs0, t))
                V_.bn_aggr(xmv[:, :], xstat[:, :, :].rearrange("p a b -> p (a b)")).then_inc(x_mv, 1)

            def norm_x(t, par):
                dve.wait_ge(x_rs, t + 1)
                dve.wait_ge(x_mv, t + 1)
                need(dve, xT_ps, t - 1)
                V_.tensor_scalar(xn[:, par, :], xin[:, par, :], xmv[:, 0:1], rs[:, 0, 1:2],
                                 ALU.subtract, ALU.mult).then_inc(x_n, 1)

            stats_x(0, 0)
            norm_x(0, 0)
            for k, s in enumerate(SHIFTS):
                V_.tensor_scalar(digit[:, k:k + 1], pidx[:, :], WAYS - 1, s if s else 2, ALU.bitwise_and,
                                 ALU.logical_shift_left if s else ALU.logical_shift_right)

            def step(i, par):
                odd = (par + 1) % 2
                t = i - 3
                if live(t):
                    plain(dve, (s_ps, t + 1), (p_ok, t), (s_nmx, t))
                    V_.tensor_tensor_reduce(masked[:, :], bank(5)[0:P, 0:P], amask[:, :], 1.0, MASKED,
                                            ALU.add, ALU.max, smax[:, 0:1]).then_inc(s_msk, 1)
                    need(dve, s_msk, t + 1)
                    V_.tensor_scalar(nmax[:, :], smax[:, :], -1.0 / ED, None, ALU.mult).then_inc(s_nmx, 1)
                t = i - 1
                if live(t):
                    need(dve, z_ps, t + 1)
                    need(dve, z_n, t)
                    V_.tensor_tensor(zb[:, :], bank(2)[0:P, 0:ED], zbias[:, :], ALU.add).then_inc(z_b, 1)
                    need(dve, z_b, t + 1)
                    V_.bn_stats(zstat[:, :], zb[:, :]).then_inc(z_st, 1)
                    plain(dve, (z_st, t + 1))
                    V_.bn_aggr(zmv[:, :], zstat[:, :]).then_inc(z_mv, 1)
                t = i - 4
                if live(t):
                    need(dve, o_ps, t + 1)
                    need(dve, g_h, t)
                    V_.reciprocal(rinv[:, :], psumr[:, par:par + 1]).then_inc(r_inv, 1)
                    need(dve, r_inv, t + 1)
                    V_.scalar_tensor_tensor(tile_of(H, t), bank(7)[0:P, 0:ED], rinv[:, 0:1], tile_of(H, t),
                                            ALU.mult, ALU.add).then_inc(g_h, 1)
                t = i - 1
                if live(t):
                    need(dve, z_rs, t + 1)
                    need(dve, h_g, t)
                    V_.tensor_scalar(zn[:, :], zb[:, :], zmv[:, 0:1], rs[:, 1, 1:2],
                                     ALU.subtract, ALU.mult).then_inc(z_n, 1)
                t = i - 4
                if live(t):
                    plain(dve, (g_h, t + 1), (g_mv, t))
                    V_.bn_stats(gstat[:, :], tile_of(H, t)).then_inc(g_st, 1)
                    plain(dve, (g_st, t + 1), (x2_ok, t))
                    V_.bn_aggr(gmv[:, :], gstat[:, :]).then_inc(g_mv, 1)
                t = i - 2
                if live(t):
                    if isinstance(t, int) and t == 0:
                        dve.wait_ge(c_a, N_A)
                    need(dve, v_ps, t + 1)
                    need(dve, o_ps, t - 1)
                    V_.tensor_tensor(v[:, par, :], bank(4)[0:P, 0:ED], bvb[:, :], ALU.add).then_inc(v_sb, 1)
                t = i + 1
                if live(t):
                    stats_x(t, odd)
                t = i - 1
                if live(t):
                    plain(dve, (h_ok, t + 1))
                    V_.bn_stats(hstat[:, :], tile_of(H, t)).then_inc(h_st, 1)
                    plain(dve, (h_st, t + 1), (x1_ok, t))
                    V_.bn_aggr(hmv[:, :], hstat[:, :]).then_inc(h_mv, 1)
                t = i - 4
                if live(t):
                    need(dve, g_rs, t + 1)
                    need(dve, x2T_ps, t - 1)
                    if isinstance(t, int):
                        need(dve, x2_out[par], 16 * (t // 2))
                    else:
                        need(dve, x2_out[par], (t - par) * 8)
                    V_.tensor_scalar(x2[:, par, :], tile_of(H, t), gmv[:, 0:1], rs[:, 3, 1:2],
                                     ALU.subtract, ALU.mult).then_inc(x2_ok, 1)
                t = i - 5
                if live(t):
                    need(dve, l_ps, t + 1)
                    V_.tensor_tensor(LG[:, :, at(t)] if not isinstance(t, int) else LG[:, :, t:t + 1],
                                     bank(7)[0:P, 0:E].rearrange("p (e a) -> p e a", a=1),
                                     rbb[:, :].rearrange("p (e a) -> p e a", a=1), ALU.add).then_inc(l_sb, 1)
                t = i - 1
                if live(t):
                    need(dve, h_rs, t + 1)
                    need(dve, x1T_ps, t - 1)
                    V_.tensor_scalar(x1[:, odd, :], tile_of(H, t), hmv[:, 0:1], rs[:, 2, 1:2],
                                     ALU.subtract, ALU.mult).then_inc(x1_ok, 1)
                t = i + 1
                if live(t):
                    norm_x(t, odd)
            pipeline(dve, step, 7, 19)

            seq = 0

            def link(inst):
                nonlocal seq
                seq += 1
                inst.then_inc(d_seq, 1)
                dve.wait_ge(d_seq, seq)

            def over_e(a):
                return a.rearrange("p e t -> p t e")

            def per_tile(a):
                return rep(a.rearrange("p (a t) -> p a t", a=1), 1, E)

            dve.wait_ge(l_sb, TILES)
            dve.wait_ge(c_pool, 5)
            scores = LG
            for k, oh in enumerate((oh1, oh2)):
                link(V_.tensor_reduce(m12[:, k, :], over_e(scores[:, :, :]), AX.X, ALU.max))
                link(V_.tensor_tensor(eqm[:, :, :], scores[:, :, :], per_tile(m12[:, k, :]), ALU.is_equal))
                link(V_.tensor_tensor(eqm[:, :, :], eqm[:, :, :], erev[:, :, :], ALU.mult))
                link(V_.tensor_reduce(f12[:, k, :], over_e(eqm[:, :, :]), AX.X, ALU.max))
                link(V_.tensor_tensor(oh[:, :, :], eqm[:, :, :], per_tile(f12[:, k, :]), ALU.is_equal))
                if k == 0:
                    link(V_.scalar_tensor_tensor(lg2[:, :, :].rearrange("p e t -> p (e t)"),
                                                 oh1[:, :, :].rearrange("p e t -> p (e t)"), MASKED,
                                                 LG[:, :, :].rearrange("p e t -> p (e t)"), ALU.mult, ALU.add))
                    scores = lg2
            V_.tensor_tensor(dl[:, :], m12[:, 1, :], m12[:, 0, :], ALU.subtract).then_inc(r_dl, 1)
            dve.wait_ge(r_ed, 1)
            link(V_.tensor_scalar(dl[:, :], ed[:, :], 1.0, None, ALU.add))
            link(V_.reciprocal(gate[:, 0, :], dl[:, :]))
            link(V_.tensor_tensor(gate[:, 0, :], gate[:, 0, :], valid[:, :], ALU.mult))
            link(V_.tensor_tensor(gate[:, 1, :], gate[:, 0, :], ed[:, :], ALU.mult))
            V_.tensor_tensor(V[:, :, 0:TILES], oh1[:, :, :], per_tile(gate[:, 0, :]), ALU.mult)
            link(V_.tensor_tensor(V2[:, :, :], oh2[:, :, :], per_tile(gate[:, 1, :]), ALU.mult))
            link(V_.tensor_tensor(V[:, :, 0:TILES], V[:, :, 0:TILES], V2[:, :, :], ALU.add))
            dve.wait_ge(s_fill, 16 * 4)
            for k in range(2):
                t0, t1 = k * PAD // 2, (k + 1) * PAD // 2
                V_.tensor_copy(vrep[:, t0:t1, :].rearrange("p t (e w) -> p t e w", w=WAYS),
                               rep(V[:, :, t0:t1].rearrange("p e (t a) -> p t e a", a=1), 3, WAYS)).then_inc(r_V, 1)
            dve.wait_ge(r_VT, 1)
            for r, s in enumerate(SHIFTS):
                link(V_.tensor_tensor(cand[:, :], thr[:, :], digit[:, r:r + 1], ALU.bitwise_or))
                link(V_.tensor_scalar(junk.rearrange("p (a b) -> p a b", a=6), pall[:, :, 0:4 * P],
                                      cand[:, :].bitcast(fp32), None, ALU.is_ge, ALU.add, accum_out=cnt[:, 0:1]))
                V_.tensor_scalar(won[:, :], cnt[:, :], CAP - 0.5, None, ALU.is_ge).then_inc(r_won, 1)
                dve.wait_ge(r_n, r + 1)
                link(V_.tensor_scalar(dwon[:, :], ps[0][:, 0:1], 0.25 if s == 0 else 1.0, -1.0, ALU.mult, ALU.add))
                link(V_.tensor_scalar(dwon[:, :], dwon[:, :], s, None, ALU.logical_shift_left))
                link(V_.tensor_tensor(thr[:, :], thr[:, :], dwon[:, :], ALU.bitwise_or))
            V_.tensor_scalar(thrrow[:, :], pick[:, :], thr[:, :].bitcast(fp32), None, ALU.mult).then_inc(r_pick, 1)
            dve.wait_ge(r_thr, 1)
            link(V_.tensor_copy(thrb[:, :], ps[0][0:P, 0:E]))
            thre = rep(thrb[:, :].rearrange("p (e a) -> p e a", a=1), 2, TILES)
            V_.tensor_tensor(ge[:, 0, :, :], V[:, :, 0:TILES], thre, ALU.is_gt)
            V_.tensor_tensor(ge[:, 1, :, :], V[:, :, 0:TILES], thre, ALU.is_equal).then_inc(r_ge, 1)
            link(V_.tensor_scalar(okeq[:, :, :], V[:, :, 0:TILES], 0.0, None, ALU.is_gt))
            dve.wait_ge(r_ge, 1)
            dve.wait_ge(r_pos, 1)
            n = 2 * E * TILES
            link(V_.tensor_tensor_scan(tincl[:, :, :].rearrange("p a t -> p (a t)"),
                                       keep0[:, :, :].rearrange("p a t -> p (a t)"), bank(3)[0:P, 0:n], 0.0,
                                       ALU.mult, ALU.add))
            posf = pos[:, :, :, :].rearrange("p s e t -> p (s e t)")
            link(V_.tensor_tensor(posf, tincl[:, :, :].rearrange("p a t -> p (a t)"), bank(3)[0:P, 0:n], ALU.subtract))
            link(V_.tensor_tensor(posf, posf, bank(2)[0:P, 0:n], ALU.add))
            above = rep(tincl[:, 0:E, TILES - 1:TILES], 2, TILES)
            link(V_.tensor_tensor(pos[:, 1, :, :], pos[:, 1, :, :], above, ALU.add))
            link(V_.tensor_tensor(okeq[:, :, :], okeq[:, :, :], ge[:, 1, :, :], ALU.mult))
            link(V_.tensor_scalar(ok[:, :, :], pos[:, 1, :, :], CAP - 0.5, None, ALU.is_le))
            link(V_.tensor_tensor(okeq[:, :, :], okeq[:, :, :], ok[:, :, :], ALU.mult))
            V_.tensor_tensor(pos[:, 0, :, :], pos[:, 0, :, :], base1[:, :, :], ALU.add)
            link(V_.tensor_tensor(pos[:, 1, :, :], pos[:, 1, :, :], base1[:, :, :], ALU.add))
            V_.tensor_tensor(pos[:, 0, :, :], pos[:, 0, :, :], ge[:, 0, :, :], ALU.mult)
            link(V_.tensor_tensor(pos[:, 1, :, :], pos[:, 1, :, :], okeq[:, :, :], ALU.mult))
            link(V_.tensor_tensor(aslot[:, :, :], pos[:, 0, :, :], pos[:, 1, :, :], ALU.add))
            for k, oh in enumerate((oh1, oh2)):
                link(V_.tensor_tensor(eqm[:, :, :], aslot[:, :, :], oh[:, :, :], ALU.mult))
                link(V_.tensor_reduce(s12[:, k, :], over_e(eqm[:, :, :]), AX.X, ALU.add))
            s12f = s12[:, :, :].rearrange("p k t -> p (k t)")
            link(V_.tensor_scalar(wtok[:, :, :].rearrange("p k t -> p (k t)"), s12f, 0.5, None, ALU.is_ge))
            link(V_.tensor_tensor(wtok[:, :, :], wtok[:, :, :], gate[:, :, :], ALU.mult))
            BIG = 1.5 * 2.0 ** 23
            link(V_.tensor_scalar(hi[:, :], s12f, 1.0 / P, -0.5 - 0.5 / P, ALU.mult, ALU.add))
            link(V_.tensor_scalar(hi[:, :], hi[:, :], BIG, None, ALU.add))
            link(V_.tensor_scalar(hi[:, :], hi[:, :], -BIG, None, ALU.add))
            link(V_.scalar_tensor_tensor(lo[:, :], hi[:, :], -float(P), s12f, ALU.mult, ALU.add))
            link(V_.tensor_scalar(lo[:, :], lo[:, :], -1.0, None, ALU.add))
            hib = rep(hi[:, :].rearrange("p (q a) -> p q a", a=1), 2, COLS)
            V_.tensor_tensor(ohhi[:, :, :], hib, rep(iorow[:, 0:COLS].rearrange("p (a c) -> p a c", a=1), 1, Q),
                             ALU.is_equal).then_inc(r_hi, 1)
            dve.wait_ge(r_hi, 1)
            V_.tensor_scalar(ohval[:, :, 0, :], ohhi[:, :, :], row1[:, 0:1], None, ALU.mult).then_inc(r_val, 1)
            for q in range(Q):
                m = V_.tensor_scalar(ohlo[:, q, :], iorowb[:, :], lo[:, q:q + 1], None, ALU.is_equal)
                if q % 4 == 3:
                    m.then_inc(r_lo, 1)
            dve.wait_ge(r_list, 1)
            link(V_.tensor_copy(drow[:, :], bank(4)[0:P, 0:COLS]))
            link(V_.tensor_scalar(kch[:, :], bank(4)[0:P, COLS:2 * COLS], TILES - 0.5, None, ALU.is_ge))
            link(V_.tensor_scalar(empty[:, :], drow[:, :], 0.5, None, ALU.is_le))
            link(V_.scalar_tensor_tensor(drow[:, :], bank(4)[0:P, COLS:2 * COLS], float(P), drow[:, :],
                                         ALU.mult, ALU.add))
            link(V_.tensor_scalar(drow[:, :], drow[:, :], -1.0, None, ALU.add))
            link(V_.scalar_tensor_tensor(idf[:, :], kch[:, :], -float(TILES * P), drow[:, :], ALU.mult, ALU.add))
            link(V_.tensor_scalar(idf[:, :], idf[:, :], 0.0, None, ALU.max))
            V_.tensor_copy(gidx[:, :], idf[:, :])
            link(V_.tensor_tensor(empty[:, :], empty[:, :], trash[:, :], ALU.mult))
            link(V_.tensor_tensor(drow[:, :], drow[:, :], empty[:, :], ALU.add))
            V_.tensor_copy(didx[:, :], drow[:, :]).then_inc(r_idx, 1)

            def h_split(e, k):
                u = e * HC + k
                dve.wait_ge(u_sb, u + 1)
                V_.tensor_copy(hh[:, k, :], hr[:, k % 2, :]).then_inc(h_hi, 1)
                dve.wait_ge(h_hi, u + 1)
                V_.tensor_tensor(hl[:, k, :], hr[:, k % 2, :], hh[:, k, :].bitcast(fp32), ALU.subtract)\
                    .then_inc(h_lo, 1)

            def x_low(e):
                dve.wait_ge(x_hi, e + 1)
                V_.tensor_tensor(xgl[:, :, :], pall[:, 2:4, 0:SLOTS], xgh[:, :, :].bitcast(fp32), ALU.subtract)\
                    .then_inc(x_lo, 1)

            def w1_low(e):
                dve.wait_ge(w1_hi, e + 1)
                V_.tensor_tensor(w1l[:, :, :], w1r[:, :, :], w1h[:, :, :].bitcast(fp32), ALU.subtract)\
                    .then_inc(w1_lo, 1)

            def take_y(e, par, first=False):
                if not first:
                    dve.wait_ge(y_out[par], e_count(e, par, 16 * JT) - 16 * JT)
                for j in range(JT):
                    dve.wait_ge(y_ps, e * JT + j + 1)
                    b2e = b2b[:, e, :] if isinstance(e, int) else b2b[:, bass.ds(e, 1), :].rearrange("p a f -> p (a f)")
                    V_.tensor_tensor(y[:, par, j, :], bank(6 + j % 2)[0:P, 0:ED], b2e, ALU.add).then_inc(y_sb, 1)

            def expert(e, par, first=False, last=False):
                for k in range(HC):
                    h_split(e, k)
                if not last:
                    x_low(e + 1)
                    w1_low(e + 1)
                take_y(e, par, first)

            dve.wait_ge(c_l, N_L)
            w1_low(0)
            x_low(0)
            expert(0, 0, first=True)
            expert(1, 1, first=True)
            with dve.Fori(0, (E - 4) // 2) as j:
                for par in range(2):
                    expert(j * 2 + 2 + par, par)
            expert(E - 2, 0)
            expert(E - 1, 1, last=True)

            def summed(q, par, first=False):
                for k in range(2):
                    t = q * 2 + k
                    dve.wait_ge(a_ok, t + 1)
                    if not first:
                        dve.wait_ge(c_d, t - 1)
                    V_.scalar_tensor_tensor(yc[:, k, :], yin[:, par, k, 1, :], col(wtok[:, 1, :], t), ya[:, k, :],
                                            ALU.mult, ALU.add).then_inc(c_ok, 1)
                for k in range(2):
                    t = q * 2 + k
                    dve.wait_ge(c_ok, t + 1)
                    V_.bn_stats(ystat[:, k, :], yc[:, k, :]).then_inc(c_st, 1)
                for k in range(2):
                    t = q * 2 + k
                    plain(dve, (c_st, t + 1)) if first else plain(dve, (c_st, t + 1), (c_rs0, q))
                    V_.bn_aggr(ymv[:, k, :], ystat[:, k, :]).then_inc(c_mv, 1)
                for k in range(2):
                    t = q * 2 + k
                    dve.wait_ge(c_mv, t + 1)
                    if not first:
                        dve.wait_ge(u_ok, t - 1)
                    V_.scalar_tensor_tensor(yd[:, k, :], yc[:, k, :], ymv[:, k, 0:1], lng[:, :],
                                            ALU.subtract, ALU.mult).then_inc(c_d, 1)

            summed(0, 0, True)
            with dve.Fori(0, (TILES // 2 - 1) // 2) as j:
                for par in range(2):
                    summed(j * 2 + 1 + par, 1 - par)

        @block.gpsimd
        def _(pool):
            G = nc.gpsimd
            p_seq = sem("p_seq")
            seq = 0

            def link(inst):
                nonlocal seq
                seq += 1
                inst.then_inc(p_seq, 1)
                pool.wait_ge(p_seq, seq)

            link(G.memset(ident[:, :], 0.0))
            G.affine_select(out=ident[:, :], in_=ident[:, :], compare_op=ALU.not_equal, fill=1.0, base=0,
                            pattern=[[-1, 128]], channel_multiplier=1).then_inc(c_pool, 1)
            G.memset(neghalf[:, :], -0.5)
            G.memset(onesrow[:, :], 1.0)
            link(G.memset(amask[:, :], MASKED))
            for m in range(PER):
                lo_, hi_ = m * L, (m + 1) * L
                blk = amask[:, lo_:hi_]
                link(G.memset(blk, 0.0))
                link(G.affine_select(out=blk, in_=blk, compare_op=ALU.is_ge, fill=MASKED, base=-lo_,
                                     pattern=[[0, L]], channel_multiplier=1))
                link(G.affine_select(out=blk, in_=blk, compare_op=ALU.is_ge, fill=MASKED, base=hi_ - 1,
                                     pattern=[[0, L]], channel_multiplier=-1))
            G.affine_select(out=amask[:, :], in_=amask[:, :], compare_op=ALU.not_equal, fill=MASKED, base=0,
                            pattern=[[-1, P]], channel_multiplier=1).then_inc(c_pool, 1)
            G.memset(onesf[:, :], 1.0)
            link(G.memset(onesb[:, :], 1.0))
            G.affine_select(out=below[:, :], in_=onesb[:, :], compare_op=ALU.is_gt, fill=0.0, base=0,
                            pattern=[[1, 128]], channel_multiplier=-1)
            g3 = grp[:, :].rearrange("p (e w) -> p e w", w=WAYS)
            link(G.affine_select(out=g3, in_=onesb[:, :].rearrange("p (e w) -> p e w", w=WAYS), compare_op=ALU.is_ge,
                                 fill=0.0, base=0, pattern=[[-WAYS, E], [0, WAYS]], channel_multiplier=1))
            link(G.affine_select(out=g3, in_=g3, compare_op=ALU.is_ge, fill=0.0, base=WAYS - 1,
                                 pattern=[[WAYS, E], [0, WAYS]], channel_multiplier=-1))
            G.affine_select(out=pick[:, :], in_=onesf[:, 0:E], compare_op=ALU.is_equal, fill=0.0, base=0,
                            pattern=[[-WAYS, E]], channel_multiplier=1).then_inc(c_pool, 1)
            link(G.memset(valid[:, :], 1.0))
            G.affine_select(out=valid[:, TILES - 1:TILES], in_=valid[:, TILES - 1:TILES], compare_op=ALU.is_gt,
                            fill=0.0, base=LIVE_LAST, pattern=[[0, 1]], channel_multiplier=-1)
            G.affine_select(out=valid[:, 0:TILES - 1], in_=valid[:, 0:TILES - 1], compare_op=ALU.is_gt,
                            fill=0.0, base=PER * L, pattern=[[0, TILES - 1]], channel_multiplier=-1)
            G.memset(keep0[:, :, :], 1.0)
            link(G.memset(row1[:, :], 0.0))
            G.memset(keep0[:, :, 0:1], 0.0)
            f = dict(allow_small_or_imprecise_dtypes=True)
            G.iota(erev[:, :, :], [[-1, E], [0, TILES]], base=E, channel_multiplier=0, **f)
            G.iota(base1[:, :, :], [[SLOTS, E], [0, TILES]], base=1, channel_multiplier=0, **f)
            G.iota(iorow[:, :], [[1, P]], base=0, channel_multiplier=0, **f)
            G.iota(iorowb[:, :], [[1, P]], base=0, channel_multiplier=0, **f)
            G.iota(qidx[:, :], [[1, Q]], base=0, channel_multiplier=0, **f)
            G.iota(trash[:, :], [[P, COLS]], base=TRASH + 1, channel_multiplier=1, **f)
            G.iota(row1[:, :], [[0, 1]], base=1, channel_multiplier=1, **f)
            G.iota(pidx[:, :], [[0, 1]], base=0, channel_multiplier=1).then_inc(c_pool, 1)
            link(G.memset(zero[:, :], 0.0))
            per = 14
            yz = y_rows[0:TRASH, :].rearrange("(q p) f -> p q f", p=P)
            k = 0
            while k * per < Q:
                m = min(per, Q - k * per)
                pool.dma_start(yz[:, k * per:k * per + m, :],
                               zero[:, 0:m * ED].rearrange("p (q f) -> p q f", f=ED)).then_inc(s_fill, 16)
                k += 1
            assert k == 4
            G.memset(neghalf[:, :], -0.5).then_inc(c_pool, 1)
            pool.wait_ge(c_pool, 5)
            pool.wait_ge(c_dve, 3)

            def rstd(slot, mv, ready, n, mid, done):
                plain(pool, (ready, n))
                G.tensor_scalar(rs[:, slot, 0:1], mv[:, 1:2], EPS, None, ALU.add).then_inc(mid, 1)
                need(pool, mid, n)
                G.tensor_tensor(rs[:, slot, 1:2], rs[:, slot, 0:1], neghalf[:, :], ALU.pow).then_inc(done, 1)

            rstd(0, xmv, x_mv, 1, x_rs0, x_rs)

            def step(i, par):
                t = i - 1
                if live(t):
                    rstd(1, zmv, z_mv, t + 1, z_rs0, z_rs)
                    need(pool, z_n, t + 1)
                    G.tensor_tensor(tile_of(H, t), zn[:, :], g2m[:, :], ALU.mult).then_inc(h_g, 1)
                    plain(pool, (h_g, t + 1))
                    G.tensor_tensor(tile_of(H, t), tile_of(H, t), posb[:, :], ALU.add).then_inc(h_ok, 1)
                t = i - 4
                if live(t):
                    need(pool, x2_ok, t)
                    rstd(3, gmv, g_mv, t + 1, g_rs0, g_rs)
                t = i + 1
                if live(t):
                    need(pool, x_n, t)
                    rstd(0, xmv, x_mv, t + 1, x_rs0, x_rs)
                t = i - 1
                if live(t):
                    need(pool, x1_ok, t)
                    rstd(2, hmv, h_mv, t + 1, h_rs0, h_rs)
            pipeline(pool, step, 7, 21)

            pool.wait_ge(r_hi, 1)
            G.tensor_tensor(ohval[:, :, 1, :], ohhi[:, :, :], rep(qidx[:, :].rearrange("p (q a) -> p q a", a=1), 2, COLS),
                            ALU.mult).then_inc(r_val, 1)

            pool.wait_ge(r_idx, 1)
            for par in range(2):
                pool.wait_ge(x2_out[par], 16 * (TILES // 2))
            pool.wait_ge(s_fill, 16 * 4)

            def icol(buf, e):
                return buf[:, e * JT:(e + 1) * JT] if isinstance(e, int) else buf[:, bass.ds(e * JT, JT)]

            def gather(e, par):
                need(pool, gT_ps, e - 1)
                G.tensor_copy(gst[:, par, :], icol(gidx, e)).then_inc(i_st, 1)
                plain(pool, (i_st, e + 1))
                for j in range(JT):
                    pool.indirect_dma_start(
                        xg[:, par, j, :], None, x2_rows,
                        bass.IndirectOffsetOnAxis(ap=gst[:, par, j:j + 1], axis=0)).then_inc(g_in[par][j], 16)

            def w2_low(e):
                for half in range(2):
                    pool.wait_ge(w2_hi, e * 2 + half + 1)
                    k = half * HC // 2
                    G.tensor_tensor(w2l[:, k:k + HC // 2, :], w2r[:, k:k + HC // 2, :],
                                    w2h[:, k:k + HC // 2, :].bitcast(fp32), ALU.subtract).then_inc(w2_lo, 1)

            def scatter(e, par):
                for j in range(JT):
                    plain(pool, (y_sb, e * JT + j + 1))
                    if j == 0:
                        G.tensor_copy(dst[:, par, :], icol(didx, e)).then_inc(i_dst, 1)
                        plain(pool, (i_dst, e + 1))
                    pool.indirect_dma_start(
                        y_rows, bass.IndirectOffsetOnAxis(ap=dst[:, par, j:j + 1], axis=0),
                        y[:, par, j, :], None).then_inc(y_out[par], 16)

            def serve(e, par, more=True):
                w2_low(e)
                if more:
                    gather(e + 2, par)
                scatter(e, par)

            gather(0, 0)
            gather(1, 1)
            w2_low(0)
            pool.wait_ge(c_l, N_L)
            with pool.Fori(0, TILES) as t:
                G.tensor_tensor(tile_of(H, t), tile_of(H, t), lnb[:, :], ALU.add).then_inc(hb, 1)
            gather(2, 0)
            scatter(0, 0)
            serve(1, 1)
            with pool.Fori(0, (E - 4) // 2) as j:
                for par in range(2):
                    serve(j * 2 + 2 + par, par)
            serve(E - 2, 0, more=False)
            serve(E - 1, 1, more=False)

            pool.wait_ge(hb, TILES)

            def finish(q, par, first=False):
                if first:
                    plain(pool, (c_mv, q * 2 + 2))
                else:
                    plain(pool, (c_mv, q * 2 + 2), (u_ok, q * 2))
                G.tensor_scalar(yrs[:, 0, :], ymv[:, :, 1], EPS, None, ALU.add).then_inc(c_rs0, 1)
                pool.wait_ge(c_rs0, q + 1)
                G.tensor_tensor(yrs[:, 1, :], yrs[:, 0, :], rep(neghalf[:, :], 1, 2), ALU.pow).then_inc(c_rs, 1)
                if not (isinstance(q, int) and q < 2):
                    pool.wait_ge(o_out[par], 32 * (q // 2) if isinstance(q, int) else (q - par) * 16)
                for k in range(2):
                    t = q * 2 + k
                    plain(pool, (u_ok, t + 1))
                    G.tensor_tensor(yo[:, 2 * par + k, :], yu[:, k, :], tile_of(H, t), ALU.add).then_inc(o_ok, 1)

            finish(0, 0, True)
            finish(1, 1)
            finish(2, 0)
            with pool.Fori(0, (TILES // 2 - 3) // 2) as j:
                for par in range(2):
                    finish(j * 2 + 3 + par, 1 - par)


def kernel(**inputs):
    import numpy as np
    import concourse.bacc as bacc
    from concourse.bass_utils import run_bass_kernel_spmd

    a = {k: np.asarray(v_) for k, v_ in inputs.items()}
    B, C, S, _ = a["x"].shape
    ED = a["L0_tok_W_proj"].shape[1]
    n = round((a["L0_tok_pos_emb"].shape[1] - 1) ** 0.5)
    p = S // n
    E, D, HID = a["L0_ffn_w1"].shape
    col = lambda w: w.reshape(-1, 128).T
    arrays = {
        "x": a["x"].reshape(B, C, n, p, n, p).transpose(0, 2, 4, 3, 5, 1).reshape(B, n * n, p * p * C),
        "ln1_g": col(a["L0_tok_ln1_g"]), "ln1_b": col(a["L0_tok_ln1_b"]),
        "w_proj": a["L0_tok_W_proj"], "b_proj": a["L0_tok_b_proj"].reshape(1, ED),
        "ln2_g": a["L0_tok_ln2_g"].reshape(1, ED), "ln2_b": a["L0_tok_ln2_b"].reshape(1, ED),
        "cls_token": a["L0_tok_cls_token"].reshape(1, ED), "pos_emb": a["L0_tok_pos_emb"][0],
        "wq_t": a["L0_attn_Wq"].T, "bq": col(a["L0_attn_bq"]),
        "wk_t": a["L0_attn_Wk"].T, "bk": col(a["L0_attn_bk"]),
        "wv_t": a["L0_attn_Wv"].T, "bv": a["L0_attn_bv"].reshape(1, ED),
        "router_w": a["L0_ffn_router_w"], "router_b": a["L0_ffn_router_b"].reshape(1, E),
        "w1": a["L0_ffn_w1"], "b1": a["L0_ffn_b1"].reshape(E * HID // 128, 128).T,
        "w2": a["L0_ffn_w2"], "b2": a["L0_ffn_b2"].reshape(1, -1),
        "ln_g": a["L0_ffn_ln_g"].reshape(1, ED), "ln_b": a["L0_ffn_ln_b"].reshape(1, ED),
    }
    arrays = {f"in_{k}": np.ascontiguousarray(v_) for k, v_ in arrays.items()}
    nc = bacc.Bacc("TRN2", target_bir_lowering=False, num_devices=1)
    ins = [nc.dram_tensor(k, v_.shape, mybir.dt.from_np(v_.dtype), kind="ExternalInput").ap()
           for k, v_ in arrays.items()]
    out = nc.dram_tensor("out", (B * (n * n + 1), ED), fp32, kind="ExternalOutput").ap()
    vit_tower(nc, *ins, out)
    got = run_bass_kernel_spmd(nc, [arrays], core_ids=[0])
    return got.results[0]["out"].reshape(B, n * n + 1, ED)
```

```python
from contextlib import ExitStack

import concourse.bass as bass
from concourse import mybir

fp32 = mybir.dt.float32
fp32r = mybir.dt.float32r
bf16 = mybir.dt.bfloat16
i32 = mybir.dt.int32
u32 = mybir.dt.uint32
u16 = mybir.dt.uint16
ALU = mybir.AluOpType
ACT = mybir.ActivationFunctionType
AX = mybir.AxisListType

EPS = 1e-5
MASKED = -3.0e38


def rep(ap, dim, n):
    shape = list(ap.shape)
    shape[dim] = n
    return ap.broadcast_to(shape)


def vit_tower(nc, x, ln1_g, ln1_b, w_proj, b_proj, ln2_g, ln2_b, cls_token, pos_emb,
              wq_t, bq, wk_t, bk, wv_t, bv, router_w, router_b, w1, b1, w2, b2, ln_g, ln_b, out):
    IMAGES, PATCHES, PD = x.shape
    ED = w_proj.shape[1]
    L = PATCHES + 1
    PER = 128 // L
    P = 112
    TILES = -(-IMAGES // PER)
    LIVE_LAST = (IMAGES - PER * (TILES - 1)) * L
    PC = PD // 128
    EC = ED // 128
    E, _, HID = w1.shape
    HC = HID // 128
    CAP = int(IMAGES * L * 1.5 / E)
    JT = -(-CAP // P)
    SLOTS = JT * P
    COLS = E * JT
    PAD = 24
    Q = 2 * TILES
    HALF = PD // 2
    TRASH = Q * P
    WAYS = 16
    SHIFTS = [12, 8, 4, 0]

    ctx = ExitStack()
    with ctx:
        def sb(name, shape, dt=fp32):
            return ctx.enter_context(nc.sbuf_tensor(name, shape, dt))

        def sem(name):
            return ctx.enter_context(nc.semaphore(name))

        x2_rows = nc.dram_tensor("x2_rows", [TILES * P, ED], fp32, kind="Internal").ap()
        y_rows = nc.dram_tensor("y_rows", [TRASH + COLS * P, ED], fp32, kind="Internal").ap()

        ident = sb("ident", [128, 128])
        wproj = sb("wproj", [128, PC, ED])
        ln1g = sb("ln1g", [128, PC])
        ln1b = sb("ln1b", [128, PC])
        onesrow = sb("onesrow", [2, 128])
        bproj = sb("bproj", [1, ED])
        zb = sb("zb", [2, ED])
        zbm = sb("zbm", [2, ED])
        zbh = sb("zbh", [2, ED], fp32r)
        ones2 = sb("ones2", [2, P], fp32r)
        zbias = sb("zbias", [2, ED], fp32r)
        ln1bb = sb("ln1bb", [128, PC, 2])
        g2m = sb("g2m", [P, ED])
        posb = sb("posb", [P, ED])
        posadd = sb("posadd", [P, ED])
        wq = sb("wq", [128, EC, ED])
        wk = sb("wk", [128, EC, ED])
        wv = sb("wv", [128, EC, ED])
        bqk = sb("bqk", [128, 2 * EC])
        bvb = sb("bvb", [P, ED])
        amask = sb("amask", [P, P])
        rw = sb("rw", [128, EC, E])
        rbb = sb("rbb", [P, E])
        neghalf = sb("neghalf", [P, 1])
        lng = sb("lng", [P, ED])
        lnb = sb("lnb", [P, ED])
        b1t = sb("b1t", [128, E * HC])
        b2b = sb("b2b", [P, E, ED])
        stage = sb("stage", [128, 2 * EC * HID])
        xin = stage[0:P, 0:2 * PD].rearrange("p (s f) -> p s f", s=2)
        xn = stage[0:P, 2 * PD:4 * PD].rearrange("p (s f) -> p s f", s=2)
        w1r = stage[:, 0:EC * HID].rearrange("p (c h) -> p c h", c=EC)
        w2r = stage[:, EC * HID:2 * EC * HID].rearrange("p (k o) -> p k o", k=HC)
        rows = sb("rows", [P, 4 * JT * ED])
        xg = rows[:, 0:2 * JT * ED].rearrange("p (s j f) -> p s j f", s=2, j=JT)
        y = rows[:, 2 * JT * ED:4 * JT * ED].rearrange("p (s j f) -> p s j f", s=2, j=JT)
        ohlo = rows[:, 0:Q * P // 2].bitcast(bf16).rearrange("p (q c) -> p q c", q=Q)
        ohhi = rows[:, Q * P // 2:Q * (P + COLS) // 2].bitcast(bf16).rearrange("p (q c) -> p q c", q=Q)
        scratch128 = sb("scratch", [128, 14 * ED])
        scratch = scratch128[0:P, :]
        ZT = 7
        FILLS = -(-Q // ZT)
        zero = scratch[:, 0:ZT * ED]
        GATES = PAD * P
        junk = scratch128[:, 0:GATES // 2].bitcast(bf16)
        lowh = scratch128[:, GATES // 2:GATES].bitcast(u16)
        vrep = scratch[:, 0:PAD * 128].rearrange("p (t m) -> p t m", m=128)

        def tiles(first, n):
            return scratch[:, first * ED:(first + n) * ED].rearrange("p (a f) -> p a f", f=ED)

        ya, yc, yd, yu = tiles(0, 2), tiles(2, 2), tiles(4, 2), tiles(6, 2)
        yo = tiles(8, 4)
        xstat = sb("xstat", [P, 2, 6])
        xmv = sb("xmv", [P, 2])
        zstat = sb("zstat", [P, 6])
        zmv = sb("zmv", [P, 2])
        zn = sb("zn", [P, ED])
        hstat = sb("hstat", [P, 6])
        hmv = sb("hmv", [P, 2])
        x1 = sb("x1", [P, 2, ED])
        x1T = sb("x1T", [128, 2, EC * P])
        qkT = sb("qkT", [128, 2 * EC, P])
        v = sb("v", [P, 2, ED])
        masked = sb("masked", [P, P])
        smax = sb("smax", [P, 1])
        nmax = sb("nmax", [P, 1])
        prob = sb("prob", [P, P])
        psumr = sb("psumr", [P, 2])
        rinv = sb("rinv", [P, 1])
        probT = sb("probT", [P, P])
        gstat = sb("gstat", [P, 6])
        gmv = sb("gmv", [P, 2])
        x2 = sb("x2", [P, 2, ED])
        x2T = sb("x2T", [128, EC * P])
        rs = sb("rs", [P, 4, 3])
        H = sb("H", [P, TILES, ED])
        LG = sb("LG", [P, E, TILES])
        erev = sb("erev", [P, E, TILES])
        eqm = sb("eqm", [P, E, TILES])
        oh1 = sb("oh1", [P, E, TILES])
        oh2 = sb("oh2", [P, E, TILES])
        lg2 = sb("lg2", [P, E, TILES])
        m12 = sb("m12", [P, 2, TILES])
        f12 = sb("f12", [P, 2, TILES])
        dl = sb("dl", [P, TILES])
        ed = sb("ed", [P, TILES])
        warm = sb("warm", [P, 1])
        gate = sb("gate", [P, 2, TILES])
        valid = sb("valid", [P, TILES])
        V = sb("V", [P, E, PAD])
        V2 = sb("V2", [P, E, TILES])
        pidx = sb("pidx", [128, 1], i32)
        way = sb("way", [128, 1])
        nextd = sb("nextd", [128, len(SHIFTS)])
        cand = sb("cand", [128, 2 * len(SHIFTS)])
        known = sb("known", [128, 2])
        thalf = sb("thalf", [128, 3])
        thi = sb("thi", [128, 3], i32)
        thr = thi[:, 2:3]
        cnt = sb("cnt", [128, 2])
        won = sb("won", [128, 1], bf16)
        grp = sb("grp", [128, 128], bf16)
        pick = sb("pick", [128, E])
        thrrow = sb("thrrow", [128, E])
        thrb = sb("thrb", [P, E])
        onesf = sb("onesf", [128, 128])
        onesb = sb("onesb", [128, 128], bf16)
        below = sb("below", [128, 128], bf16)
        ge = sb("ge", [P, 2, E, TILES], bf16)
        keep0 = sb("keep0", [P, 2 * E, TILES])
        tincl = sb("tincl", [P, 2 * E, TILES])
        pos = sb("pos", [P, 2, E, TILES])
        okeq = sb("okeq", [P, E, TILES])
        ok = sb("ok", [P, E, TILES])
        base1 = sb("base1", [P, E, TILES])
        aslot = sb("aslot", [P, E, TILES])
        s12 = sb("s12", [P, 2, TILES])
        hi = sb("hi", [P, Q])
        lo = sb("lo", [P, Q])
        wtok = sb("wtok", [P, 2, TILES])
        iorow = sb("iorow", [P, P])
        qidx = sb("qidx", [P, Q])
        row1 = sb("row1", [P, 1])
        ohval = sb("ohval", [P, Q, 2, COLS], bf16)
        trash = sb("trash", [P, COLS])
        drow = sb("drow", [P, COLS])
        empty = sb("empty", [P, COLS])
        kch = sb("kch", [P, COLS])
        idf = sb("idf", [P, COLS])
        gidx = sb("gidx", [P, COLS], u32)
        didx = sb("didx", [P, COLS], u32)
        WS = EC * HID
        halves = sb("halves", [128, 4 * WS + 2 * HC * SLOTS], fp32r)
        w1h, w1l = (halves[:, k * WS:(k + 1) * WS].rearrange("p (c h) -> p c h", c=EC) for k in range(2))
        w2h, w2l = (halves[:, k * WS:(k + 1) * WS].rearrange("p (k o) -> p k o", k=HC) for k in range(2, 4))
        hh, hl = (halves[:, 4 * WS + k * HC * SLOTS:4 * WS + (k + 1) * HC * SLOTS]
                  .rearrange("p (k s) -> p k s", k=HC) for k in range(2))
        highh = wproj.rearrange("p c e -> p (c e)")[:, 0:GATES // 2].bitcast(u16)
        xnTh, xnTl = (halves[:, k * PC * P:(k + 1) * PC * P] for k in range(2))
        assert 2 * PC * P <= WS
        wph, wpl = (halves[:, 4 * WS + k * PC * ED:4 * WS + (k + 1) * PC * ED]
                    .rearrange("p (c e) -> p c e", c=PC) for k in range(2))
        gst = sb("gst", [P, 2, JT], u32)
        dst = sb("dst", [P, 2, JT], u32)
        xgh = sb("xgh", [128, EC, SLOTS], fp32r)
        xgl = sb("xgl", [128, EC, SLOTS], fp32r)
        hr = wproj.rearrange("p c e -> p (c e)")[:, 0:2 * SLOTS].rearrange("p (s r) -> p s r", s=2)
        yin = halves[0:P, 0:Q * ED].bitcast(fp32).rearrange("p (q f) -> p q f", q=Q)
        ystat = sb("ystat", [P, 2, 6])
        ymv = sb("ymv", [P, 2, 2])
        yrs = sb("yrs", [P, 3, 2])

        pz = ctx.enter_context(nc.psum_tensor("pz", [128, 2, 512], fp32))
        pall = ctx.enter_context(nc.psum_tensor("pall", [128, 6, 512], fp32))

        def bank(b):
            return pz[:, b, :] if b < 2 else pall[:, b - 2, :]

        def low_onehot(q):
            return (rep(lo[:, q:q + 4].rearrange("p (q a) -> p q a", a=1), 2, P),
                    rep(iorow[:, :].rearrange("p (a c) -> p a c", a=1), 1, 4))

        def pall_half(a, b, which):
            return pall[:, a:b, 0:4 * P].bitcast(u16).rearrange("p b (r h) -> p b r h", h=2)[:, :, :, which]

        c_w = sem("c_w"); c_g = sem("c_g"); c_a = sem("c_a"); c_l = sem("c_l"); c_pool = sem("c_pool"); c_dve = sem("c_dve"); c_pe = sem("c_pe")
        s_zero = sem("s_zero"); s_xz = sem("s_xz"); s_fill = sem("s_fill")
        x_in = [sem("x_in0"), sem("x_in1")]
        x_st = sem("x_st"); x_mv = sem("x_mv"); x_rs0 = sem("x_rs0"); x_rs = sem("x_rs"); x_nb = sem("x_nb"); x_n = sem("x_n")
        xT_ps = sem("xT_ps"); xT_sb = sem("xT_sb"); z_ps = sem("z_ps"); xT_lo = sem("xT_lo"); wp_hi = sem("wp_hi"); c_zb = sem("c_zb")
        z_st = sem("z_st"); z_mv = sem("z_mv"); z_rs0 = sem("z_rs0"); z_rs = sem("z_rs"); z_n = sem("z_n")
        h_g = sem("h_g"); h_ok = sem("h_ok")
        h_st = sem("h_st"); h_mv = sem("h_mv"); h_rs0 = sem("h_rs0"); h_rs = sem("h_rs"); x1_ok = sem("x1_ok")
        x1T_ps = sem("x1T_ps"); x1T_sb = sem("x1T_sb"); qk_ps = sem("qk_ps"); v_ps = sem("v_ps")
        qk_sb = sem("qk_sb"); v_sb = sem("v_sb"); s_ps = sem("s_ps"); s_msk = sem("s_msk"); s_nmx = sem("s_nmx")
        p_ok = sem("p_ok"); pT_ps = sem("pT_ps"); pT_sb = sem("pT_sb"); o_ps = sem("o_ps")
        r_inv = sem("r_inv"); g_h = sem("g_h"); g_st = sem("g_st"); g_mv = sem("g_mv")
        g_rs0 = sem("g_rs0"); g_rs = sem("g_rs"); x2_ok = sem("x2_ok")
        x2_out = [sem("x2_out0"), sem("x2_out1")]
        x2T_ps = sem("x2T_ps"); x2T_sb = sem("x2T_sb"); l_ps = sem("l_ps"); l_sb = sem("l_sb")
        d_seq = sem("d_seq")
        r_dl = sem("r_dl"); r_ed = sem("r_ed"); r_V = sem("r_V"); r_VT = sem("r_VT"); r_high = sem("r_high"); r_won = sem("r_won")
        r_n = sem("r_n"); r_pick = sem("r_pick"); r_thr = sem("r_thr"); r_ge = sem("r_ge"); r_pos = sem("r_pos")
        r_lo = sem("r_lo"); r_hi = sem("r_hi"); r_val = sem("r_val"); r_list = sem("r_list"); r_idx = sem("r_idx")
        w1_in = sem("w1_in"); w2_in = sem("w2_in")
        w1_hi = sem("w1_hi"); w1_lo = sem("w1_lo"); w2_hi = sem("w2_hi"); w2_lo = sem("w2_lo")
        i_st = sem("i_st")
        i_dst = sem("i_dst")
        g_in = [[sem(f"g_in{a}_{b}") for b in range(JT)] for a in range(2)]
        gT_ps = sem("gT_ps"); x_hi = sem("x_hi"); x_lo = sem("x_lo"); h_hi = sem("h_hi"); h_lo = sem("h_lo"); u_ps = sem("u_ps"); u_sb = sem("u_sb")
        y_ps = sem("y_ps"); y_free = sem("y_free"); y_sb = sem("y_sb");
        y_out = [sem("y_out0"), sem("y_out1")]
        hb = sem("hb")
        z_in = [sem("z_in0"), sem("z_in1")]
        a_ok = sem("a_ok"); c_ok = sem("c_ok"); c_st = sem("c_st"); c_mv = sem("c_mv"); c_rs0 = sem("c_rs0")
        c_rs = sem("c_rs"); c_d = sem("c_d"); u_ok = sem("u_ok"); o_ok = sem("o_ok")
        o_out = [sem("o_out0"), sem("o_out1")]

        block = ctx.enter_context(nc.Block())

        def live(t):
            return not isinstance(t, int) or 0 <= t < TILES

        def need(eng, s, n):
            if not isinstance(n, int) or n > 0:
                eng.wait_ge(s, n)

        turn = {}

        def plain(eng, *waits):
            for w, n in waits:
                need(eng, w, n)
            if not isinstance(waits[0][1], int):
                if eng.engine not in turn:
                    turn[eng.engine] = sem(f"turn_{len(turn)}")
                eng.sem_inc(turn[eng.engine], 1)

        N_W, N_G, N_A, N_L = 16 * 4, 16 * 4 * PER, 16 * 8, 16 * 4
        SKEW = 5
        STEPS = TILES + SKEW

        def pipeline(eng, step, lo_, hi_, first=0):
            assert (hi_ - lo_) % 4 == 0
            for i in range(first, lo_):
                step(i, i % 2)
            with eng.Fori(0, (hi_ - lo_) // 4) as j:
                for k in range(4):
                    step(j * 4 + lo_ + k, (lo_ + k) % 2)
            for i in range(hi_, STEPS):
                step(i, i % 2)

        def at(t):
            return t if isinstance(t, int) else bass.ds(t, 1)

        def tile_of(buf, t):
            if isinstance(t, int):
                return buf[:, t, :]
            return buf[:, bass.ds(t, 1), :].rearrange("p a f -> p (a f)")

        def col(buf, t):
            return buf[:, t:t + 1] if isinstance(t, int) else buf[:, bass.ds(t, 1)]

        def ycount(q, par):
            return 16 * (q // 2 + 1) if isinstance(q, int) else (q - par + 2) * 8

        def e_count(e, par, n):
            return (e // 2 + 1) * n if isinstance(e, int) else (e - par + 2) * (n // 2)

        @block.sync
        def _(sp):
            def load_x(t, par):
                n = min(PER, IMAGES - PER * t) if isinstance(t, int) else PER
                for m in range(PER):
                    if m < n:
                        src = x[PER * t + m] if isinstance(t, int) else \
                            x[bass.ds(t * PER + m, 1)].rearrange("a r f -> (a r) f")
                        sp.dma_start(xin[m * L + 1:(m + 1) * L, par, :], src).then_inc(x_in[par], 16)

            yz = y_rows[0:TRASH, :].rearrange("(p q) f -> p q f", q=Q)
            x2_v = x2_rows.rearrange("(p t) f -> p t f", t=TILES)
            sp.wait_ge(s_xz, 1)
            load_x(0, 0)

            def load(done, dst_, src):
                sp.dma_start(dst_, src).then_inc(done, 16)

            sp.wait_ge(s_zero, 1)
            for m in range(PER):
                load(c_g, g2m[m * L + 1:(m + 1) * L, :], rep(ln2_g, 0, PATCHES))
                load(c_g, posadd[m * L + 1:(m + 1) * L, :], rep(ln2_b, 0, PATCHES))
                load(c_g, posadd[m * L:m * L + 1, :], cls_token)
                load(c_g, posb[m * L:(m + 1) * L, :], pos_emb)
            load_x(1, 1)
            load(c_a, wq[:, :, :], wq_t.rearrange("(c p) o -> p c o", p=128))
            load(c_a, wk[:, :, :], wk_t.rearrange("(c p) o -> p c o", p=128))
            load(c_a, wv[:, :, :], wv_t.rearrange("(c p) o -> p c o", p=128))
            load(c_a, bqk[:, 0:EC], bq)
            load(c_a, bqk[:, EC:2 * EC], bk)
            load(c_a, bvb[:, :], rep(bv, 0, P))
            load(c_a, rw[:, :, :], router_w.rearrange("(c p) e -> p c e", p=128))
            load(c_a, rbb[:, :], rep(router_b, 0, P))

            def step(i, par):
                t = i + 2
                if live(t):
                    need(sp, x_n, i + 1)
                    load_x(t, par)
                t = i - 4
                if live(t):
                    need(sp, x2_ok, t + 1)
                    dram = x2_v[:, at(t), :]
                    if isinstance(t, int):
                        dram = x2_v[:, t:t + 1, :]
                    sp.dma_start(dram, x2[:, par:par + 1, :]).then_inc(x2_out[par], 16)
                if isinstance(i, int) and i == 1:
                    load(c_l, lng[:, :], rep(ln_g, 0, P))
                    load(c_l, lnb[:, :], rep(ln_b, 0, P))
                    load(c_l, b1t[:, :], b1)
                    load(c_l, b2b[:, :, :].rearrange("p a b -> p (a b)"), rep(b2, 0, P))
                for n in range(FILLS):
                    if isinstance(i, int) and i - 2 == n // 2:
                        if n == 0:
                            sp.wait_ge(s_xz, 2)
                        a, b = n * ZT, min((n + 1) * ZT, Q)
                        sp.dma_start(yz[:, a:b, :], zero[:, 0:(b - a) * ED].rearrange("p (q f) -> p q f", f=ED))\
                            .then_inc(s_fill, 16)
            pipeline(sp, step, 7, 19)

            def load_w1(e):
                src = w1[e:e + 1] if isinstance(e, int) else w1[bass.ds(e, 1)]
                sp.dma_start(w1r[:, :, :], src.rearrange("a (c p) h -> p (a c) h", p=128)).then_inc(w1_in, 16)

            def load_w2(e):
                src = w2[e:e + 1] if isinstance(e, int) else w2[bass.ds(e, 1)]
                sp.dma_start(w2r[:, :, :], src.rearrange("a (k p) o -> p (a k) o", p=128)).then_inc(w2_in, 16)

            sp.wait_ge(x_n, TILES)
            sp.wait_ge(xT_ps, TILES)
            sp.wait_ge(z_ps, TILES)
            load_w1(0)
            load_w2(0)
            sp.wait_ge(g_in[0][JT - 1], 16)
            with sp.Fori(0, E - 1) as j:
                sp.wait_ge(w1_lo, j + 1)
                load_w1(j + 1)
                sp.wait_ge(w2_lo, j * 2 + 2)
                load_w2(j + 1)

            for par in range(2):
                sp.wait_ge(y_out[par], 16 * JT * E // 2)
            y_v = y_rows[0:TRASH, :].rearrange("(p q) f -> p q f", q=Q)
            PAIRS = TILES // 2
            o_v = out[0:(TILES - 1) * PER * L, :].rearrange("(t r) f -> r t f", r=PER * L)

            def load_y(q, par):
                cols = slice(4 * q, 4 * q + 4) if isinstance(q, int) else bass.ds(q * 4, 4)
                sp.dma_start(yin[:, cols, :], y_v[:, cols, :]).then_inc(z_in[par], 16)

            def store(q, par):
                sp.wait_ge(o_ok, q * 2 + 2)
                src = yo[:, 2 * par:2 * par + 2, :]
                dst_ = o_v[:, 2 * q:2 * q + 2, :] if isinstance(q, int) else o_v[:, bass.ds(q * 2, 2), :]
                sp.dma_start(dst_[0:96, :, :], src[0:96, :, :]).then_inc(o_out[par], 16)
                sp.dma_start(dst_[96:PER * L, :, :], src[96:PER * L, :, :]).then_inc(o_out[par], 16)

            for q in range(4):
                if q >= 2:
                    sp.wait_ge(z_in[q % 2], ycount(q - 2, q % 2))
                load_y(q, q % 2)
            with sp.Fori(0, (PAIRS - 5) // 2) as j:
                for par in range(2):
                    q = j * 2 + par
                    sp.wait_ge(z_in[par], ycount(q + 2, par))
                    load_y(q + 4, par)
                    store(q, par)
            q = PAIRS - 5
            sp.wait_ge(z_in[0], ycount(q + 2, 0))
            load_y(q + 4, 0)
            for q in range(q, PAIRS - 1):
                store(q, q % 2)
            t = TILES - 2
            sp.wait_ge(o_ok, TILES)
            rows_ = PER * L
            for a, b, k in ((0, 96, 0), (96, rows_, 0), (0, 32, 1), (32, LIVE_LAST, 1)):
                sp.dma_start(out[(t + k) * rows_ + a:(t + k) * rows_ + b, :], yo[a:b, k, :]).then_inc(o_out[0], 16)
            sp.wait_ge(o_out[0], 32 * (PAIRS // 2) + 64)
            sp.wait_ge(o_out[1], 32 * (PAIRS // 2))
            for par in range(2):
                sp.wait_ge(x2_out[par], 16 * (TILES // 2))
                sp.wait_ge(y_out[par], 16 * JT * E // 2)

        @block.scalar
        def _(act):
            def load(done, dst_, src):
                nc.scalar.dma_start(dst_, src).then_inc(done, 16)

            load(c_w, wproj[:, :, :], w_proj.rearrange("(c p) e -> p c e", p=128))
            load(c_w, ln1g[:, :], ln1_g)
            load(c_w, ln1b[:, :], ln1_b)
            load(c_w, bproj[:, :], b_proj)
            act.wait_ge(c_pool, 1)
            nc.scalar.copy(ones2[:, :], onesrow[:, 0:P])
            def norm_x(t, par):
                need(act, x_nb, t + 1)
                need(act, xT_ps, t - 1)
                nc.scalar.activation(xn[:, par, :], xin[:, par, :], ACT.Identity, bias=rs[:, 0, 2:3],
                                     scale=rs[:, 0, 1:2]).then_inc(x_n, 1)

            act.wait_ge(c_w, N_W)
            for c in range(PC):
                a = nc.scalar.activation(wph[:, c, :], wproj[:, c, :], ACT.Copy, scale=ln1g[:, c:c + 1])
            a.then_inc(wp_hi, 1)
            norm_x(0, 0)

            def step(i, par):
                t = i - 3
                if live(t):
                    need(act, s_nmx, t + 1)
                    need(act, pT_ps, t)
                    need(act, r_inv, t - 1)
                    nc.scalar.activation(prob[:, :], masked[:, :], ACT.Exp, bias=nmax[:, 0:1], scale=1.0 / ED,
                                         accum_out=psumr[:, (par + 1) % 2:(par + 1) % 2 + 1]).then_inc(p_ok, 1)
                t = i
                if live(t):
                    need(act, xT_ps, t + 1)
                    need(act, z_ps, t)
                    nc.scalar.copy(xnTh.rearrange("p (b r) -> p b r", b=2), pz[:, :, 0:3 * P]).then_inc(xT_sb, 1)
                if isinstance(i, int) and i == 2:
                    act.wait_ge(c_a, N_A)
                t = i - 2
                if live(t):
                    need(act, qk_ps, t + 1)
                    need(act, s_ps, t)
                    for c in range(2 * EC):
                        a = nc.scalar.activation(qkT[:, c, :], bank(3)[:, c * P:(c + 1) * P], ACT.Identity,
                                                 bias=bqk[:, c:c + 1])
                    a.then_inc(qk_sb, 1)
                t = i - 3
                if live(t):
                    need(act, pT_ps, t + 1)
                    need(act, o_ps, t)
                    nc.scalar.copy(probT[:, :], bank(5)[0:P, 0:P]).then_inc(pT_sb, 1)
                t = i + 1
                if live(t):
                    norm_x(t, (par + 1) % 2)
                t = i - 1
                if live(t):
                    need(act, x1T_ps, t + 1)
                    need(act, v_ps, t - 1)
                    nc.scalar.copy(x1T[:, (par + 1) % 2, :], bank(6)[:, 0:EC * P]).then_inc(x1T_sb, 1)
                t = i - 4
                if live(t):
                    need(act, x2T_ps, t + 1)
                    need(act, l_ps, t)
                    nc.scalar.copy(x2T[:, :], bank(4)[:, 0:EC * P]).then_inc(x2T_sb, 1)
            pipeline(act, step, 6, 18)

            act.wait_ge(r_dl, 1)
            nc.scalar.activation(ed[:, :], dl[:, :], ACT.Exp).then_inc(r_ed, 1)

            for k in range(2):
                act.wait_ge(r_VT, k + 1)
                nc.scalar.copy(highh[:, k * GATES // 2:(k + 1) * GATES // 2].rearrange("p (b r) -> p b r", b=3),
                               pall_half(3 * k, 3 * k + 3, 1)).then_inc(r_high, 1)

            act.wait_ge(c_l, N_L)

            def w1_high(e):
                act.wait_ge(w1_in, 16 * e + 16)
                need(act, u_ps, e * HC)
                nc.scalar.copy(w1h[:, :, :], w1r[:, :, :]).then_inc(w1_hi, 1)

            def w2_high(e, half):
                if half == 0:
                    act.wait_ge(w2_in, 16 * e + 16)
                    need(act, y_ps, e * JT)
                k = half * HC // 2
                nc.scalar.copy(w2h[:, k:k + HC // 2, :], w2r[:, k:k + HC // 2, :]).then_inc(w2_hi, 1)

            def x_high(e):
                act.wait_ge(gT_ps, e + 1)
                nc.scalar.copy(xgh[:, :, :], pall[:, 2:4, 0:SLOTS]).then_inc(x_hi, 1)

            def gelu(e, k):
                u = e * HC + k
                act.wait_ge(u_ps, u + 1)
                need(act, h_lo, u - 1)
                nc.scalar.activation(hr[:, k % 2, :], bank(k % 4)[:, 0:SLOTS], ACT.Gelu,
                                     bias=col(b1t, u)).then_inc(u_sb, 1)

            def expert(e, last=False):
                w2_high(e, 0)
                gelu(e, 0)
                gelu(e, 1)
                w2_high(e, 1)
                for k in range(2, HC):
                    gelu(e, k)
                if not last:
                    x_high(e + 1)
                    w1_high(e + 1)

            w1_high(0)
            nc.scalar.activation(warm[:, :], ed[:, 0:1], ACT.Gelu)
            x_high(0)
            expert(0)
            with act.Fori(0, E - 2) as j:
                expert(j + 1)
            expert(E - 1, last=True)

            def first_choice(q, par, k, first=False):
                t = q * 2 + k
                if k == 0:
                    act.wait_ge(z_in[par], ycount(q, par))
                if not first:
                    act.wait_ge(c_ok, t - 1)
                nc.scalar.activation(ya[:, k, :], tile_of(yin, t * 2), ACT.Copy,
                                     scale=col(wtok[:, 0, :], t)).then_inc(a_ok, 1)

            def scaled(q, par, k, first=False):
                t = q * 2 + k
                act.wait_ge(c_d, t + 1)
                act.wait_ge(c_rs, q + 1)
                if not first:
                    act.wait_ge(o_ok, t - 1)
                nc.scalar.activation(yu[:, k, :], yd[:, k, :], ACT.Copy, scale=yrs[:, 1 + par, k:k + 1]).then_inc(u_ok, 1)

            for k in range(2):
                first_choice(0, 0, k, True)
            for k in range(2):
                first_choice(1, 1, k)
            for k in range(2):
                scaled(0, 0, k, True)
            with act.Fori(0, (TILES // 2 - 3) // 2) as j:
                for par in range(2):
                    q = j * 2 + 1 + par
                    for k in range(2):
                        first_choice(q + 1, par, k)
                    for k in range(2):
                        scaled(q, 1 - par, k)
            q = TILES // 2 - 2
            for k in range(2):
                first_choice(q + 1, 0, k)
            for q in (q, q + 1):
                for k in range(2):
                    scaled(q, q % 2, k)

        @block.tensor
        def _(pe):
            pe.wait_ge(c_pool, 1)
            pe.wait_ge(c_w, N_W)
            pe.wait_ge(c_dve, 1)
            for c in range(PC):
                nc.tensor.matmul(bank(2)[0:2, 0:ED], ln1bb[:, c, :], wproj[:, c, :], start=(c == 0), stop=False)
            nc.tensor.matmul(bank(2)[0:2, 0:ED], onesrow[0:1, 0:2], bproj[0:1, :], start=False, stop=True)\
                .then_inc(c_pe, 1)

            def step(i, par):
                odd = (par + 1) % 2
                t = i
                if live(t):
                    need(pe, x_n, t + 1)
                    need(pe, xT_lo, t)
                    for c in range(PC):
                        m = nc.tensor.transpose(bank(c // 3)[:, (c % 3) * P:(c % 3 + 1) * P],
                                                xn[:, par, c * 128:(c + 1) * 128], ident[0:P, 0:P])
                    m.then_inc(xT_ps, 1)
                if isinstance(i, int) and i == 2:
                    pe.wait_ge(c_a, N_A)
                t = i - 2
                if live(t):
                    need(pe, x1T_sb, t + 1)
                    need(pe, qk_sb, t)
                    xt = x1T[:, par, :].rearrange("p (c r) -> p c r", c=EC)
                    for o in range(2 * EC):
                        w = wq if o < EC else wk
                        for c in range(EC):
                            m = nc.tensor.matmul(bank(3)[:, o * P:(o + 1) * P],
                                                 w[:, c, (o % EC) * 128:(o % EC + 1) * 128], xt[:, c, :],
                                                 start=(c == 0), stop=(c == EC - 1))
                    m.then_inc(qk_ps, 1)
                    need(pe, x2T_sb, t - 2)
                    need(pe, v_sb, t)
                    for c in range(EC):
                        m = nc.tensor.matmul(bank(4)[0:P, 0:ED], xt[:, c, :], wv[:, c, :],
                                             start=(c == 0), stop=(c == EC - 1))
                    m.then_inc(v_ps, 1)
                t = i - 3
                if live(t):
                    need(pe, p_ok, t + 1)
                    nc.tensor.transpose(bank(5)[0:P, 0:P], prob[:, :], ident[0:P, 0:P]).then_inc(pT_ps, 1)
                t = i - 5
                if live(t):
                    need(pe, x2T_sb, t + 1)
                    need(pe, l_sb, t)
                    need(pe, g_h, t + 2 if not isinstance(t, int) else min(t + 2, TILES))
                    for c in range(EC):
                        m = nc.tensor.matmul(bank(7)[0:P, 0:E], x2T[:, c * P:(c + 1) * P], rw[:, c, :],
                                             start=(c == 0), stop=(c == EC - 1))
                    m.then_inc(l_ps, 1)
                t = i
                if isinstance(i, int) and i == 0:
                    pe.wait_ge(c_dve, 2)
                if live(t):
                    need(pe, xT_lo, t + 1)
                    need(pe, z_n, t)
                    for c in range(PC):
                        for k, (xs, w) in enumerate(((xnTh, wph), (xnTh, wpl), (xnTl, wph))):
                            nc.tensor.matmul(bank(2)[0:P, 0:ED], xs[:, c * P:(c + 1) * P], w[:, c, :],
                                             start=(c == k == 0), stop=False)
                    nc.tensor.matmul(bank(2)[0:P, 0:ED], ones2[:, :], zbias[:, :], start=False, stop=True)\
                        .then_inc(z_ps, 1)
                t = i - 3
                if live(t):
                    need(pe, pT_sb, t + 1)
                    need(pe, v_sb, t + 1)
                    need(pe, l_sb, t - 1)
                    need(pe, g_h, t)
                    nc.tensor.matmul(bank(7)[0:P, 0:ED], probT[:, :], v[:, odd, :], start=True, stop=True)\
                        .then_inc(o_ps, 1)
                t = i - 2
                if live(t):
                    need(pe, qk_sb, t + 1)
                    need(pe, s_msk, t)
                    for c in range(EC):
                        m = nc.tensor.matmul(bank(5)[0:P, 0:P], qkT[:, c, :], qkT[:, EC + c, :],
                                             start=(c == 0), stop=(c == EC - 1))
                    m.then_inc(s_ps, 1)
                t = i - 1
                if live(t):
                    need(pe, x1_ok, t + 1)
                    need(pe, x1T_sb, t)
                    for c in range(EC):
                        m = nc.tensor.transpose(bank(6)[:, c * P:(c + 1) * P],
                                                x1[:, odd, c * 128:(c + 1) * 128], ident[0:P, 0:P])
                    m.then_inc(x1T_ps, 1)
                t = i - 4
                if live(t):
                    need(pe, x2_ok, t + 1)
                    if not isinstance(t, int) or t + 3 <= TILES:
                        need(pe, v_sb, t + 3)
                    for c in range(EC):
                        m = nc.tensor.transpose(bank(4)[:, c * P:(c + 1) * P],
                                                x2[:, par, c * 128:(c + 1) * 128], ident[0:P, 0:P])
                    m.then_inc(x2T_ps, 1)
            pipeline(pe, step, 6, 22)

            pe.wait_ge(l_sb, TILES)
            pe.wait_ge(g_h, TILES)
            pe.wait_ge(x2T_sb, TILES)
            pe.wait_ge(c_pool, 4)
            for t in range(PAD):
                if t % (PAD // 2) == 0:
                    pe.wait_ge(r_V, 2 * t // PAD + 1)
                m = nc.tensor.transpose(pall[:, t // 4, (t % 4) * P:(t % 4 + 1) * P], vrep[:, t, :], ident[0:P, 0:P])
                if t % (PAD // 2) == PAD // 2 - 1:
                    m.then_inc(r_VT, 1)
            for r in range(2 * len(SHIFTS)):
                pe.wait_ge(r_won, r + 1)
                nc.tensor.matmul(bank(r % 2)[:, 0:1], grp[:, :], won[:, :], start=True, stop=True).then_inc(r_n, 1)
            pe.wait_ge(r_pick, 1)
            nc.tensor.matmul(bank(0)[0:P, 0:E], onesf[:, 0:P], thrrow[:, :], start=True, stop=True).then_inc(r_thr, 1)
            pe.wait_ge(r_ge, 1)
            gev = ge[:, :, :, :].rearrange("p s e t -> p (s e t)")
            n = 2 * E * TILES
            nc.tensor.matmul(bank(2)[0:P, 0:n], below[0:P, 0:P], gev, start=True, stop=True)
            nc.tensor.matmul(bank(3)[0:P, 0:n], onesb[0:P, 0:P], gev, start=True, stop=True).then_inc(r_pos, 1)
            pe.wait_ge(r_val, 2)
            for q in range(Q):
                if q % 4 == 0:
                    pe.wait_ge(r_lo, q // 4 + 1)
                m = nc.tensor.matmul(bank(4)[0:P, 0:2 * COLS], ohlo[:, q, :],
                                     ohval[:, q, :, :].rearrange("p a b -> p (a b)"),
                                     start=(q == 0), stop=(q == Q - 1))
            m.then_inc(r_list, 1)

            def transposes(e, par):
                pe.wait_ge(x_lo, e) if not isinstance(e, int) else need(pe, x_lo, e)
                for j in range(JT):
                    pe.wait_ge(g_in[par][j], e_count(e, par, 16))
                    for c in range(EC):
                        m = nc.tensor.transpose(bank(4 + c)[:, j * P:(j + 1) * P],
                                                xg[:, par, j, c * 128:(c + 1) * 128], ident[0:P, 0:P])
                m.then_inc(gT_ps, 1)

            def expert(e, par, last=False):
                pe.wait_ge(w1_lo, e + 1)
                pe.wait_ge(x_lo, e + 1)
                for k in range(HC):
                    need(pe, u_sb, e * HC + k - 3)
                    n = 0
                    for c in range(EC):
                        for w, xs in ((w1h, xgh), (w1h, xgl), (w1l, xgh)):
                            m = nc.tensor.matmul(bank(k % 4)[:, 0:SLOTS], w[:, c, k * 128:(k + 1) * 128], xs[:, c, :],
                                                 start=(n == 0), stop=(n == 3 * EC - 1))
                            n += 1
                    m.then_inc(u_ps, 1)
                if not last:
                    transposes(e + 1, 1 - par)
                for j in range(JT):
                    need(pe, y_sb, e * JT + j - 1)
                    n = 0
                    for k in range(HC):
                        if j == 0:
                            if k % (HC // 2) == 0:
                                pe.wait_ge(w2_lo, e * 2 + 1 + 2 * k // HC)
                            pe.wait_ge(h_lo, e * HC + k + 1)
                        for hs, w in ((hh, w2h), (hh, w2l), (hl, w2h)):
                            m = nc.tensor.matmul(bank(6 + j % 2)[0:P, 0:ED], hs[:, k, j * P:(j + 1) * P], w[:, k, :],
                                                 start=(n == 0), stop=(n == 3 * HC - 1))
                            n += 1
                    m.then_inc(y_ps, 1)

            transposes(0, 0)
            expert(0, 0)
            expert(1, 1)
            with pe.Fori(0, (E - 4) // 2) as j:
                for par in range(2):
                    expert(j * 2 + 2 + par, par)
            expert(E - 2, 0)
            expert(E - 1, 1, last=True)

        @block.vector
        def _(dve):
            V_ = nc.vector
            V_.memset(xin[:, :, :], 0.0).then_inc(s_xz, 1)
            V_.memset(g2m[:, :], 0.0)
            V_.memset(posb[:, :], 0.0)
            V_.memset(posadd[:, :], 0.0).then_inc(s_zero, 1)
            V_.memset(V[:, :, :], 0.0)
            V_.memset(zero[:, :], 0.0).then_inc(s_xz, 1)
            dve.wait_ge(c_w, N_W)
            dve.wait_ge(c_pool, 1)
            V_.tensor_copy(ln1bb[:, :, :], rep(ln1b[:, :].rearrange("p (c a) -> p c a", a=1), 2, 2)).then_inc(c_dve, 1)
            def stats_x(t, par):
                need(dve, x_mv, t)
                three = 48
                if isinstance(t, int):
                    n = sum(min(PER, IMAGES - PER * s) for s in range(par, t + 1, 2))
                    dve.wait_ge(x_in[par], 16 * n)
                else:
                    dve.wait_ge(x_in[par], (t - par + 2) * (three // 2))
                for hlf in range(2):
                    m = V_.bn_stats(xstat[:, hlf, :], xin[:, par, hlf * HALF:(hlf + 1) * HALF])
                m.then_inc(x_st, 1)
                plain(dve, (x_st, t + 1), (x_nb, t))
                V_.bn_aggr(xmv[:, :], xstat[:, :, :].rearrange("p a b -> p (a b)")).then_inc(x_mv, 1)

            stats_x(0, 0)
            dve.wait_ge(wp_hi, 1)
            for c in range(PC):
                V_.scalar_tensor_tensor(wpl[:, c, :], wproj[:, c, :], ln1g[:, c:c + 1], wph[:, c, :].bitcast(fp32),
                                        ALU.mult, ALU.subtract)
            dve.wait_ge(c_pe, 1)
            V_.tensor_copy(zb[:, :], bank(2)[0:2, 0:ED]).then_inc(c_zb, 1)
            dve.wait_ge(c_zb, 1)
            V_.tensor_copy(zbh[:, :], zb[:, :]).then_inc(c_zb, 1)
            dve.wait_ge(c_zb, 2)
            V_.tensor_tensor(zb[:, :], zb[:, :], zbh[:, :].bitcast(fp32), ALU.subtract).then_inc(c_zb, 1)
            V_.tensor_scalar(zbm[:, :], zbh[:, :].bitcast(fp32), ident[0:2, 0:1], None, ALU.mult).then_inc(c_zb, 1)
            dve.wait_ge(c_zb, 4)
            V_.scalar_tensor_tensor(zbias[:, :], zb[:, :], ident[0:2, 1:2], zbm[:, :], ALU.mult, ALU.add)\
                .then_inc(c_dve, 1)

            def step(i, par):
                odd = (par + 1) % 2
                masked_t, z_t, g_t, h_t = i - 3, i - 1, i - 4, i - 1
                if live(masked_t):
                    t = masked_t
                    if isinstance(t, int) and t == 0:
                        dve.wait_ge(c_pool, 2)
                    plain(dve, (s_ps, t + 1), (p_ok, t), (s_nmx, t))
                    V_.tensor_tensor_reduce(masked[:, :], bank(5)[0:P, 0:P], amask[:, :], 1.0, MASKED,
                                            ALU.add, ALU.max, smax[:, 0:1]).then_inc(s_msk, 1)
                if live(g_t):
                    need(dve, o_ps, g_t + 1)
                    need(dve, g_h, g_t)
                    V_.reciprocal(rinv[:, :], psumr[:, par:par + 1]).then_inc(r_inv, 1)
                if live(masked_t):
                    need(dve, s_msk, masked_t + 1)
                    V_.tensor_scalar(nmax[:, :], smax[:, :], -1.0 / ED, None, ALU.mult).then_inc(s_nmx, 1)
                if live(g_t):
                    t = g_t
                    need(dve, r_inv, t + 1)
                    V_.scalar_tensor_tensor(tile_of(H, t), bank(7)[0:P, 0:ED], rinv[:, 0:1], tile_of(H, t),
                                            ALU.mult, ALU.add).then_inc(g_h, 1)
                if live(z_t):
                    t = z_t
                    need(dve, z_rs, t + 1)
                    need(dve, h_g, t)
                    V_.tensor_scalar(zn[:, :], bank(2)[0:P, 0:ED], zmv[:, 0:1], rs[:, 1, 1:2],
                                     ALU.subtract, ALU.mult).then_inc(z_n, 1)
                t = i
                if live(t):
                    need(dve, xT_sb, t + 1)
                    V_.tensor_tensor(xnTl.rearrange("p (b r) -> p b r", b=2), pz[:, :, 0:3 * P],
                                     xnTh.bitcast(fp32).rearrange("p (b r) -> p b r", b=2),
                                     ALU.subtract).then_inc(xT_lo, 1)
                if live(g_t):
                    t = g_t
                    plain(dve, (g_h, t + 1), (g_mv, t))
                    V_.bn_stats(gstat[:, :], tile_of(H, t)).then_inc(g_st, 1)
                if live(g_t):
                    t = g_t
                    plain(dve, (g_st, t + 1), (x2_ok, t))
                    V_.bn_aggr(gmv[:, :], gstat[:, :]).then_inc(g_mv, 1)
                if live(h_t):
                    t = h_t
                    plain(dve, (h_ok, t + 1))
                    V_.bn_stats(hstat[:, :], tile_of(H, t)).then_inc(h_st, 1)
                t = i - 2
                if live(t):
                    if isinstance(t, int) and t == 0:
                        dve.wait_ge(c_a, N_A)
                    need(dve, v_ps, t + 1)
                    need(dve, o_ps, t - 1)
                    V_.tensor_tensor(v[:, par, :], bank(4)[0:P, 0:ED], bvb[:, :], ALU.add).then_inc(v_sb, 1)
                t = i - 5
                if live(t):
                    need(dve, l_ps, t + 1)
                    V_.tensor_tensor(LG[:, :, at(t)] if not isinstance(t, int) else LG[:, :, t:t + 1],
                                     bank(7)[0:P, 0:E].rearrange("p (e a) -> p e a", a=1),
                                     rbb[:, :].rearrange("p (e a) -> p e a", a=1), ALU.add).then_inc(l_sb, 1)
                if live(h_t):
                    t = h_t
                    plain(dve, (h_st, t + 1), (x1_ok, t))
                    V_.bn_aggr(hmv[:, :], hstat[:, :]).then_inc(h_mv, 1)
                if isinstance(i, int) and i == 0:
                    stats_x(1, 1)
                t = i + 2
                if live(t):
                    stats_x(t, par)
                t = i - 1
                if live(t):
                    need(dve, h_rs, t + 1)
                    need(dve, x1T_ps, t - 1)
                    V_.tensor_scalar(x1[:, odd, :], tile_of(H, t), hmv[:, 0:1], rs[:, 2, 1:2],
                                     ALU.subtract, ALU.mult).then_inc(x1_ok, 1)
                t = i - 4
                if live(t):
                    need(dve, g_rs, t + 1)
                    need(dve, x2T_ps, t - 1)
                    if isinstance(t, int):
                        need(dve, x2_out[par], 16 * (t // 2))
                    else:
                        need(dve, x2_out[par], (t - par) * 8)
                    V_.tensor_scalar(x2[:, par, :], tile_of(H, t), gmv[:, 0:1], rs[:, 3, 1:2],
                                     ALU.subtract, ALU.mult).then_inc(x2_ok, 1)
                if isinstance(i, int) and i == 0:
                    dve.wait_ge(c_g, N_G)
                    V_.tensor_tensor(posb[:, :], posb[:, :], posadd[:, :], ALU.add).then_inc(c_dve, 1)
                if isinstance(i, int) and i == 6:
                    dve.wait_ge(c_pool, 4)
                    V_.tensor_scalar(thi[:, 0:1], pidx[:, :], WAYS - 1, None, ALU.bitwise_and).then_inc(c_zb, 1)
                    dve.wait_ge(c_zb, 5)
                    V_.tensor_copy(way[:, :], thi[:, 0:1]).then_inc(c_zb, 1)
                    dve.wait_ge(c_zb, 6)
                    for k, sh in enumerate(SHIFTS):
                        unit, nxt = 2.0 ** sh, 2.0 ** SHIFTS[k + 1] if k + 1 < len(SHIFTS) else 0.0
                        V_.tensor_scalar(nextd[:, k:k + 1], way[:, :], nxt - unit, -unit, ALU.mult, ALU.add)
                t = i
                if live(t):
                    need(dve, z_ps, t + 1)
                    need(dve, z_n, t)
                    V_.bn_stats(zstat[:, :], bank(2)[0:P, 0:ED]).then_inc(z_st, 1)
                t = i
                if live(t):
                    plain(dve, (z_st, t + 1))
                    V_.bn_aggr(zmv[:, :], zstat[:, :]).then_inc(z_mv, 1)
            pipeline(dve, step, 7, 19)

            seq = 0

            def link(inst):
                nonlocal seq
                seq += 1
                inst.then_inc(d_seq, 1)
                dve.wait_ge(d_seq, seq)

            def over_e(a):
                return a.rearrange("p e t -> p t e")

            def per_tile(a):
                return rep(a.rearrange("p (a t) -> p a t", a=1), 1, E)

            dve.wait_ge(l_sb, TILES)
            scores = LG
            for k, oh in enumerate((oh1, oh2)):
                link(V_.tensor_reduce(m12[:, k, :], over_e(scores[:, :, :]), AX.X, ALU.max))
                link(V_.tensor_tensor(eqm[:, :, :], scores[:, :, :], per_tile(m12[:, k, :]), ALU.is_equal))
                link(V_.tensor_tensor(eqm[:, :, :], eqm[:, :, :], erev[:, :, :], ALU.mult))
                link(V_.tensor_reduce(f12[:, k, :], over_e(eqm[:, :, :]), AX.X, ALU.max))
                link(V_.tensor_tensor(oh[:, :, :], eqm[:, :, :], per_tile(f12[:, k, :]), ALU.is_equal))
                if k == 0:
                    link(V_.scalar_tensor_tensor(lg2[:, :, :].rearrange("p e t -> p (e t)"),
                                                 oh1[:, :, :].rearrange("p e t -> p (e t)"), MASKED,
                                                 LG[:, :, :].rearrange("p e t -> p (e t)"), ALU.mult, ALU.add))
                    scores = lg2
            V_.tensor_tensor(dl[:, :], m12[:, 1, :], m12[:, 0, :], ALU.subtract).then_inc(r_dl, 1)
            dve.wait_ge(r_ed, 1)
            link(V_.tensor_scalar(dl[:, :], ed[:, :], 1.0, None, ALU.add))
            link(V_.reciprocal(gate[:, 0, :], dl[:, :]))
            link(V_.tensor_tensor(gate[:, 0, :], gate[:, 0, :], valid[:, :], ALU.mult))
            link(V_.tensor_tensor(gate[:, 1, :], gate[:, 0, :], ed[:, :], ALU.mult))
            V_.tensor_tensor(V[:, :, 0:TILES], oh1[:, :, :], per_tile(gate[:, 0, :]), ALU.mult)
            link(V_.tensor_tensor(V2[:, :, :], oh2[:, :, :], per_tile(gate[:, 1, :]), ALU.mult))
            link(V_.tensor_tensor(V[:, :, 0:TILES], V[:, :, 0:TILES], V2[:, :, :], ALU.add))
            dve.wait_ge(s_fill, 16 * FILLS)
            for k in range(2):
                t0, t1 = k * PAD // 2, (k + 1) * PAD // 2
                V_.tensor_copy(vrep[:, t0:t1, :].rearrange("p t (e w) -> p t e w", w=WAYS),
                               rep(V[:, :, t0:t1].rearrange("p e (t a) -> p t e a", a=1), 3, WAYS)).then_inc(r_V, 1)
            R4 = len(SHIFTS)

            def search(half, gates):
                link(V_.tensor_scalar(cand[:, half * R4:half * R4 + 1], way[:, :], 2.0 ** SHIFTS[0], None, ALU.mult))
                for k, sh in enumerate(SHIFTS):
                    r = half * R4 + k
                    link(V_.tensor_scalar(junk, gates, cand[:, r:r + 1], None, ALU.is_ge, ALU.add,
                                          accum_out=cnt[:, 0:1]))
                    if half == 0:
                        V_.tensor_scalar(won[:, :], cnt[:, 0:1], CAP - 0.5, None, ALU.is_ge).then_inc(r_won, 1)
                    else:
                        V_.tensor_scalar(won[:, :], cnt[:, 0:1], cnt[:, 1:2], CAP - 0.5, ALU.add, ALU.is_ge)\
                            .then_inc(r_won, 1)
                    link(V_.tensor_tensor(known[:, r % 2:r % 2 + 1], cand[:, r:r + 1], nextd[:, k:k + 1], ALU.add))
                    dve.wait_ge(r_n, r + 1)
                    to = cand[:, r + 1:r + 2] if k + 1 < R4 else thalf[:, half:half + 1]
                    link(V_.scalar_tensor_tensor(to, bank(r % 2)[:, 0:1], 2.0 ** sh, known[:, r % 2:r % 2 + 1],
                                                 ALU.mult, ALU.add))

            dve.wait_ge(r_high, 2)
            search(0, highh)
            link(V_.tensor_scalar(thalf[:, 2:3], thalf[:, 0:1], 1.0, None, ALU.add))
            link(V_.tensor_scalar(junk, highh, thalf[:, 2:3], None, ALU.is_ge, ALU.add, accum_out=cnt[:, 1:2]))
            link(V_.scalar_tensor_tensor(lowh.rearrange("p (b r) -> p b r", b=6),
                                         highh.rearrange("p (b r) -> p b r", b=6), thalf[:, 0:1],
                                         pall_half(0, 6, 0), ALU.is_equal, ALU.mult))
            search(1, lowh)
            link(V_.tensor_copy(thi[:, 0:2], thalf[:, 0:2]))
            link(V_.tensor_scalar(thi[:, 0:1], thi[:, 0:1], 16, None, ALU.logical_shift_left))
            link(V_.tensor_tensor(thr, thi[:, 0:1], thi[:, 1:2], ALU.bitwise_or))
            V_.tensor_scalar(thrrow[:, :], pick[:, :], thr.bitcast(fp32), None, ALU.mult).then_inc(r_pick, 1)
            dve.wait_ge(r_thr, 1)
            link(V_.tensor_copy(thrb[:, :], bank(0)[0:P, 0:E]))
            thre = rep(thrb[:, :].rearrange("p (e a) -> p e a", a=1), 2, TILES)
            V_.tensor_tensor(ge[:, 0, :, :], V[:, :, 0:TILES], thre, ALU.is_gt)
            V_.tensor_tensor(ge[:, 1, :, :], V[:, :, 0:TILES], thre, ALU.is_equal).then_inc(r_ge, 1)
            link(V_.tensor_scalar(okeq[:, :, :], V[:, :, 0:TILES], 0.0, None, ALU.is_gt))
            dve.wait_ge(r_ge, 1)
            dve.wait_ge(r_pos, 1)
            n = 2 * E * TILES
            link(V_.tensor_tensor_scan(tincl[:, :, :].rearrange("p a t -> p (a t)"),
                                       keep0[:, :, :].rearrange("p a t -> p (a t)"), bank(3)[0:P, 0:n], 0.0,
                                       ALU.mult, ALU.add))
            posf = pos[:, :, :, :].rearrange("p s e t -> p (s e t)")
            link(V_.tensor_tensor(posf, tincl[:, :, :].rearrange("p a t -> p (a t)"), bank(3)[0:P, 0:n], ALU.subtract))
            link(V_.tensor_tensor(posf, posf, bank(2)[0:P, 0:n], ALU.add))
            above = rep(tincl[:, 0:E, TILES - 1:TILES], 2, TILES)
            link(V_.tensor_tensor(pos[:, 1, :, :], pos[:, 1, :, :], above, ALU.add))
            link(V_.tensor_tensor(okeq[:, :, :], okeq[:, :, :], ge[:, 1, :, :], ALU.mult))
            link(V_.tensor_scalar(ok[:, :, :], pos[:, 1, :, :], CAP - 0.5, None, ALU.is_le))
            link(V_.tensor_tensor(okeq[:, :, :], okeq[:, :, :], ok[:, :, :], ALU.mult))
            V_.tensor_tensor(pos[:, 0, :, :], pos[:, 0, :, :], base1[:, :, :], ALU.add)
            link(V_.tensor_tensor(pos[:, 1, :, :], pos[:, 1, :, :], base1[:, :, :], ALU.add))
            V_.tensor_tensor(pos[:, 0, :, :], pos[:, 0, :, :], ge[:, 0, :, :], ALU.mult)
            link(V_.tensor_tensor(pos[:, 1, :, :], pos[:, 1, :, :], okeq[:, :, :], ALU.mult))
            link(V_.tensor_tensor(aslot[:, :, :], pos[:, 0, :, :], pos[:, 1, :, :], ALU.add))
            for k, oh in enumerate((oh1, oh2)):
                link(V_.tensor_tensor(eqm[:, :, :], aslot[:, :, :], oh[:, :, :], ALU.mult))
                link(V_.tensor_reduce(s12[:, k, :], over_e(eqm[:, :, :]), AX.X, ALU.add))
            s12f = s12[:, :, :].rearrange("p k t -> p (k t)")
            link(V_.tensor_scalar(wtok[:, :, :].rearrange("p k t -> p (k t)"), s12f, 0.5, None, ALU.is_ge))
            link(V_.tensor_tensor(wtok[:, :, :], wtok[:, :, :], gate[:, :, :], ALU.mult))
            BIG = 1.5 * 2.0 ** 23
            link(V_.tensor_scalar(hi[:, :], s12f, 1.0 / P, -0.5 - 0.5 / P, ALU.mult, ALU.add))
            link(V_.tensor_scalar(hi[:, :], hi[:, :], BIG, None, ALU.add))
            link(V_.tensor_scalar(hi[:, :], hi[:, :], -BIG, None, ALU.add))
            link(V_.scalar_tensor_tensor(lo[:, :], hi[:, :], -float(P), s12f, ALU.mult, ALU.add))
            link(V_.tensor_scalar(lo[:, :], lo[:, :], -1.0, None, ALU.add))
            hib = rep(hi[:, :].rearrange("p (q a) -> p q a", a=1), 2, COLS)
            V_.tensor_tensor(ohhi[:, :, :], hib, rep(iorow[:, 0:COLS].rearrange("p (a c) -> p a c", a=1), 1, Q),
                             ALU.is_equal).then_inc(r_hi, 1)
            dve.wait_ge(r_hi, 1)
            V_.tensor_scalar(ohval[:, :, 0, :], ohhi[:, :, :], row1[:, 0:1], None, ALU.mult).then_inc(r_val, 1)
            for q in range(0, Q, 4):
                V_.tensor_tensor(ohlo[:, q:q + 4, :], *low_onehot(q), ALU.is_equal).then_inc(r_lo, 1)
            dve.wait_ge(r_list, 1)
            V_.tensor_scalar(empty[:, :], bank(4)[0:P, 0:COLS], 0.5, None, ALU.is_le)
            link(V_.tensor_copy(kch[:, :], bank(4)[0:P, COLS:2 * COLS]))
            V_.tensor_tensor(empty[:, :], empty[:, :], trash[:, :], ALU.mult)
            link(V_.scalar_tensor_tensor(drow[:, :], bank(4)[0:P, 0:COLS], float(Q), kch[:, :], ALU.mult, ALU.add))
            link(V_.tensor_scalar(idf[:, :], drow[:, :], float(Q), 0.0, ALU.subtract, ALU.max))
            link(V_.tensor_copy(gidx[:, :], idf[:, :]))
            V_.tensor_scalar(gidx[:, :], gidx[:, :], 1, None, ALU.logical_shift_right).then_inc(r_idx, 1)
            link(V_.scalar_tensor_tensor(drow[:, :], drow[:, :], -float(Q), empty[:, :], ALU.add, ALU.add))
            V_.tensor_copy(didx[:, :], drow[:, :]).then_inc(r_idx, 1)

            def h_split(e, k):
                u = e * HC + k
                dve.wait_ge(u_sb, u + 1)
                V_.tensor_copy(hh[:, k, :], hr[:, k % 2, :]).then_inc(h_hi, 1)
                dve.wait_ge(h_hi, u + 1)
                V_.tensor_tensor(hl[:, k, :], hr[:, k % 2, :], hh[:, k, :].bitcast(fp32), ALU.subtract)\
                    .then_inc(h_lo, 1)

            def x_low(e):
                dve.wait_ge(x_hi, e + 1)
                V_.tensor_tensor(xgl[:, :, :], pall[:, 2:4, 0:SLOTS], xgh[:, :, :].bitcast(fp32), ALU.subtract)\
                    .then_inc(x_lo, 1)

            def w1_low(e):
                dve.wait_ge(w1_hi, e + 1)
                V_.tensor_tensor(w1l[:, :, :], w1r[:, :, :], w1h[:, :, :].bitcast(fp32), ALU.subtract)\
                    .then_inc(w1_lo, 1)

            def take_y(e, par, first, last):
                if not first:
                    dve.wait_ge(y_out[par], e_count(e, par, 16 * JT) - 16 * JT)
                for j in range(JT):
                    if j == 1 and not last:
                        w1_low(e + 1)
                    dve.wait_ge(y_ps, e * JT + j + 1)
                    b2e = b2b[:, e, :] if isinstance(e, int) else b2b[:, bass.ds(e, 1), :].rearrange("p a f -> p (a f)")
                    V_.tensor_tensor(y[:, par, j, :], bank(6 + j % 2)[0:P, 0:ED], b2e, ALU.add).then_inc(y_sb, 1)

            def expert(e, par, first=False, last=False):
                for k in range(HC):
                    h_split(e, k)
                if not last:
                    x_low(e + 1)
                take_y(e, par, first, last)

            dve.wait_ge(c_l, N_L)
            w1_low(0)
            x_low(0)
            expert(0, 0, first=True)
            expert(1, 1, first=True)
            with dve.Fori(0, (E - 4) // 2) as j:
                for par in range(2):
                    expert(j * 2 + 2 + par, par)
            expert(E - 2, 0)
            expert(E - 1, 1, last=True)

            def summed(q, first=False):
                for k in range(2):
                    t = q * 2 + k
                    dve.wait_ge(a_ok, t + 1)
                    if not first:
                        dve.wait_ge(c_d, t - 1)
                    V_.scalar_tensor_tensor(yc[:, k, :], tile_of(yin, t * 2 + 1), col(wtok[:, 1, :], t), ya[:, k, :],
                                            ALU.mult, ALU.add).then_inc(c_ok, 1)
                for k in range(2):
                    t = q * 2 + k
                    dve.wait_ge(c_ok, t + 1)
                    V_.bn_stats(ystat[:, k, :], yc[:, k, :]).then_inc(c_st, 1)
                for k in range(2):
                    t = q * 2 + k
                    plain(dve, (c_st, t + 1)) if first else plain(dve, (c_st, t + 1), (c_rs0, q))
                    V_.bn_aggr(ymv[:, k, :], ystat[:, k, :]).then_inc(c_mv, 1)
                for k in range(2):
                    t = q * 2 + k
                    dve.wait_ge(c_mv, t + 1)
                    if not first:
                        dve.wait_ge(u_ok, t - 1)
                    V_.scalar_tensor_tensor(yd[:, k, :], yc[:, k, :], ymv[:, k, 0:1], lng[:, :],
                                            ALU.subtract, ALU.mult).then_inc(c_d, 1)

            summed(0, True)
            with dve.Fori(0, (TILES // 2 - 1) // 5) as j:
                for k in range(5):
                    summed(j * 5 + 1 + k)

        @block.gpsimd
        def _(pool):
            G = nc.gpsimd
            p_seq = sem("p_seq")
            seq = 0

            def link(inst):
                nonlocal seq
                seq += 1
                inst.then_inc(p_seq, 1)
                pool.wait_ge(p_seq, seq)

            G.memset(neghalf[:, :], -0.5)
            G.memset(onesrow[:, :], 1.0)
            link(G.memset(ident[:, :], 0.0))
            G.affine_select(out=ident[:, :], in_=ident[:, :], compare_op=ALU.not_equal, fill=1.0, base=0,
                            pattern=[[-1, 128]], channel_multiplier=1).then_inc(c_pool, 1)
            link(G.memset(amask[:, :], MASKED))
            for m in range(PER):
                lo_, hi_ = m * L, (m + 1) * L
                blk = amask[:, lo_:hi_]
                link(G.memset(blk, 0.0))
                link(G.affine_select(out=blk, in_=blk, compare_op=ALU.is_ge, fill=MASKED, base=-lo_,
                                     pattern=[[0, L]], channel_multiplier=1))
                link(G.affine_select(out=blk, in_=blk, compare_op=ALU.is_ge, fill=MASKED, base=hi_ - 1,
                                     pattern=[[0, L]], channel_multiplier=-1))
            G.affine_select(out=amask[:, :], in_=amask[:, :], compare_op=ALU.not_equal, fill=MASKED, base=0,
                            pattern=[[-1, P]], channel_multiplier=1).then_inc(c_pool, 1)
            pool.wait_ge(c_pool, 2)

            def rstd(slot, mv, ready, n, mid, done):
                plain(pool, (ready, n))
                G.tensor_scalar(rs[:, slot, 0:1], mv[:, 1:2], EPS, None, ALU.add).then_inc(mid, 1)
                need(pool, mid, n)
                G.tensor_tensor(rs[:, slot, 1:2], rs[:, slot, 0:1], neghalf[:, :], ALU.pow).then_inc(done, 1)

            def scale_x(t):
                rstd(0, xmv, x_mv, t + 1, x_rs0, x_rs)
                plain(pool, (x_rs, t + 1))
                G.tensor_scalar(rs[:, 0, 2:3], xmv[:, 0:1], rs[:, 0, 1:2], -1.0, ALU.mult, ALU.mult).then_inc(x_nb, 1)

            scale_x(0)

            def masks_table():
                G.memset(onesf[:, :], 1.0)
                link(G.memset(onesb[:, :], 1.0))
                G.affine_select(out=below[:, :], in_=onesb[:, :], compare_op=ALU.is_gt, fill=0.0, base=0,
                                pattern=[[1, 128]], channel_multiplier=-1)
                g3 = grp[:, :].rearrange("p (e w) -> p e w", w=WAYS)
                link(G.affine_select(out=g3, in_=onesb[:, :].rearrange("p (e w) -> p e w", w=WAYS), compare_op=ALU.is_ge,
                                     fill=0.0, base=0, pattern=[[-WAYS, E], [0, WAYS]], channel_multiplier=1))
                link(G.affine_select(out=g3, in_=g3, compare_op=ALU.is_ge, fill=0.0, base=WAYS - 1,
                                     pattern=[[WAYS, E], [0, WAYS]], channel_multiplier=-1))
                G.affine_select(out=pick[:, :], in_=onesf[:, 0:E], compare_op=ALU.is_equal, fill=0.0, base=0,
                                pattern=[[-WAYS, E]], channel_multiplier=1).then_inc(c_pool, 1)

            def live_table():
                link(G.memset(valid[:, :], 1.0))
                G.affine_select(out=valid[:, TILES - 1:TILES], in_=valid[:, TILES - 1:TILES], compare_op=ALU.is_gt,
                                fill=0.0, base=LIVE_LAST, pattern=[[0, 1]], channel_multiplier=-1)
                G.affine_select(out=valid[:, 0:TILES - 1], in_=valid[:, 0:TILES - 1], compare_op=ALU.is_gt,
                                fill=0.0, base=PER * L, pattern=[[0, TILES - 1]], channel_multiplier=-1)
                G.memset(keep0[:, :, :], 1.0)
                link(G.memset(row1[:, :], 0.0))
                G.memset(keep0[:, :, 0:1], 0.0)

            def index_table():
                f = dict(allow_small_or_imprecise_dtypes=True)
                G.iota(erev[:, :, :], [[-1, E], [0, TILES]], base=E, channel_multiplier=0, **f)
                G.iota(base1[:, :, :], [[SLOTS, E], [0, TILES]], base=1, channel_multiplier=0, **f)
                G.iota(iorow[:, :], [[1, P]], base=0, channel_multiplier=0, **f)
                G.iota(qidx[:, :], [[1, 2], [2, TILES]], base=0, channel_multiplier=0, **f)
                G.iota(trash[:, :], [[P, COLS]], base=TRASH + Q, channel_multiplier=1, **f)
                G.iota(row1[:, :], [[0, 1]], base=1, channel_multiplier=1, **f)
                G.iota(pidx[:, :], [[0, 1]], base=0, channel_multiplier=1).then_inc(c_pool, 1)

            def step(i, par):
                t = i - 1
                if live(t):
                    need(pool, z_n, t + 1)
                    if isinstance(t, int) and t == 0:
                        pool.wait_ge(c_g, N_G)
                        pool.wait_ge(c_dve, 3)
                    G.tensor_tensor(tile_of(H, t), zn[:, :], g2m[:, :], ALU.mult).then_inc(h_g, 1)
                    plain(pool, (h_g, t + 1))
                    G.tensor_tensor(tile_of(H, t), tile_of(H, t), posb[:, :], ALU.add).then_inc(h_ok, 1)
                t = i - 4
                if live(t):
                    need(pool, x2_ok, t)
                    rstd(3, gmv, g_mv, t + 1, g_rs0, g_rs)
                t = i - 1
                if live(t):
                    need(pool, x1_ok, t)
                    rstd(2, hmv, h_mv, t + 1, h_rs0, h_rs)
                if isinstance(i, int) and i == 0:
                    pool.wait_ge(x_n, 1)
                    scale_x(1)
                t = i + 2
                if live(t):
                    need(pool, x_n, t)
                    scale_x(t)
                if isinstance(i, int) and 2 <= i < 5:
                    (masks_table, live_table, index_table)[i - 2]()
                t = i
                if live(t):
                    rstd(1, zmv, z_mv, t + 1, z_rs0, z_rs)
            pipeline(pool, step, 7, 19)

            pool.wait_ge(x2_ok, TILES)
            pool.wait_ge(c_l, N_L)
            with pool.Fori(0, TILES) as t:
                G.tensor_tensor(tile_of(H, t), tile_of(H, t), lnb[:, :], ALU.add).then_inc(hb, 1)
            pool.wait_ge(r_hi, 1)
            G.tensor_tensor(ohval[:, :, 1, :], ohhi[:, :, :], rep(qidx[:, :].rearrange("p (q a) -> p q a", a=1), 2, COLS),
                            ALU.mult).then_inc(r_val, 1)

            pool.wait_ge(r_idx, 1)
            for par in range(2):
                pool.wait_ge(x2_out[par], 16 * (TILES // 2))
            pool.wait_ge(s_fill, 16 * FILLS)

            def icol(buf, e):
                return buf[:, e * JT:(e + 1) * JT] if isinstance(e, int) else buf[:, bass.ds(e * JT, JT)]

            def gather(e, par):
                need(pool, gT_ps, e - 1)
                G.tensor_copy(gst[:, par, :], icol(gidx, e)).then_inc(i_st, 1)
                plain(pool, (i_st, e + 1))
                for j in range(JT):
                    pool.indirect_dma_start(
                        xg[:, par, j, :], None, x2_rows,
                        bass.IndirectOffsetOnAxis(ap=gst[:, par, j:j + 1], axis=0)).then_inc(g_in[par][j], 16)

            def w2_low(e):
                for half in range(2):
                    pool.wait_ge(w2_hi, e * 2 + half + 1)
                    k = half * HC // 2
                    G.tensor_tensor(w2l[:, k:k + HC // 2, :], w2r[:, k:k + HC // 2, :],
                                    w2h[:, k:k + HC // 2, :].bitcast(fp32), ALU.subtract).then_inc(w2_lo, 1)

            def scatter(e, par):
                for j in range(JT):
                    plain(pool, (y_sb, e * JT + j + 1))
                    if j == 0:
                        G.tensor_copy(dst[:, par, :], icol(didx, e)).then_inc(i_dst, 1)
                        plain(pool, (i_dst, e + 1))
                    pool.indirect_dma_start(
                        y_rows, bass.IndirectOffsetOnAxis(ap=dst[:, par, j:j + 1], axis=0),
                        y[:, par, j, :], None).then_inc(y_out[par], 16)

            def serve(e, par, more=True):
                w2_low(e)
                if more:
                    gather(e + 2, par)
                scatter(e, par)

            gather(0, 0)
            gather(1, 1)
            w2_low(0)
            pool.wait_ge(r_idx, 2)
            gather(2, 0)
            scatter(0, 0)
            serve(1, 1)
            with pool.Fori(0, (E - 4) // 2) as j:
                for par in range(2):
                    serve(j * 2 + 2 + par, par)
            serve(E - 2, 0, more=False)
            serve(E - 1, 1, more=False)

            pool.wait_ge(hb, TILES)

            def rstd_pair(q, par):
                plain(pool, (c_mv, q * 2 + 2), (c_rs, q))
                G.tensor_scalar(yrs[:, 0, :], ymv[:, :, 1], EPS, None, ALU.add).then_inc(c_rs0, 1)
                pool.wait_ge(c_rs0, q + 1)
                G.tensor_tensor(yrs[:, 1 + par, :], yrs[:, 0, :], rep(neghalf[:, :], 1, 2), ALU.pow)\
                    .then_inc(c_rs, 1)

            def finish(q, par):
                if not (isinstance(q, int) and q < 2):
                    pool.wait_ge(o_out[par], 32 * (q // 2) if isinstance(q, int) else (q - par) * 16)
                for k in range(2):
                    t = q * 2 + k
                    plain(pool, (u_ok, t + 1))
                    G.tensor_tensor(yo[:, 2 * par + k, :], yu[:, k, :], tile_of(H, t), ALU.add).then_inc(o_ok, 1)

            PAIRS = TILES // 2
            rstd_pair(0, 0)
            for q in range(3):
                rstd_pair(q + 1, (q + 1) % 2)
                finish(q, q % 2)
            with pool.Fori(0, (PAIRS - 5) // 2) as j:
                for par in range(2):
                    rstd_pair(j * 2 + 4 + par, par)
                    finish(j * 2 + 3 + par, 1 - par)
            rstd_pair(PAIRS - 1, 0)
            finish(PAIRS - 2, 1)
            finish(PAIRS - 1, 0)


def kernel(**inputs):
    import numpy as np
    import concourse.bacc as bacc
    from concourse.bass_utils import run_bass_kernel_spmd

    a = {k: np.asarray(v_) for k, v_ in inputs.items()}
    B, C, S, _ = a["x"].shape
    ED = a["L0_tok_W_proj"].shape[1]
    n = round((a["L0_tok_pos_emb"].shape[1] - 1) ** 0.5)
    p = S // n
    E, D, HID = a["L0_ffn_w1"].shape
    col = lambda w: w.reshape(-1, 128).T
    arrays = {
        "x": a["x"].reshape(B, C, n, p, n, p).transpose(0, 2, 4, 3, 5, 1).reshape(B, n * n, p * p * C),
        "ln1_g": col(a["L0_tok_ln1_g"]), "ln1_b": col(a["L0_tok_ln1_b"]),
        "w_proj": a["L0_tok_W_proj"], "b_proj": a["L0_tok_b_proj"].reshape(1, ED),
        "ln2_g": a["L0_tok_ln2_g"].reshape(1, ED), "ln2_b": a["L0_tok_ln2_b"].reshape(1, ED),
        "cls_token": a["L0_tok_cls_token"].reshape(1, ED), "pos_emb": a["L0_tok_pos_emb"][0],
        "wq_t": a["L0_attn_Wq"].T, "bq": col(a["L0_attn_bq"]),
        "wk_t": a["L0_attn_Wk"].T, "bk": col(a["L0_attn_bk"]),
        "wv_t": a["L0_attn_Wv"].T, "bv": a["L0_attn_bv"].reshape(1, ED),
        "router_w": a["L0_ffn_router_w"], "router_b": a["L0_ffn_router_b"].reshape(1, E),
        "w1": a["L0_ffn_w1"], "b1": a["L0_ffn_b1"].reshape(E * HID // 128, 128).T,
        "w2": a["L0_ffn_w2"], "b2": a["L0_ffn_b2"].reshape(1, -1),
        "ln_g": a["L0_ffn_ln_g"].reshape(1, ED), "ln_b": a["L0_ffn_ln_b"].reshape(1, ED),
    }
    arrays = {f"in_{k}": np.ascontiguousarray(v_) for k, v_ in arrays.items()}
    nc = bacc.Bacc("TRN2", target_bir_lowering=False, num_devices=1)
    ins = [nc.dram_tensor(k, v_.shape, mybir.dt.from_np(v_.dtype), kind="ExternalInput").ap()
           for k, v_ in arrays.items()]
    out = nc.dram_tensor("out", (B * (n * n + 1), ED), fp32, kind="ExternalOutput").ap()
    vit_tower(nc, *ins, out)
    got = run_bass_kernel_spmd(nc, [arrays], core_ids=[0])
    return got.results[0]["out"].reshape(B, n * n + 1, ED)
```
